# Optimizing a Trainium2 kernel written in Bass

```python
import numpy as np
import jax
import jax.numpy as jnp

def _softmax(x, axis=-1):
    return jax.nn.softmax(x, axis=axis)

def _gelu(x):
    return jax.nn.gelu(x, approximate=True)

def _silu(x):
    return jax.nn.silu(x)

def _sigmoid(x):
    return jax.nn.sigmoid(x)

def _layernorm(x, axis=-1, eps=1e-05):
    m = jnp.mean(x, axis=axis, keepdims=True)
    v = jnp.var(x, axis=axis, keepdims=True)
    return (x - m) / jnp.sqrt(v + eps)

def _scatter_add(tgt, idx, src, axis=0):
    return tgt.at[idx].add(src)

def _segment_sum(src, seg, n):
    return jax.ops.segment_sum(src, seg, n)
kernel_name = 'mk_flamingo_gated_d2_seqx_r8_b738f5'

def setup_inputs(seed: int=0):
    np.random.seed(seed)
    _w = jnp.asarray

    def _rec_inputs():
        import jax
        import jax.numpy as jnp
        _rk = jax.random.key(seed)
        x = -0.0002928 + 1 * jax.random.normal(jax.random.fold_in(_rk, 1), (8, 128, 256), jnp.float32)
        _lenS = 128 - jax.random.randint(jax.random.fold_in(_rk, 7), (8,), 0, max(1, 128 // 4) + 1, jnp.int32)
        _lenS2 = 128 - jax.random.randint(jax.random.fold_in(_rk, 8), (8,), 0, max(1, 128 // 4) + 1, jnp.int32)
        _ctx_2048P = jax.random.normal(jax.random.fold_in(_rk, 11), (8, 16, 256), jnp.float32)
        _ctx_2048c = jax.random.dirichlet(jax.random.fold_in(_rk, 511), 0.3 * jnp.ones((16,), jnp.float32), (8, 128))
        _ctx_2048t = jnp.einsum('bsk,bkd->bsd', _ctx_2048c, _ctx_2048P)
        _ctx_2048t = _ctx_2048t * jax.lax.rsqrt(jnp.mean(jnp.square(_ctx_2048t)) + 1e-12) * 0.953939
        ctx_2048 = -1.39393e-06 + 0.999914 * (_ctx_2048t + 0.3 * jax.random.normal(jax.random.fold_in(_rk, 611), (8, 128, 256), jnp.float32))
        _validS = jnp.arange(128)[None, :] < _lenS[:, None]
        _validS2 = jnp.arange(128)[None, :] < _lenS2[:, None]
        _causal = jnp.tril(jnp.ones((128, 128), dtype=bool))
        mask_Bx1x2048_fk1 = jnp.where(jnp.ones((8, 1, 256), dtype=bool), 1.0, 0.0).astype(jnp.float32)
        _g = jax.random.normal(jax.random.fold_in(_rk, 9001), (2, 2), jnp.float32)
        _g = jnp.sign(_g) * jnp.maximum(jnp.abs(_g), 1.0) + (_g == 0) * 1.0
        g_xattn = _g[0]
        g_ffn = _g[1]
        return (x, ctx_2048, mask_Bx1x2048_fk1, g_xattn, g_ffn)
    x, ctx_2048, mask_Bx1x2048_fk1, g_xattn, g_ffn = _rec_inputs()

    def _L0_xattn_setup():
        import math
        import jax, jax.numpy as jnp
        import numpy as np
        SIZE = 128
        HEADS = 16
        HEAD_DIM = SIZE // HEADS
        B, T, S = (2, 256, 256)
        NEG = 1000000.0
        key = jax.random.key(seed)
        ks = jax.random.split(key, 10)
        target = jax.random.normal(ks[0], (B, SIZE, T), dtype=jnp.float32)
        source = jax.random.normal(ks[1], (B, SIZE, S), dtype=jnp.float32)
        target_mask = (jax.random.uniform(ks[2], (B, 1, T)) > 0.1).astype(jnp.float32)
        source_mask = (jax.random.uniform(ks[3], (B, 1, S)) > 0.1).astype(jnp.float32)
        scale = 1.0 / math.sqrt(SIZE)
        Wq = jax.random.normal(ks[4], (SIZE, SIZE), dtype=jnp.float32) * scale
        Wk = jax.random.normal(ks[5], (SIZE, SIZE), dtype=jnp.float32) * scale
        Wv = jax.random.normal(ks[6], (SIZE, SIZE), dtype=jnp.float32) * scale
        bq = jax.random.normal(ks[7], (SIZE,), dtype=jnp.float32) * 0.01
        bk = jax.random.normal(ks[8], (SIZE,), dtype=jnp.float32) * 0.01
        bv = jax.random.normal(ks[9], (SIZE,), dtype=jnp.float32) * 0.01
        return {'target': target, 'source': source, 'target_mask': target_mask, 'source_mask': source_mask, 'Wq': Wq, 'bq': bq, 'Wk': Wk, 'bk': bk, 'Wv': Wv, 'bv': bv}
    _L0_xattn_all = _L0_xattn_setup()
    _L0_xattn_in = {k: v for k, v in _L0_xattn_all.items() if k in ('Wq', 'bq', 'Wk', 'bk', 'Wv', 'bv')}
    del _L0_xattn_all

    def _L0_ffn_setup():
        import jax, jax.numpy as jnp
        import numpy as np
        EPS = 1e-05

        def _act_quant(x):
            scale = 127.0 / jnp.clip(jnp.max(jnp.abs(x), axis=-1, keepdims=True), EPS, None)
            return jnp.clip(jnp.round(x * scale), -128.0, 127.0) / scale

        def _weight_quant(w):
            scale = 1.0 / jnp.clip(jnp.mean(jnp.abs(w)), EPS, None)
            return jnp.clip(jnp.round(w * scale), -1.0, 1.0) / scale

        def _ste(x, q):
            return x + jax.lax.stop_gradient(q - x)

        def _bitlinear(x, w, b):
            xq = _ste(x, _act_quant(x))
            wq = _ste(w, _weight_quant(w))
            return jnp.einsum('bsd,hd->bsh', xq, wq) + b
        key = jax.random.key(seed)
        k1, k2, k3 = jax.random.split(key, 3)
        dim, hidden = (256, 1024)
        x = jax.random.normal(k1, (4, 256, dim), dtype=jnp.float32)
        w1 = jax.random.normal(k2, (hidden, dim), dtype=jnp.float32) * 0.02
        b1 = jnp.zeros((hidden,), dtype=jnp.float32)
        w2 = jax.random.normal(k3, (dim, hidden), dtype=jnp.float32) * 0.02
        b2 = jnp.zeros((dim,), dtype=jnp.float32)
        return {'x': x, 'w1': w1, 'b1': b1, 'w2': w2, 'b2': b2}
    _L0_ffn_all = _L0_ffn_setup()
    _L0_ffn_in = {k: v for k, v in _L0_ffn_all.items() if k in ('w1', 'b1', 'w2', 'b2')}
    del _L0_ffn_all

    def _L1_xattn_setup():
        import jax, jax.numpy as jnp
        import numpy as np
        HIDDEN = 256
        NUM_HEADS = 16
        HEAD_DIM = HIDDEN // NUM_HEADS
        CHUNK = 128
        SCALE = HEAD_DIM ** (-0.5)

        def _chunked_causal_attention(q, k, v):
            B, H, S, D = q.shape
            n_chunks = S // CHUNK
            kc = k.reshape(B, H, n_chunks, CHUNK, D).transpose(2, 0, 1, 3, 4)
            vc = v.reshape(B, H, n_chunks, CHUNK, D).transpose(2, 0, 1, 3, 4)
            j0s = jnp.arange(n_chunks) * CHUNK
            q_idx = jnp.arange(S)[:, None]
            k_off = jnp.arange(CHUNK)[None, :]
            out0 = jnp.zeros_like(q)
            m0 = jnp.full((B, H, S, 1), -jnp.inf, dtype=q.dtype)
            s0 = jnp.zeros((B, H, S, 1), dtype=q.dtype)

            def step(carry, inputs):
                out, m, s = carry
                kj, vj, j0 = inputs
                scores = jnp.einsum('bhqd,bhkd->bhqk', q, kj) * SCALE
                causal = j0 + k_off > q_idx
                scores = jnp.where(causal[None, None], -jnp.inf, scores)
                chunk_max = scores.max(axis=-1, keepdims=True)
                new_m = jnp.maximum(m, chunk_max)
                exp_old = jnp.exp(m - new_m)
                exp_c = jnp.exp(scores - new_m)
                new_s = s * exp_old + exp_c.sum(axis=-1, keepdims=True)
                out = out * (s / new_s) * exp_old + jnp.einsum('bhqk,bhkd->bhqd', exp_c / new_s, vj)
                return ((out, new_m, new_s), None)
            (out, _, _), _ = jax.lax.scan(step, (out0, m0, s0), (kc, vc, j0s))
            return out
        key = jax.random.key(seed)
        kq, kk, kv = jax.random.split(key, 3)
        B, S = (2, 512)
        return {'query': jax.random.normal(kq, (B, S, HIDDEN), dtype=jnp.float32), 'key': jax.random.normal(kk, (B, S, HIDDEN), dtype=jnp.float32), 'value': jax.random.normal(kv, (B, S, HIDDEN), dtype=jnp.float32)}
    _L1_xattn_all = _L1_xattn_setup()
    _L1_xattn_in = {k: v for k, v in _L1_xattn_all.items() if k in ()}
    del _L1_xattn_all

    def _L1_ffn_setup():
        import jax, jax.numpy as jnp
        import numpy as np
        B, S, H, E, D, K = (2, 256, 256, 8, 256, 2)
        key = jax.random.key(seed)
        ks = jax.random.split(key, 4)
        return {'x': jax.random.normal(ks[0], (B, S, H), jnp.float32), 'router_w': jax.random.normal(ks[1], (H, E), jnp.float32) / np.sqrt(H).astype(np.float32), 'router_b': jnp.zeros((E,), jnp.float32), 'expert_w': jax.random.normal(ks[2], (E, H, D), jnp.float32) / np.sqrt(H).astype(np.float32), 'expert_b': jnp.zeros((E, D), jnp.float32), 'out_w': jax.random.normal(ks[3], (D, D), jnp.float32) / np.sqrt(D).astype(np.float32), 'out_b': jnp.zeros((D,), jnp.float32)}
    _L1_ffn_all = _L1_ffn_setup()
    _L1_ffn_in = {k: v for k, v in _L1_ffn_all.items() if k in ('router_w', 'router_b', 'expert_w', 'expert_b', 'out_w', 'out_b')}
    del _L1_ffn_all
    return {'x': x, 'ctx_2048': ctx_2048, 'mask_Bx1x2048_fk1': mask_Bx1x2048_fk1, 'g_xattn': g_xattn, 'g_ffn': g_ffn, 'L0_xattn_Wq': _L0_xattn_in['Wq'], 'L0_xattn_bq': _L0_xattn_in['bq'], 'L0_xattn_Wk': _L0_xattn_in['Wk'], 'L0_xattn_bk': _L0_xattn_in['bk'], 'L0_xattn_Wv': _L0_xattn_in['Wv'], 'L0_xattn_bv': _L0_xattn_in['bv'], 'L0_ffn_w1': _L0_ffn_in['w1'], 'L0_ffn_b1': _L0_ffn_in['b1'], 'L0_ffn_w2': _L0_ffn_in['w2'], 'L0_ffn_b2': _L0_ffn_in['b2'], 'L1_ffn_router_w': _L1_ffn_in['router_w'], 'L1_ffn_router_b': _L1_ffn_in['router_b'], 'L1_ffn_expert_w': _L1_ffn_in['expert_w'], 'L1_ffn_expert_b': _L1_ffn_in['expert_b'], 'L1_ffn_out_w': _L1_ffn_in['out_w'], 'L1_ffn_out_b': _L1_ffn_in['out_b']}

def reference(x, ctx_2048, mask_Bx1x2048_fk1, g_xattn, g_ffn, L0_xattn_Wq, L0_xattn_bq, L0_xattn_Wk, L0_xattn_bk, L0_xattn_Wv, L0_xattn_bv, L0_ffn_w1, L0_ffn_b1, L0_ffn_w2, L0_ffn_b2, L1_ffn_router_w, L1_ffn_router_b, L1_ffn_expert_w, L1_ffn_expert_b, L1_ffn_out_w, L1_ffn_out_b):
    import jax
    import jax.numpy as jnp

    def _L0_xattn_ref(target, source, target_mask, source_mask, Wq, bq, Wk, bk, Wv, bv):
        import math
        import jax, jax.numpy as jnp
        import numpy as np
        SIZE = 128
        HEADS = 16
        HEAD_DIM = SIZE // HEADS
        B, T, S = (2, 256, 256)
        NEG = 1000000.0
        b, _, t = target.shape
        s = source.shape[-1]
        q = jnp.einsum('oc,bct->bot', Wq, target) + bq[None, :, None]
        k = jnp.einsum('oc,bcs->bos', Wk, source) + bk[None, :, None]
        v = jnp.einsum('oc,bcs->bos', Wv, source) + bv[None, :, None]
        q = q.reshape(b, HEADS, HEAD_DIM, t)
        k = k.reshape(b, HEADS, HEAD_DIM, s)
        v = v.reshape(b, HEADS, HEAD_DIM, s)
        dot = jnp.einsum('bhdt,bhds->bhts', q, k) / math.sqrt(HEAD_DIM)
        mask = target_mask[:, :, :, None] * source_mask[:, :, None, :]
        dot = mask * dot - (1.0 - mask) * NEG
        amap = jax.nn.softmax(dot, axis=-1) * mask
        out = jnp.einsum('bhts,bhds->bhdt', amap, v)
        return out.reshape(b, HEADS * HEAD_DIM, t)

    def _L0_ffn_ref(x, w1, b1, w2, b2):
        import jax, jax.numpy as jnp
        import numpy as np
        EPS = 1e-05

        def _act_quant(x):
            scale = 127.0 / jnp.clip(jnp.max(jnp.abs(x), axis=-1, keepdims=True), EPS, None)
            return jnp.clip(jnp.round(x * scale), -128.0, 127.0) / scale

        def _weight_quant(w):
            scale = 1.0 / jnp.clip(jnp.mean(jnp.abs(w)), EPS, None)
            return jnp.clip(jnp.round(w * scale), -1.0, 1.0) / scale

        def _ste(x, q):
            return x + jax.lax.stop_gradient(q - x)

        def _bitlinear(x, w, b):
            xq = _ste(x, _act_quant(x))
            wq = _ste(w, _weight_quant(w))
            return jnp.einsum('bsd,hd->bsh', xq, wq) + b
        h = jax.nn.gelu(_bitlinear(x, w1, b1), approximate=False)
        return _bitlinear(h, w2, b2)

    def _L1_xattn_ref(query, key, value):
        import jax, jax.numpy as jnp
        import numpy as np
        HIDDEN = 256
        NUM_HEADS = 16
        HEAD_DIM = HIDDEN // NUM_HEADS
        CHUNK = 128
        SCALE = HEAD_DIM ** (-0.5)

        def _chunked_causal_attention(q, k, v):
            B, H, S, D = q.shape
            n_chunks = S // CHUNK
            kc = k.reshape(B, H, n_chunks, CHUNK, D).transpose(2, 0, 1, 3, 4)
            vc = v.reshape(B, H, n_chunks, CHUNK, D).transpose(2, 0, 1, 3, 4)
            j0s = jnp.arange(n_chunks) * CHUNK
            q_idx = jnp.arange(S)[:, None]
            k_off = jnp.arange(CHUNK)[None, :]
            out0 = jnp.zeros_like(q)
            m0 = jnp.full((B, H, S, 1), -jnp.inf, dtype=q.dtype)
            s0 = jnp.zeros((B, H, S, 1), dtype=q.dtype)

            def step(carry, inputs):
                out, m, s = carry
                kj, vj, j0 = inputs
                scores = jnp.einsum('bhqd,bhkd->bhqk', q, kj) * SCALE
                causal = j0 + k_off > q_idx
                scores = jnp.where(causal[None, None], -jnp.inf, scores)
                chunk_max = scores.max(axis=-1, keepdims=True)
                new_m = jnp.maximum(m, chunk_max)
                exp_old = jnp.exp(m - new_m)
                exp_c = jnp.exp(scores - new_m)
                new_s = s * exp_old + exp_c.sum(axis=-1, keepdims=True)
                out = out * (s / new_s) * exp_old + jnp.einsum('bhqk,bhkd->bhqd', exp_c / new_s, vj)
                return ((out, new_m, new_s), None)
            (out, _, _), _ = jax.lax.scan(step, (out0, m0, s0), (kc, vc, j0s))
            return out
        B, S, _ = query.shape
        q = query.reshape(B, S, NUM_HEADS, HEAD_DIM).transpose(0, 2, 1, 3)
        k = key.reshape(B, S, NUM_HEADS, HEAD_DIM).transpose(0, 2, 1, 3)
        v = value.reshape(B, S, NUM_HEADS, HEAD_DIM).transpose(0, 2, 1, 3)
        out = _chunked_causal_attention(q, k, v)
        return out.transpose(0, 2, 1, 3).reshape(B, S, HIDDEN)

    def _L1_ffn_ref(x, router_w, router_b, expert_w, expert_b, out_w, out_b):
        import jax, jax.numpy as jnp
        import numpy as np
        B, S, H, E, D, K = (2, 256, 256, 8, 256, 2)
        num_experts = expert_w.shape[0]
        router_logits = jnp.einsum('bsh,he->bse', x, router_w) + router_b
        router_probs = jax.nn.softmax(router_logits, axis=-1)
        top_k_probs, top_k_indices = jax.lax.top_k(router_probs, K)
        top_k_probs = top_k_probs / jnp.sum(top_k_probs, axis=-1, keepdims=True)
        onehot = jax.nn.one_hot(top_k_indices, num_experts, dtype=x.dtype)
        gates = jnp.einsum('bsk,bske->bse', top_k_probs, onehot)
        expert_out = jax.nn.gelu(jnp.einsum('bsh,ehd->ebsd', x, expert_w) + expert_b[:, None, None, :])
        combined = jnp.einsum('bse,ebsd->bsd', gates, expert_out)
        return jnp.einsum('bsd,df->bsf', combined, out_w) + out_b
    x = x + jnp.tanh(g_xattn[0]) * _L0_xattn_ref(_layernorm(x, axis=-1), ctx_2048, mask_Bx1x2048_fk1, mask_Bx1x2048_fk1, L0_xattn_Wq, L0_xattn_bq, L0_xattn_Wk, L0_xattn_bk, L0_xattn_Wv, L0_xattn_bv)
    x = x + jnp.tanh(g_ffn[0]) * _L0_ffn_ref(_layernorm(x, axis=-1), L0_ffn_w1, L0_ffn_b1, L0_ffn_w2, L0_ffn_b2)
    x = x + jnp.tanh(g_xattn[1]) * _L1_xattn_ref(_layernorm(x, axis=-1), ctx_2048, ctx_2048)
    x = x + jnp.tanh(g_ffn[1]) * _L1_ffn_ref(_layernorm(x, axis=-1), L1_ffn_router_w, L1_ffn_router_b, L1_ffn_expert_w, L1_ffn_expert_b, L1_ffn_out_w, L1_ffn_out_b)
    return x

_drawn_inputs = setup_inputs


def setup_inputs(seed=0):
    import zlib

    import numpy as np

    out = dict(_drawn_inputs(seed))
    spreads = {'g_ffn': (-1.0, 0.2),
     'L0_ffn_b1': (0.0, 0.1),
     'L0_ffn_b2': (0.0, 0.1),
     'L1_ffn_router_b': (0.0, 0.1),
     'L1_ffn_expert_b': (0.0, 0.1),
     'L1_ffn_out_b': (0.0, 0.1)}
    factors = {'L0_xattn_bq': 7.982, 'L0_xattn_bk': 8.0, 'L0_xattn_bv': 7.441}
    for name, (base, spread) in spreads.items():
        noise = np.random.default_rng([zlib.crc32(name.encode()), seed]).standard_normal(out[name].shape)
        drawn = base * np.exp(spread * noise) if base else spread * noise
        out[name] = jnp.asarray(drawn.astype(out[name].dtype))
    for name, factor in factors.items():
        out[name] = (out[name] * factor).astype(out[name].dtype)
    return out
```

```python
import concourse.bass as bass
import numpy as np
from concourse import mybir
from contextlib import ExitStack


def gated_cross_attention_blocks(nc, x_in, ctx_in, mask_rows, mask_cols, g_xattn, g_ffn,
                                 wq_t, bq_in, wk_t, bk_in, wv_t, bv_in,
                                 w1_t, b1_in, w2_t, b2_in,
                                 router_w, router_b, expert_w, expert_b, out_w, out_b, out):
    f32, bf16, u16, u32 = mybir.dt.float32, mybir.dt.bfloat16, mybir.dt.uint16, mybir.dt.uint32
    ALU, ACT, AX = mybir.AluOpType, mybir.ActivationFunctionType, mybir.AxisListType

    NB, T, F = x_in.shape
    P = 128
    H0, D0 = 16, T // 16
    H1, D1 = 16, F // 16
    NP = H0 // 2
    HID = w1_t.shape[1]
    HC = HID // P
    FC = F // P
    NE = router_w.shape[1]
    EPS_LN, EPS_Q = 1e-5, 1e-5
    SCALE0, SCALE1 = float(D0) ** -0.5, float(D1) ** -0.5
    ROUND = 12582912.0
    MASKED = -1e30

    NT = 6
    ROW_MAX, ROW_NEG = NT * D0, NT * D0 + 2
    NSTACK = 4

    def bf16_bits(v):
        u = int(np.float32(v).view(np.uint32))
        return (u + 0x7FFF + ((u >> 16) & 1)) >> 16

    def bf16_value(bits):
        return float(np.uint32(bits << 16).view(np.float32))

    neg = float(np.float32(1e6 / SCALE0))
    neg_bits = []
    for _ in range(3):
        neg_bits.append(bf16_bits(neg))
        neg -= bf16_value(neg_bits[-1])
    q_rows = np.zeros((5, NP * F), np.uint16)
    q_rows[2:5] = np.array(neg_bits, np.uint16)[:, None]
    one_bits = bf16_bits(1.0)

    c_ident = nc.inline_tensor(np.eye(P, dtype=np.float32), "c_ident").ap()
    c_causal = nc.inline_tensor(np.triu(np.full((P, P), MASKED, np.float32), 1), "c_causal").ap()
    c_qrows = nc.inline_tensor(q_rows, "c_qrows").ap()
    c_krows = nc.inline_tensor(np.full((2, NP * F), one_bits, np.uint16), "c_krows").ap()
    c_head = nc.inline_tensor((np.arange(P)[:, None] // D1 == np.arange(P // D1)[None]).astype(np.float32),
                              "c_head").ap()
    c_iota = nc.inline_tensor(np.tile(np.arange(NE, dtype=np.float32), (P, NB)), "c_iota").ap()

    q_parts = nc.dram_tensor("q_parts", (P, NT, F), bf16, kind="Internal").ap()
    k_parts = nc.dram_tensor("k_parts", (P, NT, F), bf16, kind="Internal").ap()
    maxima = nc.dram_tensor("maxima", (2, 2, NP * F), bf16, kind="Internal").ap()
    mask_less_one = nc.dram_tensor("mask_less_one", (NB, F), bf16, kind="Internal").ap()

    stack = ExitStack()
    with stack:
        def sb(name, shape, dt=f32):
            return stack.enter_context(nc.sbuf_tensor(name, shape, dt))

        def sem(name):
            return stack.enter_context(nc.semaphore(name))

        PS = stack.enter_context(nc.psum_tensor("PS", [P, 8, 512], f32))

        ident = sb("ident", [P, P])
        ident_b = sb("ident_b", [P, P], bf16)
        causal = sb("causal", [P, P])
        causal_b = sb("causal_b", [P, 4, P], bf16)
        head_of = sb("head_of", [P, P // D1])
        iota_e = sb("iota_e", [P, NB * NE])
        ones = sb("ones", [P, P])
        wq = sb("wq", [P, P])
        wk = sb("wk", [P, P])
        wv = sb("wv", [P, P])
        bq = sb("bq", [P, 1])
        bk = sb("bk", [P, 1])
        bv = sb("bv", [P, P])
        w1f = sb("w1f", [P, FC, HID])
        w2f = sb("w2f", [P, HC, F])
        w1q = sb("w1q", [P, FC, HID], bf16)
        w2q = sb("w2q", [P, HC, F], bf16)
        b1 = sb("b1", [P, HID])
        b2 = sb("b2", [P, F])
        rw = sb("rw", [P, FC, NE])
        rb = sb("rb", [P, NE])
        ew = [w[:, :, :].rearrange("p a b -> p (a b)").rearrange("p (e d) -> p e d", e=NE) for w in (w1f, w2f)]
        ow = sb("ow", [P, FC, F])
        ob = sb("ob", [P, F])
        g_raw = sb("g_raw", [P, 4])
        tg = sb("tg", [P, 4])
        wsum = sb("wsum", [P, 2])
        wmean = sb("wmean", [P, 2])
        wscale = sb("wscale", [P, 2])
        mean127 = sb("mean127", [P, 2])

        xs = sb("xs", [P, NB, F])
        cs = sb("cs", [P, NB, F])
        stats = sb("stats", [P, 2, 6])
        mv = [sb(f"mv{n}", [P, NB, 2]) for n in range(4)]
        var_eps = sb("var_eps", [P, 4, NB])
        rstd = sb("rstd", [P, 4, NB])
        power = sb("power", [P, NB])
        xn = sb("xn", [P, 2, F])

        gate_mask = sb("gate_mask", [P, NB, F])
        src_mask = sb("src_mask", [P, NB, 2])
        mask_f = sb("mask_f", [NB, F])
        mask_b = sb("mask_b", [NB, F], bf16)
        nat = sb("nat", [P, 2 * F])
        rest = sb("rest", [P, 2 * F])
        parts = sb("parts", [P, 3, 2 * F], bf16)
        qst = sb("qst", [P, NSTACK, NP, F], bf16)
        kst = sb("kst", [P, NSTACK, NP, 2, F], bf16)
        vsb = sb("vsb", [P, 2, P])
        VW = 4 * (P + D0)
        vz = sb("vz", [P, 2, 2, VW])
        oz = sb("oz", [P, VW])
        m32 = sb("m32", [P, 2, 2, NP])
        mparts = sb("mparts", [P, 2, 2, 2, NP], bf16)
        mrows = sb("mrows", [2 * H0, 2, P], bf16)
        prob = sb("prob", [P, 4, 4 * F])
        recip_z = sb("recip_z", [P, F])
        attn = sb("attn", [P, F])

        amax = sb("amax", [P, 2, 4])
        amax2 = sb("amax2", [P, 2, 4])
        inv1 = sb("inv1", [P, 2])
        inv2 = sb("inv2", [P, 2])
        xr = sb("xr", [P, 2, F])
        xq = sb("xq", [P, 2, FC, P], bf16)
        hs = sb("hs", [P, 2, HID])
        hg = sb("hg", [P, 2, HID])
        hr = sb("hr", [P, 2, HID])
        hq = sb("hq", [P, 2, HC, P], bf16)
        y_ffn = sb("y_ffn", [P, F])

        flat_k = kst[:, :, :, :, :].rearrange("p a b c d -> p (a b c d)").bitcast(f32)
        flat_p = prob[:, :, :].rearrange("p a b -> p (a b)")
        NH2 = P // D1
        kz = flat_k[:, 0:2 * FC * NH2 * P].rearrange("p (a c v s) -> p a c v s", a=2, c=FC, v=NH2)
        qt = nat[:, :].rearrange("p (a c t) -> p a c t", a=2, c=FC)
        kt = rest[:, 0:F].rearrange("p (c s) -> p c s", c=FC)
        dif = flat_p[:, 0:2 * H1 * P].rearrange("p (a h s) -> p a h s", a=2, h=H1)
        pt = hs[:, :, :].rearrange("p a (h t) -> p a h t", h=NH2)
        vaug = sb("vaug", [P, 3, H1, D1 + 1])
        m1 = sb("m1", [P, 2, 2, NH2])
        rz1 = sb("rz1", [P, H1])

        xt = sb("xt", [P, NB, FC, P])
        eb = hg[:, :, :].rearrange("p a b -> p (a b)")
        logits = sb("logits", [P, NB, NE])
        top = sb("top", [P, NB, 8])
        topi = sb("topi", [P, NB, 8], u32)
        topf = sb("topf", [P, NB, 8])
        p2 = sb("p2", [P, 4, NB])
        oh = sb("oh", [P, 2, NB, NE])
        gates = sb("gates", [P, NB, NE])
        hb = hr[:, 0, :].rearrange("p (a f) -> p a f", a=2)
        he = hr[:, 1, :].rearrange("p (a f) -> p a f", a=2)
        acc = sb("acc", [P, 2, F])
        acct = sb("acct", [P, 2, FC, P])
        yo = sb("yo", [P, 2, F])

        names = """ld_const ld_attn ld_x ld_ctx ld_w ld_rest ld_rows st_mask setup_pool setup_dve setup_act
            wsum_done wsum_ps wscale_done w1_done w2_done w1_abs ln_x ln_mv ln_rstd ln_pool
            xn_ready qk_ps v_ps nat_ready v_ready split_chain split_ready stored stacked vz_ready
            s_ps s_max m_parts m_ps m_rows m_stored m_stacked t_ps prob_ready o_ps o_read x0_ready mv1_ready rstd1
            dve_chain
            a_round a_ps a_bf h_ps h_lin h_gelu h_amax h_round h_rps h_bf y_ps y_read x1_ready mv2 rstd2 pool_chain
            c_xn c_ps c_evac c_kz c_s c_dif c_exp c_tps c_pt c_ops c_oread x2_ready mv3 rstd3
            d_xn d_ps d_xt d_router d_chain d_e d_gates
            e_ps e_lin e_gelu e_acc e_tps e_acct e_yps e_y e_out ld_eb""".split()
        S = {n: sem(n) for n in names}

        block = stack.enter_context(nc.Block())

        def pair(u):
            return (u % 2) * 4 + u // 2

        def bcast(ap1d, n):
            return ap1d.partition_broadcast(n)

        @block.sync
        def _(sp):
            sp.dma_start(xs[:, 0:2, :], x_in[0:2].rearrange("b p f -> p b f")).then_inc(S["ld_x"], 16)
            sp.dma_start(xs[:, 2:NB, :], x_in[2:NB].rearrange("b p f -> p b f")).then_inc(S["ld_x"], 16)
            for dst, src in ((wq[:, :], wq_t), (wk[:, :], wk_t), (wv[:, :], wv_t),
                             (bq[:, :], bq_in.rearrange("(p a) -> p a", a=1)),
                             (bk[:, :], bk_in.rearrange("(p a) -> p a", a=1)),
                             (bv[:, :], bcast(bv_in, P))):
                sp.dma_start(dst, src).then_inc(S["ld_attn"], 16)
            sp.dma_start(cs[:, :, :], ctx_in.rearrange("b p f -> p b f")).then_inc(S["ld_ctx"], 16)
            for dst, src in ((ident[:, :], c_ident), (g_raw[:, 0:2], bcast(g_xattn, P)),
                             (g_raw[:, 2:4], bcast(g_ffn, P)),
                             (mask_f[:, :], mask_rows), (src_mask[:, :, :], mask_cols),
                             (gate_mask[:, :, :], bcast(mask_rows, P)),
                             (causal[:, :], c_causal), (head_of[:, :], c_head), (iota_e[:, :], c_iota)):
                sp.dma_start(dst, src).then_inc(S["ld_const"], 16)
            sp.dma_start(w1f[:, :, :], w1_t.rearrange("(c p) h -> p c h", p=P)).then_inc(S["ld_w"], 16)
            sp.dma_start(w2f[:, :, :], w2_t.rearrange("(c p) f -> p c f", p=P)).then_inc(S["ld_w"], 16)
            sp.wait_ge(S["setup_pool"], 4)
            n_rows = 0
            for z in range(NSTACK):
                for e in range(2):
                    r0 = 64 * e + ROW_MAX
                    sp.dma_start(qst[r0:r0 + 5, z].rearrange("p a f -> p (a f)").bitcast(u16), c_qrows)\
                        .then_inc(S["ld_rows"], 16)
                    sp.dma_start(kst[r0:r0 + 2, z, :, e, :].bitcast(u16),
                                 c_krows.rearrange("k (a f) -> k a f", a=NP)).then_inc(S["ld_rows"], 16)
                    n_rows += 32
            sp.wait_ge(S["setup_dve"], 1)
            sp.dma_start(mask_less_one, mask_b[:, :]).then_inc(S["st_mask"], 16)
            sp.wait_ge(S["st_mask"], 16)
            sp.wait_ge(S["ld_rows"], n_rows)
            for dst, src in ((b1[:, :], bcast(b1_in, P)), (b2[:, :], bcast(b2_in, P)),
                             (rw[:, :, :], router_w.rearrange("(c p) e -> p c e", p=P)),
                             (rb[:, :], bcast(router_b, P)),
                             (ow[:, :, :], out_w.rearrange("(c p) f -> p c f", p=P)),
                             (ob[:, :], bcast(out_b, P))):
                sp.dma_start(dst, src).then_inc(S["ld_rest"], 16)

            def stack_operands(b):
                sp.wait_ge(S["split_ready"], b + 1)
                if b:
                    sp.wait_ge(S["stacked"], 128 * b)
                for w, dst, c0 in ((0, q_parts, 0), (1, k_parts, F)):
                    for n0, runs in ((0, 3), (3, 2), (5, 1)):
                        if w == 0:
                            src = parts[:, 0:runs, c0:c0 + F]
                        else:
                            src = parts[:, 3 - runs:4 - runs, c0:c0 + F]
                            if runs > 1:
                                src = src.broadcast_to([P, runs, F])
                        sp.dma_start(dst[:, n0:n0 + runs, :], src).then_inc(S["stored"], 16)
                sp.wait_ge(S["stored"], 96 * (b + 1))
                if b >= NSTACK:
                    sp.wait_ge(S["t_ps"], NP * (b - NSTACK + 1))
                    sp.wait_ge(S["m_stacked"], 32 * (b - NSTACK + 1))
                z = b % NSTACK
                for e in range(2):
                    rows = slice(64 * e, 64 * e + NT * D0)
                    sp.dma_start(qst[rows, z], q_parts[64 * e:64 * e + 64].rearrange("(a d) k t -> (d k) a t", d=D0))\
                        .then_inc(S["stacked"], 16)
                    sp.dma_start(kst[rows, z, :, e, :],
                                 k_parts[64 * e:64 * e + 64].rearrange("(a d) k t -> (d k) a t", d=D0))\
                        .then_inc(S["stacked"], 16)
                    r0 = 64 * e + ROW_MAX
                    sp.dma_start(qst[r0:r0 + 2, z].rearrange("p a f -> p (a f)").bitcast(u16), c_qrows[0:2, :])\
                        .then_inc(S["stacked"], 16)
                    r0 = 64 * e + ROW_NEG
                    sp.dma_start(kst[r0:r0 + 3, z, :, e, :],
                                 mask_less_one[b:b + 1, :].unsqueeze(1).broadcast_to([3, NP, F]))\
                        .then_inc(S["stacked"], 16)

            def stack_maxima(b):
                sp.wait_ge(S["m_rows"], b + 1)
                z = b % NSTACK
                if b:
                    sp.wait_ge(S["m_stacked"], 32 * b)
                sp.dma_start(maxima.rearrange("l e (a t) -> (l e a) t", a=NP), mrows[:, :, :].rearrange("k a t -> k (a t)"))\
                    .then_inc(S["m_stored"], 16)
                sp.wait_ge(S["m_stored"], 16 * (b + 1))
                for e in range(2):
                    r0 = 64 * e + ROW_MAX
                    sp.dma_start(qst[r0:r0 + 2, z].rearrange("p a f -> p (a f)"), maxima[:, e, :])\
                        .then_inc(S["m_stacked"], 16)

            for i in range(NB + 1):
                if i < NB:
                    stack_operands(i)
                if i >= 1:
                    stack_maxima(i - 1)

            sp.wait_ge(S["w1_done"], 3)
            sp.wait_ge(S["w2_done"], 3)
            for c in range(FC):
                sp.dma_start(ew[c], expert_w[:, c * P:(c + 1) * P, :].rearrange("e p d -> p e d"))\
                    .then_inc(S["ld_eb"], 16)
            sp.wait_ge(S["h_round"], NB)
            sp.dma_start(eb.rearrange("p (e d) -> p e d", e=NE), bcast(expert_b, P)).then_inc(S["ld_eb"], 16)
            for b in range(NB):
                sp.wait_ge(S["e_y"], b + 1)
                sp.dma_start(out[b], yo[:, b % 2, :]).then_inc(S["e_out"], 16)
                sp.wait_ge(S["e_out"], 16 * (b + 1))

        @block.gpsimd
        def _(pool):
            chain = [0]

            def link(ins):
                chain[0] += 1
                ins.then_inc(S["pool_chain"], 1)
                pool.wait_ge(S["pool_chain"], chain[0])

            link(pool.memset(power[:, :], -0.5))
            pool.memset(qst[:, :, :, :].rearrange("p a b c -> p (a b c)").bitcast(f32), 0.0).then_inc(S["setup_pool"], 1)
            pool.memset(flat_k, 0.0).then_inc(S["setup_pool"], 1)
            pool.memset(vz[:, :, :, :], 0.0).then_inc(S["setup_pool"], 1)
            pool.memset(vaug[:, :, :, :], 1.0).then_inc(S["setup_pool"], 1)

            def rstd_of(n, b, ready, value, done):
                pool.wait_ge(S[ready], value)
                link(pool.tensor_scalar(var_eps[:, n, b:b + 1], mv[n][:, b, 1:2], EPS_LN, None, ALU.add))
                pool.tensor_tensor(rstd[:, n, b:b + 1], var_eps[:, n, b:b + 1], power[:, 0:1], ALU.pow)\
                    .then_inc(S[done], 1)

            for b in range(NB):
                rstd_of(0, b, "ln_mv", b + 1, "ln_rstd")

            def split(b):
                pool.wait_ge(S["nat_ready"], 2 * (b + 1))
                if b:
                    pool.wait_ge(S["stored"], 96 * b)
                link(pool.tensor_copy(parts[:, 0, :], nat[:, :]))
                link(pool.tensor_tensor(rest[:, :], nat[:, :], parts[:, 0, :], ALU.subtract))
                link(pool.tensor_copy(parts[:, 1, :], rest[:, :]))
                pool.tensor_tensor(parts[:, 2, :], rest[:, :], parts[:, 1, :], ALU.subtract)\
                    .then_inc(S["split_ready"], 1)

            def spread_v(b):
                pool.wait_ge(S["v_ready"], b + 1)
                if b >= 2:
                    pool.wait_ge(S["o_ps"], 4 * (b - 1))
                for st in range(2):
                    dst = vz[:, b % 2, st, :].rearrange("p (r y) -> p r y", r=4)[:, :, 0:P]\
                        .rearrange("p r (j y) -> p r j y", j=4)[:, :, :, 0:D0]
                    src = vsb[:, st, :].rearrange("p (j r d) -> p r j d", j=4, r=4)
                    pool.tensor_scalar(dst, src, src_mask[:, b, st:st + 1], None, ALU.mult)\
                        .then_inc(S["vz_ready"], 1)

            def quantise_weights(w, src, dst, done):
                if w == 0:
                    pool.wait_ge(S["wscale_done"], 1)
                pool.tensor_scalar(src, src, wscale[:, w:w + 1], 1.0, ALU.mult, ALU.min).then_inc(S[done], 1)
                pool.wait_ge(S[done], 1)
                pool.tensor_scalar(src, src, -1.0, ROUND, ALU.max, ALU.add).then_inc(S[done], 1)
                pool.wait_ge(S[done], 2)
                pool.tensor_scalar(dst, src, ROUND, None, ALU.subtract).then_inc(S[done], 1)

            for i in range(NB + 4):
                if i < NB:
                    split(i)
                if 2 <= i < NB + 2:
                    spread_v(i - 2)
                if i == 3:
                    quantise_weights(0, w1f[:, :, :].rearrange("p a b -> p (a b)"),
                                     w1q[:, :, :].rearrange("p a b -> p (a b)"), "w1_done")
                if i == 4:
                    quantise_weights(1, w2f[:, :, :].rearrange("p a b -> p (a b)"),
                                     w2q[:, :, :].rearrange("p a b -> p (a b)"), "w2_done")
                if i >= 4:
                    rstd_of(1, i - 4, "mv1_ready", i - 3, "rstd1")

            def round_hidden(b):
                pool.wait_ge(S["h_amax"], b + 1)
                if b >= 2:
                    pool.wait_ge(S["h_rps"], b - 1)
                pool.tensor_scalar(hr[:, b % 2, :], hg[:, b % 2, :], amax2[:, b % 2, 3:4], ROUND, ALU.mult, ALU.add)\
                    .then_inc(S["h_round"], 1)

            for i in range(NB + 3):
                if 2 <= i < NB + 2:
                    round_hidden(i - 2)
                if i >= 3:
                    rstd_of(2, i - 3, "mv2", i - 2, "rstd2")

            def spread_k(b):
                pool.wait_ge(S["c_evac"], 2 * (b + 1))
                if b == 0:
                    pool.wait_ge(S["t_ps"], NP * NB)
                if b >= 2:
                    pool.wait_ge(S["c_s"], 2 * (b - 1))
                if b >= 3:
                    pool.wait_ge(S["c_ops"], b - 2)
                for v in range(NH2):
                    pool.tensor_scalar(kz[:, b % 2, :, v, :], kt, head_of[:, v:v + 1], None, ALU.mult)
                pool.tensor_copy(vaug[:, b % 3, :, 0:D1], cs[:, b, :].rearrange("p (h d) -> p h d", h=H1))\
                    .then_inc(S["c_kz"], 1)

            for i in range(NB + 3):
                if i < NB:
                    spread_k(i)
                if i >= 3:
                    rstd_of(3, i - 3, "mv3", i - 2, "rstd3")

        @block.scalar
        def _(act):
            act.wait_ge(S["ld_const"], 16 * 9)
            act.activation(tg[:, :], g_raw[:, :], ACT.Tanh).then_inc(S["setup_act"], 1)
            act.wait_ge(S["ld_w"], 32)
            act.activation(hs[:, :, :].rearrange("p a b -> p (a b)"), w1f[:, :, :].rearrange("p a b -> p (a b)"),
                           ACT.Abs, accum_out=wsum[:, 0:1]).then_inc(S["w1_abs"], 1)
            act.activation(hg[:, :, :].rearrange("p a b -> p (a b)"), w2f[:, :, :].rearrange("p a b -> p (a b)"),
                           ACT.Abs, accum_out=wsum[:, 1:2]).then_inc(S["w1_abs"], 1)

            def evac_qk(b):
                act.wait_ge(S["qk_ps"], b + 1)
                if b:
                    act.wait_ge(S["split_ready"], b)
                act.activation(nat[:, 0:F], PS[:, 7, 0:F], ACT.Identity, bias=bq[:, 0:1]).then_inc(S["nat_ready"], 1)
                act.activation(nat[:, F:2 * F], PS[:, 7, F:2 * F], ACT.Identity, bias=bk[:, 0:1])\
                    .then_inc(S["nat_ready"], 1)

            def exps(b, u):
                n = NP * b + u
                act.wait_ge(S["t_ps"], n + 1)
                if n >= 4:
                    act.wait_ge(S["o_ps"], n // 2 - 1)
                bank = 2 + 2 * (u % 2)
                act.activation(prob[:, u % 4, :], PS[:, bank:bank + 2, :].rearrange("p a f -> p (a f)"),
                               ACT.Exp, scale=SCALE0).then_inc(S["prob_ready"], 1)

            def evac_maxima(b):
                act.wait_ge(S["m_ps"], b + 1)
                if b:
                    act.wait_ge(S["m_stored"], 16 * b)
                act.activation(mrows[:, :, :].rearrange("p a t -> p (a t)"),
                               PS[0:2 * H0, 7, 0:P].bitcast(bf16), ACT.Copy).then_inc(S["m_rows"], 1)

            for i in range(NB + 3):
                for u in range(NP):
                    if i >= 3:
                        exps(i - 3, u)
                    if i < NB and u == 0:
                        evac_qk(i)
                if 1 <= i <= NB:
                    evac_maxima(i - 1)

            def evac_x(b):
                act.wait_ge(S["a_ps"], b + 1)
                if b >= 2:
                    act.wait_ge(S["h_ps"], b - 1)
                act.activation(xq[:, b % 2, :, :].rearrange("p c t -> p (c t)"), PS[:, 7, 0:F], ACT.Copy, bias=-ROUND)\
                    .then_inc(S["a_bf"], 1)

            def gelu(b):
                act.wait_ge(S["h_lin"], b + 1)
                if b >= 2:
                    act.wait_ge(S["h_round"], b - 1)
                act.activation(hg[:, b % 2, :], hs[:, b % 2, :], ACT.Gelu).then_inc(S["h_gelu"], 1)

            def evac_h(b):
                act.wait_ge(S["h_rps"], b + 1)
                if b >= 2:
                    act.wait_ge(S["y_ps"], b - 1)
                act.activation(hq[:, b % 2, :, :].rearrange("p c t -> p (c t)"),
                               PS[:, 2:4, :].rearrange("p a f -> p (a f)"), ACT.Copy, bias=-ROUND)\
                    .then_inc(S["h_bf"], 1)

            for i in range(NB + 2):
                if i < NB:
                    evac_x(i)
                if 2 <= i:
                    evac_h(i - 2)
                if 1 <= i <= NB:
                    gelu(i - 1)

            def evac_t(b):
                act.wait_ge(S["c_ps"], b + 1)
                if b == 0:
                    act.wait_ge(S["split_ready"], NB)
                if b >= 2:
                    act.wait_ge(S["c_s"], 2 * (b - 1))
                if b >= 1:
                    act.wait_ge(S["c_kz"], b)
                act.activation(qt[:, b % 2, :, :].rearrange("p c t -> p (c t)"), PS[:, 7, 0:F], ACT.Copy)\
                    .then_inc(S["c_evac"], 1)
                act.activation(kt.rearrange("p c t -> p (c t)"), PS[:, 7, F:2 * F], ACT.Copy)\
                    .then_inc(S["c_evac"], 1)

            def exp1(b, hf):
                act.wait_ge(S["c_dif"], 2 * b + hf + 1)
                d = dif[:, b % 2, hf * NH2:(hf + 1) * NH2, :].rearrange("p h s -> p (h s)")
                act.activation(d, d, ACT.Exp, scale=SCALE1).then_inc(S["c_exp"], 1)

            def evac_p(b, hf):
                n = 2 * b + hf
                act.wait_ge(S["c_tps"], n + 1)
                if n >= 2:
                    act.wait_ge(S["c_ops"], (n - 2) // 2 + 1)
                act.activation(pt[:, hf, :, :].rearrange("p h t -> p (h t)"),
                               PS[:, 4:6, :].rearrange("p a f -> p (a f)"), ACT.Copy).then_inc(S["c_pt"], 1)

            for i in range(NB + 2):
                if i < NB:
                    evac_t(i)
                for hf in range(2):
                    if 2 <= i:
                        evac_p(i - 2, hf)
                    if 1 <= i <= NB:
                        exp1(i - 1, hf)

            for b in range(NB):
                act.wait_ge(S["d_ps"], b + 1)
                act.activation(xt[:, b, :, :].rearrange("p c t -> p (c t)"), PS[:, 4 + b % 2, 0:F], ACT.Copy)\
                    .then_inc(S["d_xt"], 1)
            act.wait_ge(S["d_chain"], 1)
            act.activation(p2[:, 1, :], p2[:, 0, :], ACT.Exp).then_inc(S["d_e"], 1)

            def gelu_experts(n):
                act.wait_ge(S["e_lin"], n + 1)
                if n >= 2:
                    act.wait_ge(S["e_acc"], 2 * (n - 1))
                act.activation(he[:, n % 2, :], hb[:, n % 2, :], ACT.Gelu_apprx_tanh).then_inc(S["e_gelu"], 1)

            def evac_acc(b):
                act.wait_ge(S["e_tps"], b + 1)
                if b >= 2:
                    act.wait_ge(S["e_yps"], b - 1)
                act.activation(acct[:, b % 2, :, :].rearrange("p c t -> p (c t)"), PS[:, 4, 0:F], ACT.Copy)\
                    .then_inc(S["e_acct"], 1)

            for n in range(4 * NB + 3):
                if n < 4 * NB:
                    gelu_experts(n)
                if n % 4 == 2 and n >= 6:
                    evac_acc((n - 6) // 4)

        @block.vector
        def _(dve):
            chain = [0]

            def link(ins):
                chain[0] += 1
                ins.then_inc(S["dve_chain"], 1)
                dve.wait_ge(S["dve_chain"], chain[0])

            def stats_of(n, b, done):
                link(dve.bn_stats(stats[:, b % 2, :], xs[:, b, :]))
                dve.bn_aggr(mv[n][:, b, :], stats[:, b % 2, :]).then_inc(S[done], 1)

            def normalise(n, b, dst):
                return dve.tensor_scalar(dst, xs[:, b, :], mv[n][:, b, 0:1], rstd[:, n, b:b + 1],
                                         ALU.subtract, ALU.mult)

            dve.memset(ones[:, :], 1.0)
            link(dve.memset(oz[:, :], 0.0))
            for r in range(4):
                v = oz[:, r * (P + D0):r * (P + D0) + P].rearrange("p (j y) -> p j y", j=4)[:, :, 0:D0]
                dve.memset(v, 1.0)
            dve.wait_ge(S["ld_x"], 32)
            for b in range(NB):
                stats_of(0, b, "ln_mv")
            dve.wait_ge(S["ld_const"], 16 * 9)
            dve.tensor_scalar(mask_b[:, :], mask_f[:, :], -1.0, None, ALU.add).then_inc(S["setup_dve"], 1)
            dve.tensor_copy(ident_b[:, :], ident[:, :]).then_inc(S["setup_dve"], 1)
            for c in range(4):
                dve.tensor_copy(causal_b[:, c, :], causal[:, :])
            dve.wait_ge(S["setup_act"], 1)
            dve.tensor_scalar(gate_mask[:, :, :], gate_mask[:, :, :], tg[:, 0:1], None, ALU.mult)\
                .then_inc(S["setup_dve"], 1)
            dve.wait_ge(S["ld_attn"], 96)

            def norm_x(b):
                dve.wait_ge(S["ln_rstd"], b + 1)
                if b >= 2:
                    dve.wait_ge(S["qk_ps"], b - 1)
                normalise(0, b, xn[:, b % 2, :]).then_inc(S["xn_ready"], 1)

            def bias_v(b):
                dve.wait_ge(S["v_ps"], b + 1)
                if b:
                    dve.wait_ge(S["vz_ready"], 2 * b)
                dve.tensor_tensor(vsb[:, :, :], PS[:, 7, 0:2 * P].rearrange("p (a o) -> p a o", a=2),
                                  bv[:, :].unsqueeze(1).broadcast_to([P, 2, P]), ALU.add).then_inc(S["v_ready"], 1)

            def row_max(b, k):
                n = 16 * b + k
                dve.wait_ge(S["s_ps"], n + 1)
                pr, tt = k // 2, k % 2
                dve.tensor_reduce(m32[:, tt, :, pr], PS[:, k % 2, :].rearrange("p (e s) -> p e s", e=2),
                                  AX.X, ALU.max, negate=True).then_inc(S["s_max"], 1)

            def split_maxima(b):
                dve.wait_ge(S["s_max"], 16 * (b + 1))
                if b:
                    dve.wait_ge(S["m_ps"], b)
                dve.tensor_copy(mparts[:, :, 0, :, :], m32[:, :, :, :]).then_inc(S["m_parts"], 1)
                dve.wait_ge(S["m_parts"], 2 * b + 1)
                dve.tensor_tensor(mparts[:, :, 1, :, :], m32[:, :, :, :], mparts[:, :, 0, :, :], ALU.subtract)\
                    .then_inc(S["m_parts"], 1)

            def attn_out(b):
                dve.wait_ge(S["o_ps"], 4 * (b + 1))
                link(dve.reciprocal(recip_z[:, :], PS[:, 6, F:2 * F]))
                dve.tensor_tensor(attn[:, :], PS[:, 6, 0:F], recip_z[:, :], ALU.mult).then_inc(S["o_read"], 1)
                dve.wait_ge(S["o_read"], b + 1)
                link(dve.tensor_tensor(attn[:, :], attn[:, :], gate_mask[:, b, :], ALU.mult))
                link(dve.tensor_tensor(xs[:, b, :], xs[:, b, :], attn[:, :], ALU.add))
                stats_of(1, b, "mv1_ready")

            norm_x(0)
            for i in range(NB + 4):
                if i + 1 < NB:
                    norm_x(i + 1)
                for k in range(16):
                    if 1 <= i <= NB:
                        row_max(i - 1, k)
                    if k == 1 and i >= 4:
                        attn_out(i - 4)
                    if k == 6 and 2 <= i < NB + 2:
                        bias_v(i - 2)
                if 1 <= i <= NB:
                    split_maxima(i - 1)
                if i == 0:
                    dve.wait_ge(S["wsum_ps"], 1)
                    link(dve.tensor_scalar(wmean[:, :], PS[:, 6, 0:2], 1.0 / (HID * F), EPS_Q, ALU.mult, ALU.max))
                    dve.tensor_scalar(mean127[:, :], wmean[:, :], 1.0 / 127.0, None, ALU.mult)
                    dve.reciprocal(wscale[:, :], wmean[:, :]).then_inc(S["wscale_done"], 1)

            def scales(a, inv, w, b):
                link(dve.tensor_scalar(a[:, 1:2], a[:, 0:1], EPS_Q, None, ALU.max))
                dve.tensor_scalar(inv, a[:, 1:2], mean127[:, w:w + 1], None, ALU.mult)
                link(dve.reciprocal(a[:, 2:3], a[:, 1:2]))
                return dve.tensor_scalar(a[:, 3:4], a[:, 2:3], 127.0, None, ALU.mult)

            def quantise_x(b):
                dve.wait_ge(S["rstd1"], b + 1)
                link(normalise(1, b, xn[:, b % 2, :]))
                link(dve.tensor_reduce(amax[:, b % 2, 0:1], xn[:, b % 2, :], AX.X, ALU.max, apply_absolute_value=True))
                link(scales(amax[:, b % 2, :], inv1[:, b % 2:b % 2 + 1], 0, b))
                if b >= 2:
                    dve.wait_ge(S["a_ps"], b - 1)
                dve.tensor_scalar(xr[:, b % 2, :], xn[:, b % 2, :], amax[:, b % 2, 3:4], ROUND, ALU.mult, ALU.add)\
                    .then_inc(S["a_round"], 1)

            def hidden(b):
                dve.wait_ge(S["h_ps"], b + 1)
                if b == 0:
                    dve.wait_ge(S["ld_rest"], 96)
                    dve.wait_ge(S["w1_abs"], 2)
                if b >= 2:
                    dve.wait_ge(S["h_gelu"], b - 1)
                bank = 4 * (b % 2)
                dve.scalar_tensor_tensor(out=hs[:, b % 2, :], in0=PS[:, bank:bank + 2, :].rearrange("p a f -> p (a f)"),
                                         scalar=inv1[:, b % 2:b % 2 + 1], in1=b1[:, :], op0=ALU.mult, op1=ALU.add)\
                    .then_inc(S["h_lin"], 1)

            def hidden_scales(b):
                dve.wait_ge(S["h_gelu"], b + 1)
                if b >= 2:
                    dve.wait_ge(S["h_round"], b - 1)
                link(dve.tensor_reduce(amax2[:, b % 2, 0:1], hg[:, b % 2, :], AX.X, ALU.max, apply_absolute_value=True))
                scales(amax2[:, b % 2, :], inv2[:, b % 2:b % 2 + 1], 1, b).then_inc(S["h_amax"], 1)

            def ffn_out(b):
                dve.wait_ge(S["y_ps"], b + 1)
                dve.scalar_tensor_tensor(out=y_ffn[:, :], in0=PS[:, 6, 0:F], scalar=inv2[:, b % 2:b % 2 + 1],
                                         in1=b2[:, :], op0=ALU.mult, op1=ALU.add).then_inc(S["y_read"], 1)
                dve.wait_ge(S["y_read"], b + 1)
                link(dve.scalar_tensor_tensor(out=xs[:, b, :], in0=y_ffn[:, :], scalar=tg[:, 2:3], in1=xs[:, b, :],
                                              op0=ALU.mult, op1=ALU.add))
                stats_of(2, b, "mv2")

            for i in range(NB + 3):
                if i >= 3:
                    ffn_out(i - 3)
                if 2 <= i < NB + 2:
                    hidden_scales(i - 2)
                if i < NB:
                    quantise_x(i)
                if 1 <= i <= NB:
                    hidden(i - 1)

            def norm_1(b):
                dve.wait_ge(S["rstd2"], b + 1)
                if b >= 2:
                    dve.wait_ge(S["c_ps"], b - 1)
                normalise(2, b, xn[:, b % 2, :]).then_inc(S["c_xn"], 1)

            def less_max(b, hf):
                dve.wait_ge(S["c_s"], 2 * b + hf + 1)
                if b >= 2:
                    dve.wait_ge(S["c_tps"], 2 * (b - 2) + hf + 1)
                s = PS[:, 2 * hf:2 * hf + 2, :].rearrange("p a (h s) -> p (a h) s", h=4)
                link(dve.tensor_reduce(m1[:, b % 2, hf, :], s, AX.X, ALU.max))
                dve.tensor_tensor(dif[:, b % 2, hf * NH2:(hf + 1) * NH2, :], s,
                                  m1[:, b % 2, hf, :].unsqueeze(2).broadcast_to([P, NH2, P]), ALU.subtract)\
                    .then_inc(S["c_dif"], 1)

            def attn1_out(b):
                dve.wait_ge(S["c_ops"], b + 1)
                o = PS[:, 6, 0:H1 * (D1 + 1)].rearrange("p (h d) -> p h d", h=H1)
                link(dve.reciprocal(rz1[:, :], o[:, :, D1:D1 + 1].rearrange("p h d -> p (h d)")))
                dve.tensor_tensor(attn[:, :].rearrange("p (h d) -> p h d", h=H1), o[:, :, 0:D1],
                                  rz1[:, :].unsqueeze(2).broadcast_to([P, H1, D1]), ALU.mult).then_inc(S["c_oread"], 1)
                dve.wait_ge(S["c_oread"], b + 1)
                link(dve.scalar_tensor_tensor(out=xs[:, b, :], in0=attn[:, :], scalar=tg[:, 1:2], in1=xs[:, b, :],
                                              op0=ALU.mult, op1=ALU.add))
                stats_of(3, b, "mv3")

            for i in range(NB + 3):
                if i < NB:
                    norm_1(i)
                for hf in range(2):
                    if 1 <= i <= NB:
                        less_max(i - 1, hf)
                if i >= 3:
                    attn1_out(i - 3)

            for b in range(NB):
                dve.wait_ge(S["rstd3"], b + 1)
                if b >= 2:
                    dve.wait_ge(S["d_ps"], b - 1)
                normalise(3, b, xn[:, b % 2, :]).then_inc(S["d_xn"], 1)
            dve.wait_ge(S["d_router"], 1)
            link(dve.tensor_tensor(logits[:, :, :], PS[:, 6, 0:NB * NE].rearrange("p (b e) -> p b e", b=NB),
                                   rb[:, :].unsqueeze(1).broadcast_to([P, NB, NE]), ALU.add))
            for b in range(NB):
                last = dve.max(top[:, b, :], logits[:, b, :])
            link(last)
            for b in range(NB):
                last = dve.max_index(topi[:, b, :], top[:, b, :], logits[:, b, :])
            link(last)
            dve.tensor_tensor(p2[:, 0, :], top[:, :, 1], top[:, :, 0], ALU.subtract).then_inc(S["d_chain"], 1)
            link(dve.tensor_copy(topf[:, :, :], topi[:, :, :]))
            io = iota_e[:, :].rearrange("p (b e) -> p b e", b=NB)
            for k in range(2):
                dve.tensor_tensor(oh[:, k, :, :], io, topf[:, :, k:k + 1].broadcast_to([P, NB, NE]), ALU.is_equal)
            dve.wait_ge(S["d_e"], 1)
            link(dve.tensor_scalar(p2[:, 2, :], p2[:, 1, :], 1.0, None, ALU.add))
            link(dve.reciprocal(p2[:, 2, :], p2[:, 2, :]))
            link(dve.tensor_tensor(p2[:, 3, :], p2[:, 1, :], p2[:, 2, :], ALU.mult))
            for k in range(2):
                link(dve.tensor_tensor(oh[:, k, :, :], oh[:, k, :, :],
                                       p2[:, 2 + k, :].unsqueeze(2).broadcast_to([P, NB, NE]), ALU.mult))
            dve.tensor_tensor(gates[:, :, :], oh[:, 0, :, :], oh[:, 1, :, :], ALU.add).then_inc(S["d_gates"], 1)
            dve.wait_ge(S["d_gates"], 1)
            dve.wait_ge(S["ld_eb"], 48)

            def expert_bias(n):
                dve.wait_ge(S["e_ps"], n + 1)
                if n >= 2:
                    dve.wait_ge(S["e_gelu"], n - 1)
                c = n % 4
                dve.tensor_tensor(hb[:, n % 2, :], PS[:, n % 4, :], eb[:, 512 * c:512 * (c + 1)], ALU.add)\
                    .then_inc(S["e_lin"], 1)

            def gate_experts(n):
                dve.wait_ge(S["e_gelu"], n + 1)
                b, c = n // 4, n % 4
                for e in range(2):
                    g = gates[:, b, 2 * c + e:2 * c + e + 1]
                    h = he[:, n % 2, e * F:(e + 1) * F]
                    if c == 0 and e == 0:
                        if b >= 2:
                            dve.wait_ge(S["e_tps"], b - 1)
                        dve.tensor_scalar(acc[:, b % 2, :], h, g, None, ALU.mult).then_inc(S["e_acc"], 1)
                    else:
                        dve.wait_ge(S["e_acc"], 2 * n + e)
                        dve.scalar_tensor_tensor(out=acc[:, b % 2, :], in0=h, scalar=g, in1=acc[:, b % 2, :],
                                                 op0=ALU.mult, op1=ALU.add).then_inc(S["e_acc"], 1)

            def result(b):
                dve.wait_ge(S["e_yps"], b + 1)
                if b >= 2:
                    dve.wait_ge(S["e_out"], 16 * (b - 1))
                link(dve.tensor_tensor(yo[:, b % 2, :], PS[:, 5, 0:F], ob[:, :], ALU.add))
                dve.scalar_tensor_tensor(out=yo[:, b % 2, :], in0=yo[:, b % 2, :], scalar=tg[:, 3:4], in1=xs[:, b, :],
                                         op0=ALU.mult, op1=ALU.add).then_inc(S["e_y"], 1)

            for n in range(4 * NB + 5):
                if n < 4 * NB:
                    expert_bias(n)
                if 1 <= n <= 4 * NB:
                    gate_experts(n - 1)
                if n >= 8 and n % 4 == 0:
                    result((n - 8) // 4)

        @block.tensor
        def _(pe):
            pe.wait_ge(S["ld_attn"], 96)
            pe.wait_ge(S["ld_ctx"], 16)

            def project_qk(b):
                pe.wait_ge(S["xn_ready"], b + 1)
                if b >= 2:
                    pe.wait_ge(S["m_rows"], b - 1)
                if b >= 3:
                    pe.wait_ge(S["v_ready"], b - 2)
                pe.matmul(PS[:, 7, 0:F], wq[:, :], xn[:, b % 2, :], start=True, stop=True)
                pe.matmul(PS[:, 7, F:2 * F], wk[:, :], cs[:, b, :], start=True, stop=True).then_inc(S["qk_ps"], 1)

            def project_v(b):
                pe.wait_ge(S["nat_ready"], 2 * min(b + 3, NB))
                if b >= 6:
                    pe.wait_ge(S["m_rows"], b)
                for st in range(2):
                    mm = pe.matmul(PS[:, 7, st * P:(st + 1) * P], cs[:, b, st * P:(st + 1) * P], wv[:, :],
                                   start=True, stop=True)
                mm.then_inc(S["v_ps"], 1)

            def scores_for_max(b, k):
                n = 16 * b + k
                if k == 0:
                    pe.wait_ge(S["stacked"], 128 * (b + 1))
                if n >= 2:
                    pe.wait_ge(S["s_max"], n - 1)
                pr, tt = k // 2, k % 2
                z = b % NSTACK
                pe.matmul(PS[:, k % 2, :], qst[:, z, pr, tt * P:(tt + 1) * P],
                          kst[:, z, pr, :, :].rearrange("p e s -> p (e s)"), start=True, stop=True)\
                    .then_inc(S["s_ps"], 1)

            def turn_maxima(b):
                pe.wait_ge(S["m_parts"], 2 * (b + 1))
                pe.wait_ge(S["nat_ready"], 2 * min(b + 2, NB))
                if b:
                    pe.wait_ge(S["v_ready"], b)
                pe.wait_ge(S["setup_dve"], 2)
                for tt in range(2):
                    mm = pe.transpose(PS[0:2 * H0, 7, tt * 64:(tt + 1) * 64].bitcast(bf16),
                                      mparts[:, tt, :, :, :].rearrange("p a e k -> p (a e k)"), ident_b[:, :])
                mm.then_inc(S["m_ps"], 1)

            def scores_less_max(b, u):
                n = NP * b + u
                if u == 0:
                    pe.wait_ge(S["m_stacked"], 32 * (b + 1))
                if n >= 2:
                    pe.wait_ge(S["prob_ready"], n - 1)
                z, pr = b % NSTACK, pair(u)
                for st in range(2):
                    for e in range(2):
                        mm = pe.matmul(PS[:, 2 + 2 * (u % 2) + st, e * F:(e + 1) * F],
                                       kst[:, z, pr, e, st * P:(st + 1) * P], qst[:, z, pr, :], start=True, stop=True)
                mm.then_inc(S["t_ps"], 1)

            def weigh_values(b, r):
                pe.wait_ge(S["prob_ready"], NP * b + 2 * r + 2)
                if r == 0:
                    pe.wait_ge(S["vz_ready"], 2 * (b + 1))
                    if b == 0:
                        pe.wait_ge(S["wscale_done"], 1)
                    if b:
                        pe.wait_ge(S["o_read"], b)
                for st in range(2):
                    for what in range(2):
                        for j in range(4):
                            c0 = r * P + 32 * j
                            w = vz[:, b % 2, st, :] if what == 0 else oz[:, :]
                            lhs = w[:, c0:c0 + 32]
                            p = prob[:, (2 * r + j // 2) % 4, st * 2 * F + (j % 2) * F:st * 2 * F + (j % 2 + 1) * F]
                            mm = pe.matmul(PS[32 * j:32 * j + 32, 6, what * F:(what + 1) * F], lhs, p,
                                           start=(r == 0 and st == 0 and what == 0), stop=(r == 3 and st == 1),
                                           skip_group_check=True)
                mm.then_inc(S["o_ps"], 1)

            for i in range(NB + 3):
                for u in range(NP):
                    if i >= 3:
                        scores_less_max(i - 3, u)
                    if 1 <= i <= NB:
                        for k in range(3 * u, min(3 * u + 3, 16)):
                            scores_for_max(i - 1, k)
                    if u == 0 and i < NB:
                        project_qk(i)
                    if u == 2 and 2 <= i < NB + 2:
                        project_v(i - 2)
                    if i >= 3 and u % 2 == 1 and u >= 3:
                        weigh_values(i - 3, (u - 3) // 2)
                    if u == 6 and 1 <= i <= NB:
                        turn_maxima(i - 1)
                if i >= 3:
                    weigh_values(i - 3, 3)
                if i == 0:
                    pe.wait_ge(S["w1_abs"], 2)
                    pe.matmul(PS[:, 6, 0:2], ones[:, :], wsum[:, :], start=True, stop=True).then_inc(S["wsum_ps"], 1)

            def turn_x(b):
                pe.wait_ge(S["a_round"], b + 1)
                if b == 0:
                    pe.wait_ge(S["m_rows"], NB)
                if b:
                    pe.wait_ge(S["a_bf"], b)
                for c in range(FC):
                    mm = pe.transpose(PS[:, 7, c * P:(c + 1) * P], xr[:, b % 2, c * P:(c + 1) * P], ident[:, :])
                mm.then_inc(S["a_ps"], 1)

            def up(b):
                pe.wait_ge(S["a_bf"], b + 1)
                if b == 0:
                    pe.wait_ge(S["w1_done"], 3)
                    pe.wait_ge(S["s_max"], 16 * NB)
                if b == 1:
                    pe.wait_ge(S["prob_ready"], NP * NB)
                if b >= 2:
                    pe.wait_ge(S["h_lin"], b - 1)
                for hh in range(2):
                    for c in range(FC):
                        mm = pe.matmul(PS[:, 4 * (b % 2) + hh, :], xq[:, b % 2, c, :], w1q[:, c, hh * 512:(hh + 1) * 512],
                                       start=(c == 0), stop=(c == FC - 1))
                mm.then_inc(S["h_ps"], 1)

            def turn_h(b):
                pe.wait_ge(S["h_round"], b + 1)
                if b == 0:
                    pe.wait_ge(S["prob_ready"], NP * NB)
                if b:
                    pe.wait_ge(S["h_bf"], b)
                for c in range(HC):
                    mm = pe.transpose(PS[:, 2 + c // 4, (c % 4) * P:(c % 4 + 1) * P], hr[:, b % 2, c * P:(c + 1) * P],
                                      ident[:, :])
                mm.then_inc(S["h_rps"], 1)

            def down(b):
                pe.wait_ge(S["h_bf"], b + 1)
                if b == 0:
                    pe.wait_ge(S["w2_done"], 3)
                    pe.wait_ge(S["o_read"], NB)
                if b:
                    pe.wait_ge(S["y_read"], b)
                for c in range(HC):
                    mm = pe.matmul(PS[:, 6, 0:F], hq[:, b % 2, c, :], w2q[:, c, :], start=(c == 0), stop=(c == HC - 1))
                mm.then_inc(S["y_ps"], 1)

            for i in range(NB + 2):
                if 1 <= i <= NB:
                    up(i - 1)
                if i < NB:
                    turn_x(i)
                if i >= 2:
                    turn_h(i - 2)
                    down(i - 2)

            def turn_1(b):
                pe.wait_ge(S["c_xn"], b + 1)
                if b == 0:
                    pe.wait_ge(S["a_bf"], NB)
                if b:
                    pe.wait_ge(S["c_evac"], 2 * b)
                for c in range(FC):
                    pe.transpose(PS[:, 7, c * P:(c + 1) * P], xn[:, b % 2, c * P:(c + 1) * P], ident[:, :])
                for c in range(FC):
                    mm = pe.transpose(PS[:, 7, F + c * P:F + (c + 1) * P], cs[:, b, c * P:(c + 1) * P], ident[:, :])
                mm.then_inc(S["c_ps"], 1)

            def scores_1(b, hf):
                pe.wait_ge(S["c_kz"], b + 1)
                if b == 0:
                    pe.wait_ge(S["h_lin"], NB)
                    pe.wait_ge(S["h_bf"], NB)
                if b:
                    pe.wait_ge(S["c_dif"], 2 * (b - 1) + hf + 1)
                for q in range(2):
                    pe.matmul(PS[:, 2 * hf + q, :], ident_b[:, :], causal_b[:, :, :].rearrange("p a s -> p (a s)"),
                              start=True, stop=False)
                    mm = pe.matmul(PS[:, 2 * hf + q, :], qt[:, b % 2, hf, :],
                                   kz[:, b % 2, hf, 4 * q:4 * q + 4, :].rearrange("p v s -> p (v s)"),
                                   start=False, stop=True)
                mm.then_inc(S["c_s"], 1)

            def turn_p(b, hf):
                n = 2 * b + hf
                pe.wait_ge(S["c_exp"], n + 1)
                if n == 0:
                    pe.wait_ge(S["h_lin"], NB)
                if n:
                    pe.wait_ge(S["c_pt"], n)
                for h in range(NH2):
                    mm = pe.transpose(PS[:, 4 + h // 4, (h % 4) * P:(h % 4 + 1) * P], dif[:, b % 2, hf * NH2 + h, :],
                                      ident[:, :])
                mm.then_inc(S["c_tps"], 1)

            def weigh_1(b):
                pe.wait_ge(S["c_pt"], 2 * (b + 1))
                if b == 0:
                    pe.wait_ge(S["y_read"], NB)
                if b:
                    pe.wait_ge(S["c_oread"], b)
                for h in range(H1):
                    mm = pe.matmul(PS[:, 6, h * (D1 + 1):(h + 1) * (D1 + 1)], pt[:, h // NH2, h % NH2, :],
                                   vaug[:, b % 3, h, :], start=True, stop=True)
                mm.then_inc(S["c_ops"], 1)

            for i in range(NB + 2):
                if i < NB:
                    turn_1(i)
                for hf in range(2):
                    if i >= 2:
                        turn_p(i - 2, hf)
                    if 1 <= i <= NB:
                        scores_1(i - 1, hf)
                if i >= 2:
                    weigh_1(i - 2)

            for b in range(NB + 1):
                if b < NB:
                    pe.wait_ge(S["d_xn"], b + 1)
                    if b == 0:
                        pe.wait_ge(S["c_pt"], 2 * NB)
                    if b >= 2:
                        pe.wait_ge(S["d_xt"], b - 1)
                    for c in range(FC):
                        mm = pe.transpose(PS[:, 4 + b % 2, c * P:(c + 1) * P], xn[:, b % 2, c * P:(c + 1) * P], ident[:, :])
                    mm.then_inc(S["d_ps"], 1)
                if b >= 1:
                    pe.wait_ge(S["d_xt"], b)
                    if b == 1:
                        pe.wait_ge(S["c_oread"], NB)
                    for c in range(FC):
                        mm = pe.matmul(PS[:, 6, (b - 1) * NE:b * NE], xt[:, b - 1, c, :], rw[:, c, :],
                                       start=(c == 0), stop=(c == FC - 1))
                    if b == NB:
                        mm.then_inc(S["d_router"], 1)
            pe.wait_ge(S["ld_eb"], 48)
            pe.wait_ge(S["c_dif"], 2 * NB)

            def experts(n):
                b, q = n // 4, n % 4
                if n >= 4:
                    pe.wait_ge(S["e_lin"], n - 3)
                for c in range(FC):
                    mm = pe.matmul(PS[:, q, :], xt[:, b, c, :], ew[c][:, 2 * q:2 * q + 2, :].rearrange("p e d -> p (e d)"),
                                   start=(c == 0), stop=(c == FC - 1))
                mm.then_inc(S["e_ps"], 1)

            def turn_acc(b):
                pe.wait_ge(S["e_acc"], 8 * (b + 1))
                if b:
                    pe.wait_ge(S["e_acct"], b)
                for c in range(FC):
                    mm = pe.transpose(PS[:, 4, c * P:(c + 1) * P], acc[:, b % 2, c * P:(c + 1) * P], ident[:, :])
                mm.then_inc(S["e_tps"], 1)

            def project_out(b):
                pe.wait_ge(S["e_acct"], b + 1)
                if b:
                    pe.wait_ge(S["e_y"], b)
                for c in range(FC):
                    mm = pe.matmul(PS[:, 5, 0:F], acct[:, b % 2, c, :], ow[:, c, :], start=(c == 0), stop=(c == FC - 1))
                mm.then_inc(S["e_yps"], 1)

            for n in range(4 * NB + 4):
                if n < 4 * NB:
                    experts(n)
                if n >= 5 and n % 4 == 1:
                    turn_acc((n - 5) // 4)
                if n >= 7 and n % 4 == 3:
                    project_out((n - 7) // 4)


def _heads_in_stack_order(n_tokens, heads):
    d = n_tokens // heads
    return [64 * jj + 32 * e + 8 * r + c for e in range(2) for jj in range(2) for r in range(4) for c in range(d)]


def kernel(**inputs):
    import concourse.bacc as _bacc
    from concourse import mybir as _mybir
    from concourse.bass_utils import run_bass_kernel_spmd as _run

    a = {k: np.asarray(v) for k, v in inputs.items()}
    NB, T, F = a["x"].shape
    order = _heads_in_stack_order(T, 16)
    mask = a["mask_Bx1x2048_fk1"].reshape(NB, F)
    laid = {
        "x": a["x"], "ctx": a["ctx_2048"],
        "mask_rows": mask, "mask_cols": mask.reshape(NB, 2, 128).transpose(2, 0, 1),
        "g_xattn": a["g_xattn"], "g_ffn": a["g_ffn"],
        "wq_t": a["L0_xattn_Wq"][order].T, "bq": a["L0_xattn_bq"][order],
        "wk_t": a["L0_xattn_Wk"][order].T, "bk": a["L0_xattn_bk"][order],
        "wv_t": a["L0_xattn_Wv"].T, "bv": a["L0_xattn_bv"],
        "w1_t": a["L0_ffn_w1"].T, "b1": a["L0_ffn_b1"], "w2_t": a["L0_ffn_w2"].T, "b2": a["L0_ffn_b2"],
        "router_w": a["L1_ffn_router_w"], "router_b": a["L1_ffn_router_b"],
        "expert_w": a["L1_ffn_expert_w"], "expert_b": a["L1_ffn_expert_b"],
        "out_w": a["L1_ffn_out_w"], "out_b": a["L1_ffn_out_b"],
    }
    nc = _bacc.Bacc("TRN2", target_bir_lowering=False, num_devices=1)
    arrays, args = {}, []
    for name, v in laid.items():
        v = np.ascontiguousarray(v)
        arrays[f"in_{name}"] = v
        args.append(nc.dram_tensor(f"in_{name}", v.shape, _mybir.dt.from_np(v.dtype), kind="ExternalInput").ap())
    args.append(nc.dram_tensor("out_0", a["x"].shape, _mybir.dt.from_np(a["x"].dtype), kind="ExternalOutput").ap())
    gated_cross_attention_blocks(nc, *args)
    r = _run(nc, [arrays], core_ids=[0])
    return r.results[0]["out_0"]
```

```python
import concourse.bass as bass
import numpy as np
from concourse import mybir
from contextlib import ExitStack


def gated_cross_attention_blocks(nc, x_in, ctx_in, mask_rows, mask_cols, g_xattn, g_ffn,
                                 wq_t, bq_in, wk_t, bk_in, wv_t, bv_in,
                                 w1_t, b1_in, w2_t, b2_in,
                                 router_w, router_b, expert_w, expert_b, out_w, out_b, out):
    f32, bf16, u16, u32 = mybir.dt.float32, mybir.dt.bfloat16, mybir.dt.uint16, mybir.dt.uint32
    ALU, ACT, AX = mybir.AluOpType, mybir.ActivationFunctionType, mybir.AxisListType

    NB, T, F = x_in.shape
    P = 128
    H0, D0 = 16, T // 16
    H1, D1 = 16, F // 16
    NP = H0 // 2
    HID = w1_t.shape[1]
    HC = HID // P
    FC = F // P
    NE = router_w.shape[1]
    EPS_LN, EPS_Q = 1e-5, 1e-5
    SCALE0, SCALE1 = float(D0) ** -0.5, float(D1) ** -0.5
    ROUND = 12582912.0
    MASKED = -1e30

    NT, SLOTS = 6, 8
    NSTACK = 5

    def bf16_bits(v):
        u = int(np.float32(v).view(np.uint32))
        return (u + 0x7FFF + ((u >> 16) & 1)) >> 16

    def bf16_value(bits):
        return float(np.uint32(bits << 16).view(np.float32))

    neg = float(np.float32(1e6 / SCALE0))
    neg_bits = []
    for _ in range(3):
        neg_bits.append(bf16_bits(neg))
        neg -= bf16_value(neg_bits[-1])
    free_rows = np.zeros((2, D0, SLOTS - NT, F), np.uint16)
    free_rows[0, 1:4, 0] = np.array(neg_bits, np.uint16)[:, None]
    free_rows[1, 0] = bf16_bits(1.0)

    c_ident = nc.inline_tensor(np.eye(P, dtype=np.float32), "c_ident").ap()
    c_causal = nc.inline_tensor(np.triu(np.full((P, P), MASKED, np.float32), 1), "c_causal").ap()
    c_free = nc.inline_tensor(free_rows, "c_free").ap()
    c_head = nc.inline_tensor((np.arange(P)[:, None] // D1 == np.arange(P // D1)[None]).astype(np.float32),
                              "c_head").ap()
    c_iota = nc.inline_tensor(np.tile(np.arange(NE, dtype=np.float32), (P, NB)), "c_iota").ap()

    qk_rows = nc.dram_tensor("qk_rows", (2, P, SLOTS, F), bf16, kind="Internal").ap()
    maxima = nc.dram_tensor("maxima", (2, 2, NP * F), bf16, kind="Internal").ap()
    mask_less_one = nc.dram_tensor("mask_less_one", (NB, F), bf16, kind="Internal").ap()

    stack = ExitStack()
    with stack:
        def sb(name, shape, dt=f32):
            return stack.enter_context(nc.sbuf_tensor(name, shape, dt))

        def sem(name):
            return stack.enter_context(nc.semaphore(name))

        PS = stack.enter_context(nc.psum_tensor("PS", [P, 8, 512], f32))

        ident = sb("ident", [P, P])
        ident_b = sb("ident_b", [P, P], bf16)
        causal = sb("causal", [P, P])
        causal_b = sb("causal_b", [P, 4, P], bf16)
        head_of = sb("head_of", [P, P // D1])
        iota_e = sb("iota_e", [P, NB * NE])
        ones = sb("ones", [P, P])
        wq = sb("wq", [P, P])
        wk = sb("wk", [P, P])
        wv = sb("wv", [P, P])
        bq = sb("bq", [P, 1])
        bk = sb("bk", [P, 1])
        bv = sb("bv", [P, P])
        w1f = sb("w1f", [P, FC, HID])
        w2f = sb("w2f", [P, HC, F])
        w1q = sb("w1q", [P, FC, HID], bf16)
        w2q = sb("w2q", [P, HC, F], bf16)
        b1 = sb("b1", [P, HID])
        b2 = sb("b2", [P, F])
        rw = sb("rw", [P, FC, NE])
        rb = sb("rb", [P, NE])
        ew = [w[:, :, :].rearrange("p a b -> p (a b)").rearrange("p (e d) -> p e d", e=NE) for w in (w1f, w2f)]
        ow = sb("ow", [P, FC, F])
        ob = sb("ob", [P, F])
        g_raw = sb("g_raw", [P, 4])
        tg = sb("tg", [P, 4])
        wsum = sb("wsum", [P, 2])
        wmean = sb("wmean", [P, 2])
        wscale = sb("wscale", [P, 2])
        mean127 = sb("mean127", [P, 2])

        xs = sb("xs", [P, NB, F])
        cs = sb("cs", [P, NB, F])
        stats = sb("stats", [P, 2, 6])
        mv = [sb(f"mv{n}", [P, NB, 2]) for n in range(4)]
        var_eps = sb("var_eps", [P, 4, NB])
        rstd = sb("rstd", [P, 4, NB])
        power = sb("power", [P, NB])
        xn = sb("xn", [P, 2, F])

        gate_mask = sb("gate_mask", [P, NB, F])
        src_mask = sb("src_mask", [P, NB, 2])
        mask_f = sb("mask_f", [NB, F])
        mask_b = sb("mask_b", [NB, F], bf16)
        nat = sb("nat", [P, 2 * F])
        rest = sb("rest", [P, 2 * F])
        parts = sb("parts", [P, 6, F], bf16)
        hi_parts, mid_parts, lo_parts = [parts[:, n:n + 1 + 5 - 2 * n:5 - 2 * n, :] for n in range(3)]
        qst = sb("qst", [P, NSTACK, NP, F], bf16)
        kst = sb("kst", [P, NSTACK, NP, 2, F], bf16)
        vsb = sb("vsb", [P, 2, P])
        VW = 4 * (P + D0)
        vz = sb("vz", [P, 2, 2, VW])
        oz = sb("oz", [P, VW])
        m32 = sb("m32", [P, 2, 2, NP])
        mparts = sb("mparts", [P, 2, 2, 2, NP], bf16)
        mrows = sb("mrows", [2 * H0, 2, P], bf16)
        wide = sb("wide", [P, 4 * 4 * F])
        prob = wide[:, :].rearrange("p (a f) -> p a f", a=4)
        recip_z = sb("recip_z", [P, F])
        attn = sb("attn", [P, F])
        zero = sb("zero", [P, 1])

        amax = sb("amax", [P, NB, 4])
        amax2 = sb("amax2", [P, NB, 4])
        inv1 = sb("inv1", [P, NB])
        inv2 = sb("inv2", [P, NB])
        xr = rest[:, :].rearrange("p (a f) -> p a f", a=2)
        ozs = sb("ozs", [P, 2 * F])
        xq = sb("xq", [P, NB, FC, P], bf16)
        hs = wide[:, 0:2 * HID].rearrange("p (a h) -> p a h", a=2)
        hg = wide[:, 2 * HID:4 * HID].rearrange("p (a h) -> p a h", a=2)
        hr = sb("hr", [P, 2, HID])
        hq = sb("hq", [P, 2, HC, P], bf16)
        y_ffn = sb("y_ffn", [P, F])

        flat_k = kst[:, :, :, :, :].rearrange("p a b c d -> p (a b c d)").bitcast(f32)
        flat_q = qst[:, :, :, :].rearrange("p a b c -> p (a b c)").bitcast(f32)
        NH2 = P // D1
        KA = 3
        kz = flat_k[:, 0:2 * FC * NH2 * P].rearrange("p (a c v s) -> p a c v s", a=2, c=FC, v=NH2)
        qt = nat[:, :].rearrange("p (a c t) -> p a c t", a=2, c=FC)
        kt = rest[:, 0:F].rearrange("p (c s) -> p c s", c=FC)
        dif = flat_q[:, 0:2 * H1 * P].rearrange("p (a h s) -> p a h s", a=2, h=H1)
        pt = hs[:, :, :].rearrange("p a (h t) -> p a h t", h=NH2)
        VC = 32
        vaug = sb("vaug", [P, 2, H1, VC])
        ot = hr[:, 0, 0:4 * P]
        m1 = sb("m1", [P, 2, 2, NH2])
        rz1 = sb("rz1", [P, H1])
        xn3 = ozs[:, :].rearrange("p (a f) -> p a f", a=2)
        R0 = F

        xt = sb("xt", [P, NB, FC, P])
        eb = hg[:, :, :].rearrange("p a b -> p (a b)")
        logits = sb("logits", [P, NB, NE])
        top = sb("top", [P, NB, 8])
        topi = sb("topi", [P, NB, 8], u32)
        topf = sb("topf", [P, NB, 8])
        p2 = sb("p2", [P, 4, NB])
        oh = sb("oh", [P, 2, NB, NE])
        gates = sb("gates", [P, NB, NE])
        hb = hr[:, 0, :].rearrange("p (a f) -> p a f", a=2)
        he = hr[:, 1, :].rearrange("p (a f) -> p a f", a=2)
        acc = sb("acc", [P, 2, F])
        acct = sb("acct", [P, 2, FC, P])
        yo = sb("yo", [P, 2, F])

        names = """ld_x ld_x2 ld_ctx ld_ctx2 ld_qk ld_v ld_mask ld_const ld_gate ld_w ld_rest
            free_stored st_mask masks_stored setup_zero mask_ready ident_ready gate_ready tanh_ready
            zero_lower zero_upper zero_v
            wsum_done wsum_ps wscale_done w1_done w2_done w1_abs ln_x ln_mv ln_rstd ln_pool
            xn_ready qk_ps v_ps nat_ready hi_ready rest_ready mid_ready v_ready split_chain split_ready stored stacked vz_ready
            s_ps s_max m_parts m_ps m_rows m_stored m_stacked t_ps prob_ready o_ps o_read z_recip o_scaled v_evac x0_ready mv1_ready rstd1
            dve_chain
            a_round a_ps a_bf h_ps h_lin h_gelu h_scales h_round h_rps h_bf y_ps y_read x1_ready mv2 rstd2 pool_chain
            c_xn c_ps c_evac c_kz c_kza c_vaug c_s c_dif c_exp c_tps c_pt c_ops c_ot c_ots c_oread x2_ready mv3 rstd3
            d_xn d_ps d_xt d_router d_chain d_e d_gates
            e_ps e_lin e_gelu e_acc e_tps e_acct e_yps e_y e_out ld_ew ld_eb""".split()
        S = {n: sem(n) for n in names}

        block = stack.enter_context(nc.Block())

        def pair(u):
            return (u % 2) * 4 + u // 2

        def both(tile):
            return tile[:, :].rearrange("p (w t) -> p w t", w=2)

        def v_place(i):
            return 0 if i == 3 else 3

        def maxima_place(i):
            return 1 if i == 3 else 5

        LAST = NB + 4
        QUANTISE_X = {(LAST - 2, 11): 0, (LAST - 2, 12): 1, (LAST - 1, 7): 2, (LAST - 1, 8): 3, (LAST - 1, 9): 4,
                      (LAST, 10): 5, (LAST, 11): 6, (LAST, 14): 7}
        TURN_X = {(LAST - 1, 2): 0, (LAST - 1, 3): 1, (LAST - 1, 6): 2, (LAST - 1, 7): 3,
                  (LAST, 2): 4, (LAST, 3): 5, (LAST, 4): 6, (LAST, 5): 7}

        def bcast(ap1d, n):
            return ap1d.partition_broadcast(n)

        @block.sync
        def _(sp):
            def load(name, *pairs):
                for dst, src in pairs:
                    sp.dma_start(dst, src).then_inc(S[name], 16)

            load("ld_x", (xs[:, 0, :], x_in[0]))
            load("ld_qk", (wq[:, :], wq_t), (wk[:, :], wk_t),
                 (bq[:, :], bq_in.rearrange("(p a) -> p a", a=1)), (bk[:, :], bk_in.rearrange("(p a) -> p a", a=1)))
            load("ld_ctx", (cs[:, 0, :], ctx_in[0]))
            load("ld_mask", (mask_f[:, :], mask_rows))
            load("ld_x2", (xs[:, 1:NB, :], x_in[1:NB].rearrange("b p f -> p b f")))
            for w in range(2):
                sp.dma_start(qk_rows[w, :, NT:SLOTS, :].rearrange("(h d) k t -> h d (k t)", d=D0).bitcast(u16),
                             c_free[w].rearrange("d k t -> d (k t)").unsqueeze(0).broadcast_to([H0, D0, (SLOTS - NT) * F]))\
                    .then_inc(S["free_stored"], 16)
            load("ld_ctx2", (cs[:, 1:NB, :], ctx_in[1:NB].rearrange("b p f -> p b f")))
            sp.wait_ge(S["mask_ready"], 1)
            sp.dma_start(mask_less_one, mask_b[:, :]).then_inc(S["st_mask"], 16)
            sp.wait_ge(S["st_mask"], 16)
            sp.wait_ge(S["free_stored"], 32)

            def store_masks(b):
                if b:
                    sp.wait_ge(S["stacked"], 48 * b)
                sp.dma_start(qk_rows[1, :, NT, :].rearrange("(h d) t -> d h t", d=D0)[1:4],
                             mask_less_one[b:b + 1, :].unsqueeze(1).broadcast_to([3, H0, F])).then_inc(S["masks_stored"], 16)

            def store_parts(b):
                sp.wait_ge(S["split_ready"], b + 1)
                both = parts[:, :, :].rearrange("p n t -> p (n t)")
                dst = qk_rows.rearrange("w p k t -> p w (k t)")
                for n0, first, far in ((0, 3, 3), (3, 2, 4), (5, 1, 5)):
                    src = bass.AP(both.tensor, both.offset, [list(both.ap[0]), [far * F, 2], [1, first * F]])
                    sp.dma_start(dst[:, :, n0 * F:(n0 + first) * F], src).then_inc(S["stored"], 16)

            def load_stacks(b):
                sp.wait_ge(S["stored"], 48 * (b + 1))
                sp.wait_ge(S["masks_stored"], 16 * (b + 1))
                if b >= NSTACK:
                    sp.wait_ge(S["t_ps"], NP * (b - NSTACK + 1))
                z = b % NSTACK
                rows = qk_rows.rearrange("w (a e d) k t -> w (e d k) a t", a=NP, e=2)
                sp.dma_start(qst[:, z], rows[0]).then_inc(S["stacked"], 16)
                for e in range(2):
                    r = slice(64 * e, 64 * e + 64)
                    sp.dma_start(kst[r, z, :, e, :], rows[1, r]).then_inc(S["stacked"], 16)

            def store_maxima(b):
                sp.wait_ge(S["m_rows"], b + 1)
                if b:
                    sp.wait_ge(S["m_stacked"], 32 * b)
                sp.dma_start(maxima.rearrange("l e (a t) -> (l e a) t", a=NP), mrows[:, :, :].rearrange("k a t -> k (a t)"))\
                    .then_inc(S["m_stored"], 16)

            def load_maxima(b):
                sp.wait_ge(S["m_stored"], 16 * (b + 1))
                sp.wait_ge(S["s_ps"], 16 * (b + 1))
                for e in range(2):
                    sp.dma_start(qst[64 * e + NT:64 * e + SLOTS, b % NSTACK].rearrange("p a f -> p (a f)"), maxima[:, e, :])\
                        .then_inc(S["m_stacked"], 16)

            for i in range(NB + 3):
                if i == 3:
                    store_maxima(0)
                    load_maxima(0)
                if i < NB:
                    store_masks(i)
                    store_parts(i)
                if i > 3:
                    store_maxima(i - 3)
                    load_maxima(i - 3)
                if i < NB:
                    load_stacks(i)
                if i == 0:
                    load("ld_const", (ident[:, :], c_ident), (src_mask[:, :, :], mask_cols),
                         (g_raw[:, 0:2], bcast(g_xattn, P)), (g_raw[:, 2:4], bcast(g_ffn, P)),
                         (causal[:, :], c_causal), (head_of[:, :], c_head), (iota_e[:, :], c_iota))
                    load("ld_v", (wv[:, :], wv_t), (bv[:, :], bcast(bv_in, P)))
                if i == 1:
                    load("ld_w", (w1f[:, :, :], w1_t.rearrange("(c p) h -> p c h", p=P)),
                         (w2f[:, :, :], w2_t.rearrange("(c p) f -> p c f", p=P)))
                if i == 2:
                    load("ld_gate", (gate_mask[:, :, :], bcast(mask_rows, P)))
                if i == 3:
                    load("ld_rest", (b1[:, :], bcast(b1_in, P)), (b2[:, :], bcast(b2_in, P)),
                         (rw[:, :, :], router_w.rearrange("(c p) e -> p c e", p=P)), (rb[:, :], bcast(router_b, P)),
                         (ow[:, :, :], out_w.rearrange("(c p) f -> p c f", p=P)), (ob[:, :], bcast(out_b, P)))

            sp.wait_ge(S["w1_done"], 3)
            sp.wait_ge(S["w2_done"], 3)
            for c in range(FC):
                sp.dma_start(ew[c], expert_w[:, c * P:(c + 1) * P, :].rearrange("e p d -> p e d"))\
                    .then_inc(S["ld_ew"], 16)
            sp.wait_ge(S["h_round"], NB)
            sp.dma_start(eb.rearrange("p (e d) -> p e d", e=NE), bcast(expert_b, P)).then_inc(S["ld_eb"], 16)
            for b in range(NB):
                sp.wait_ge(S["e_y"], b + 1)
                sp.dma_start(out[b], yo[:, b % 2, :]).then_inc(S["e_out"], 16)
                sp.wait_ge(S["e_out"], 16 * (b + 1))

        @block.gpsimd
        def _(pool):
            chain = [0]

            def link(ins):
                chain[0] += 1
                ins.then_inc(S["pool_chain"], 1)
                pool.wait_ge(S["pool_chain"], chain[0])

            link(pool.memset(power[:, :], -0.5))
            def rstd_of(n, b, ready, value, done):
                pool.wait_ge(S[ready], value)
                link(pool.tensor_scalar(var_eps[:, n, b:b + 1], mv[n][:, b, 1:2], EPS_LN, None, ALU.add))
                pool.tensor_tensor(rstd[:, n, b:b + 1], var_eps[:, n, b:b + 1], power[:, 0:1], ALU.pow)\
                    .then_inc(S[done], 1)

            def split(b):
                pool.wait_ge(S["hi_ready"], b + 1)
                if b:
                    pool.wait_ge(S["stored"], 48 * b)
                pool.tensor_tensor(both(rest), both(nat), hi_parts, ALU.subtract).then_inc(S["rest_ready"], 1)
                pool.wait_ge(S["mid_ready"], b + 1)
                pool.tensor_tensor(lo_parts, both(rest), mid_parts, ALU.subtract)\
                    .then_inc(S["split_ready"], 1)

            def spread_v(b):
                pool.wait_ge(S["v_evac"], b + 1)
                if b == 0:
                    pool.wait_ge(S["zero_v"], 1)
                    pool.wait_ge(S["ld_v"], 32)
                    pool.wait_ge(S["ld_const"], 16 * 7)
                pool.tensor_tensor(vsb[:, :, :], vsb[:, :, :], bv[:, :].unsqueeze(1).broadcast_to([P, 2, P]), ALU.add)\
                    .then_inc(S["v_ready"], 1)
                pool.wait_ge(S["v_ready"], b + 1)
                if b >= 2:
                    pool.wait_ge(S["o_ps"], 8 * (b - 1))
                for st in range(2):
                    dst = vz[:, b % 2, st, :].rearrange("p (r y) -> p r y", r=4)[:, :, 0:P]\
                        .rearrange("p r (j y) -> p r j y", j=4)[:, :, :, 0:D0]
                    src = vsb[:, st, :].rearrange("p (j r d) -> p r j d", j=4, r=4)
                    pool.tensor_scalar(dst, src, src_mask[:, b, st:st + 1], None, ALU.mult)\
                        .then_inc(S["vz_ready"], 1)

            def attn_out(b):
                pool.wait_ge(S["z_recip"], b + 1)
                pool.tensor_tensor(attn[:, :], ozs[:, 0:F], recip_z[:, :], ALU.mult).then_inc(S["o_scaled"], 1)
                pool.wait_ge(S["o_scaled"], b + 1)
                if b == 0:
                    pool.wait_ge(S["gate_ready"], 1)
                link(pool.tensor_tensor(attn[:, :], attn[:, :], gate_mask[:, b, :], ALU.mult))
                pool.tensor_tensor(xs[:, b, :], xs[:, b, :], attn[:, :], ALU.add).then_inc(S["x0_ready"], 1)

            for b in range(NB):
                rstd_of(0, b, "ln_mv", b + 1, "ln_rstd")
                if b < NSTACK:
                    pool.memset(kst[0:64, b, :, 1, :].bitcast(f32), 0.0).then_inc(S["zero_lower"], 1)
                if b == 0:
                    split(0)
            link(pool.memset(vaug[:, :, :, :], 0.0))
            link(pool.memset(vaug[:, :, :, D1:D1 + 1], 1.0))

            for i in range(NB + 6):
                if 1 <= i < NB:
                    split(i)
                if i >= 6:
                    rstd_of(1, i - 6, "mv1_ready", i - 5, "rstd1")
                if 5 <= i < NB + 5:
                    attn_out(i - 5)
                if 3 <= i < NB + 3:
                    spread_v(i - 3)

            def round_hidden(b):
                pool.wait_ge(S["h_scales"], b + 1)
                if b >= 2:
                    pool.wait_ge(S["h_rps"], b - 1)
                pool.tensor_scalar(hr[:, b % 2, :], hg[:, b % 2, :], amax2[:, b, 3:4], ROUND, ALU.mult, ALU.add)\
                    .then_inc(S["h_round"], 1)

            for i in range(NB + 6):
                if i >= 6:
                    rstd_of(2, i - 6, "mv2", i - 5, "rstd2")
                if 2 <= i < NB + 2:
                    round_hidden(i - 2)

            def augment_v(b):
                if b >= 2:
                    pool.wait_ge(S["c_ops"], b - 1)
                pool.tensor_copy(vaug[:, b % 2, :, 0:D1], cs[:, b, :].rearrange("p (h d) -> p h d", h=H1))\
                    .then_inc(S["c_vaug"], 1)

            for i in range(NB + 3):
                if i < NB:
                    augment_v(i)
                if i >= 3:
                    rstd_of(3, i - 3, "mv3", i - 2, "rstd3")

        @block.scalar
        def _(act):
            act.wait_ge(S["setup_zero"], 1)
            for z in range(NSTACK):
                act.activation(kst[64:P, z, :, 0, :].bitcast(f32),
                               zero[64:P, 0:1].unsqueeze(2).broadcast_to([64, NP, F // 2]), ACT.Copy)\
                    .then_inc(S["zero_upper"], 1)

            def sum_magnitudes(w, src, scratch):
                act.wait_ge(S["ld_w"], 32)
                act.activation(scratch[:, :, :].rearrange("p a b -> p (a b)"), src[:, :, :].rearrange("p a b -> p (a b)"),
                               ACT.Abs, accum_out=wsum[:, w:w + 1]).then_inc(S["w1_abs"], 1)

            def evac_qk(b):
                act.wait_ge(S["qk_ps"], b + 1)
                if b:
                    act.wait_ge(S["split_ready"], b)
                act.activation(nat[:, 0:F], PS[:, 7, 0:F], ACT.Identity, bias=bq[:, 0:1]).then_inc(S["nat_ready"], 1)
                act.activation(nat[:, F:2 * F], PS[:, 7, F:2 * F], ACT.Identity, bias=bk[:, 0:1])\
                    .then_inc(S["nat_ready"], 1)
                act.wait_ge(S["nat_ready"], 2 * (b + 1))
                if b:
                    act.wait_ge(S["stored"], 48 * b)
                act.activation(hi_parts, both(nat), ACT.Copy).then_inc(S["hi_ready"], 1)

            def middle_parts(b):
                act.wait_ge(S["rest_ready"], b + 1)
                act.activation(mid_parts, both(rest), ACT.Copy).then_inc(S["mid_ready"], 1)

            def exps(b, u):
                n = NP * b + u
                act.wait_ge(S["t_ps"], n + 1)
                if n >= 4:
                    act.wait_ge(S["o_ps"], n // 2 * 2 - 2)
                bank = 2 + 2 * (u % 2)
                act.activation(prob[:, u % 4, :], PS[:, bank:bank + 2, :].rearrange("p a f -> p (a f)"),
                               ACT.Exp, scale=SCALE0).then_inc(S["prob_ready"], 1)

            def evac_maxima(b):
                act.wait_ge(S["m_ps"], b + 1)
                if b:
                    act.wait_ge(S["m_stored"], 16 * b)
                act.activation(mrows[:, :, :].rearrange("p a t -> p (a t)"),
                               PS[0:2 * H0, 7, 0:P].bitcast(bf16), ACT.Copy).then_inc(S["m_rows"], 1)

            def evac_v(b):
                act.wait_ge(S["v_ps"], b + 1)
                if b:
                    act.wait_ge(S["vz_ready"], 2 * b)
                act.activation(vsb[:, :, :].rearrange("p a o -> p (a o)"), PS[:, 7, 0:2 * P], ACT.Copy)\
                    .then_inc(S["v_evac"], 1)

            def evac_oz(b):
                act.wait_ge(S["o_ps"], 8 * (b + 1))
                if b:
                    act.wait_ge(S["o_scaled"], b)
                act.activation(ozs[:, :], PS[:, 6, :], ACT.Copy).then_inc(S["o_read"], 1)

            def evac_x(b):
                act.wait_ge(S["a_ps"], b + 1)
                act.activation(xq[:, b, :, :].rearrange("p c t -> p (c t)"), PS[:, 7, 0:F], ACT.Copy, bias=-ROUND)\
                    .then_inc(S["a_bf"], 1)

            for i in range(NB + 5):
                for u in range(NP):
                    if 4 <= i < NB + 4:
                        exps(i - 4, u)
                    if (i, u) in TURN_X:
                        evac_x(TURN_X[i, u])
                    if i < NB and u == 0:
                        evac_qk(i)
                    if i >= 5 and u == 1:
                        evac_oz(i - 5)
                    if i < NB and u == 2:
                        middle_parts(i)
                    if 3 <= i < NB + 3 and u == v_place(i):
                        evac_v(i - 3)
                    if 3 <= i < NB + 3 and u == maxima_place(i):
                        evac_maxima(i - 3)
                if i == 2:
                    act.wait_ge(S["ld_const"], 16 * 7)
                    act.activation(tg[:, :], g_raw[:, :], ACT.Tanh).then_inc(S["tanh_ready"], 1)
                if i == 3:
                    sum_magnitudes(0, w1f, hs)
                    sum_magnitudes(1, w2f, hg)

            def gelu(b):
                act.wait_ge(S["h_lin"], b + 1)
                if b >= 2:
                    act.wait_ge(S["h_round"], b - 1)
                act.activation(hg[:, b % 2, :], hs[:, b % 2, :], ACT.Gelu).then_inc(S["h_gelu"], 1)

            def evac_h(b):
                act.wait_ge(S["h_rps"], b + 1)
                if b >= 2:
                    act.wait_ge(S["y_ps"], b - 1)
                act.activation(hq[:, b % 2, :, :].rearrange("p c t -> p (c t)"),
                               PS[:, 2:4, :].rearrange("p a f -> p (a f)"), ACT.Copy, bias=-ROUND)\
                    .then_inc(S["h_bf"], 1)

            for i in range(NB + 3):
                if 1 <= i <= NB:
                    gelu(i - 1)
                if i >= 3:
                    evac_h(i - 3)

            def evac_t(b):
                act.wait_ge(S["c_ps"], b + 1)
                if b == 0:
                    act.wait_ge(S["split_ready"], NB)
                if b >= 2:
                    act.wait_ge(S["c_s"], 2 * (b - 1))
                if b >= 1:
                    act.wait_ge(S["c_kz"], b)
                    act.wait_ge(S["c_kza"], b)
                act.activation(qt[:, b % 2, :, :].rearrange("p c t -> p (c t)"), PS[:, 7, 0:F], ACT.Copy)\
                    .then_inc(S["c_evac"], 1)
                act.activation(kt.rearrange("p c t -> p (c t)"), PS[:, 7, F:2 * F], ACT.Copy)\
                    .then_inc(S["c_evac"], 1)

            def spread_k_a(b):
                act.wait_ge(S["c_evac"], 2 * (b + 1))
                if b == 0:
                    act.wait_ge(S["t_ps"], NP * NB)
                for v in range(KA):
                    mm = act.activation(kz[:, b % 2, :, v, :], kt, ACT.Copy, scale=head_of[:, v:v + 1])
                mm.then_inc(S["c_kza"], 1)

            def exp1(b, hf):
                act.wait_ge(S["c_dif"], 2 * b + hf + 1)
                d = dif[:, b % 2, hf * NH2:(hf + 1) * NH2, :].rearrange("p h s -> p (h s)")
                act.activation(d, d, ACT.Exp, scale=SCALE1).then_inc(S["c_exp"], 1)

            def evac_p(b, hf):
                n = 2 * b + hf
                act.wait_ge(S["c_tps"], n + 1)
                if n >= 2:
                    act.wait_ge(S["c_ops"], (n - 2) // 2 + 1)
                act.activation(pt[:, hf, :, :].rearrange("p h t -> p (h t)"),
                               PS[:, 4:6, :].rearrange("p a f -> p (a f)"), ACT.Copy).then_inc(S["c_pt"], 1)

            def evac_ot(b):
                act.wait_ge(S["c_ops"], b + 1)
                if b:
                    act.wait_ge(S["c_ots"], b)
                act.activation(ot, PS[:, 6, :], ACT.Copy).then_inc(S["c_ot"], 1)

            def evac_x3(b):
                act.wait_ge(S["d_ps"], b + 1)
                act.activation(xt[:, b, :, :].rearrange("p c t -> p (c t)"), PS[:, 7, 0:F], ACT.Copy)\
                    .then_inc(S["d_xt"], 1)

            for i in range(NB + 5):
                if 3 <= i < NB + 3:
                    evac_ot(i - 3)
                if i < NB:
                    evac_t(i)
                if 2 <= i < NB + 2:
                    evac_p(i - 2, 0)
                if i >= 5:
                    evac_x3(i - 5)
                if i < NB:
                    spread_k_a(i)
                if 2 <= i < NB + 2:
                    evac_p(i - 2, 1)
                for hf in range(2):
                    if 1 <= i <= NB:
                        exp1(i - 1, hf)

            act.wait_ge(S["d_chain"], 1)
            act.activation(p2[:, 1, :], p2[:, 0, :], ACT.Exp).then_inc(S["d_e"], 1)

            def gelu_experts(n):
                act.wait_ge(S["e_lin"], n + 1)
                if n >= 2:
                    act.wait_ge(S["e_acc"], 2 * (n - 1))
                act.activation(he[:, n % 2, :], hb[:, n % 2, :], ACT.Gelu_apprx_tanh).then_inc(S["e_gelu"], 1)

            def evac_acc(b):
                act.wait_ge(S["e_tps"], b + 1)
                if b >= 2:
                    act.wait_ge(S["e_yps"], b - 1)
                act.activation(acct[:, b % 2, :, :].rearrange("p c t -> p (c t)"), PS[:, 4, 0:F], ACT.Copy)\
                    .then_inc(S["e_acct"], 1)

            for n in range(4 * NB + 3):
                if n < 4 * NB:
                    gelu_experts(n)
                if n % 4 == 2 and n >= 6:
                    evac_acc((n - 6) // 4)

        @block.vector
        def _(dve):
            chain = [0]

            def link(ins):
                chain[0] += 1
                ins.then_inc(S["dve_chain"], 1)
                dve.wait_ge(S["dve_chain"], chain[0])

            def stats_of(n, b, done):
                link(dve.bn_stats(stats[:, b % 2, :], xs[:, b, :]))
                dve.bn_aggr(mv[n][:, b, :], stats[:, b % 2, :]).then_inc(S[done], 1)

            def normalise(n, b, dst):
                return dve.tensor_scalar(dst, xs[:, b, :], mv[n][:, b, 0:1], rstd[:, n, b:b + 1],
                                         ALU.subtract, ALU.mult)

            dve.memset(zero[:, :], 0.0).then_inc(S["setup_zero"], 1)
            dve.memset(ones[:, :], 1.0)
            link(dve.memset(oz[:, :], 0.0))
            for r in range(4):
                v = oz[:, r * (P + D0):r * (P + D0) + P].rearrange("p (j y) -> p j y", j=4)[:, :, 0:D0]
                dve.memset(v, 1.0)
            def norm_x(b):
                dve.wait_ge(S["ln_rstd"], b + 1)
                if b >= 2:
                    dve.wait_ge(S["qk_ps"], b - 1)
                normalise(0, b, xn[:, b % 2, :]).then_inc(S["xn_ready"], 1)

            def row_max(b, k):
                n = 16 * b + k
                dve.wait_ge(S["s_ps"], n + 1)
                if k == 0 and b:
                    dve.wait_ge(S["m_parts"], 2 * b)
                pr, tt = k // 2, k % 2
                dve.tensor_reduce(m32[:, tt, :, pr], PS[:, k % 2, :].rearrange("p (e s) -> p e s", e=2),
                                  AX.X, ALU.max, negate=True).then_inc(S["s_max"], 1)

            def split_maxima(b):
                dve.wait_ge(S["s_max"], 16 * (b + 1))
                if b:
                    dve.wait_ge(S["m_ps"], b)
                dve.tensor_copy(mparts[:, :, 0, :, :], m32[:, :, :, :]).then_inc(S["m_parts"], 1)
                dve.wait_ge(S["m_parts"], 2 * b + 1)
                dve.tensor_tensor(mparts[:, :, 1, :, :], m32[:, :, :, :], mparts[:, :, 0, :, :], ALU.subtract)\
                    .then_inc(S["m_parts"], 1)

            def recip_sums(b):
                dve.wait_ge(S["o_read"], b + 1)
                if b:
                    dve.wait_ge(S["x0_ready"], b)
                dve.reciprocal(recip_z[:, :], ozs[:, F:2 * F]).then_inc(S["z_recip"], 1)

            def stats_x0(b):
                dve.wait_ge(S["x0_ready"], b + 1)
                stats_of(1, b, "mv1_ready")

            def weight_scales():
                dve.wait_ge(S["wsum_ps"], 1)
                link(dve.tensor_scalar(wmean[:, :], PS[:, 6, 0:2], 1.0 / (HID * F), EPS_Q, ALU.mult, ALU.max))
                dve.tensor_scalar(mean127[:, :], wmean[:, :], 1.0 / 127.0, None, ALU.mult)
                dve.reciprocal(wscale[:, :], wmean[:, :]).then_inc(S["wscale_done"], 1)
                dve.wait_ge(S["wscale_done"], 1)

            def quantise_weights(w, src, dst, done, step):
                src = src[:, :, :].rearrange("p a b -> p (a b)")
                if step:
                    dve.wait_ge(S[done], step)
                if step == 0:
                    dve.tensor_scalar(src, src, wscale[:, w:w + 1], 1.0, ALU.mult, ALU.min).then_inc(S[done], 1)
                elif step == 1:
                    dve.tensor_scalar(src, src, -1.0, ROUND, ALU.max, ALU.add).then_inc(S[done], 1)
                else:
                    dve.tensor_scalar(dst[:, :, :].rearrange("p a b -> p (a b)"), src, ROUND, None, ALU.subtract)\
                        .then_inc(S[done], 1)

            def scales(a, inv, w, b):
                link(dve.tensor_scalar(a[:, 1:2], a[:, 0:1], EPS_Q, None, ALU.max))
                dve.tensor_scalar(inv, a[:, 1:2], mean127[:, w:w + 1], None, ALU.mult)
                link(dve.reciprocal(a[:, 2:3], a[:, 1:2]))
                return dve.tensor_scalar(a[:, 3:4], a[:, 2:3], 127.0, None, ALU.mult)

            def quantise_x(b):
                dve.wait_ge(S["rstd1"], b + 1)
                if b == 0:
                    dve.wait_ge(S["split_ready"], NB)
                    dve.wait_ge(S["qk_ps"], NB)
                link(normalise(1, b, xn[:, b % 2, :]))
                link(dve.tensor_reduce(amax[:, b, 0:1], xn[:, b % 2, :], AX.X, ALU.max, apply_absolute_value=True))
                link(scales(amax[:, b, :], inv1[:, b:b + 1], 0, b))
                if b >= 2:
                    dve.wait_ge(S["a_ps"], b - 1)
                dve.tensor_scalar(xr[:, b % 2, :], xn[:, b % 2, :], amax[:, b, 3:4], ROUND, ALU.mult, ALU.add)\
                    .then_inc(S["a_round"], 1)

            dve.wait_ge(S["ld_x"], 16)
            stats_of(0, 0, "ln_mv")
            norm_x(0)
            dve.wait_ge(S["ld_mask"], 16)
            dve.tensor_scalar(mask_b[:, :], mask_f[:, :], -1.0, None, ALU.add).then_inc(S["mask_ready"], 1)
            dve.wait_ge(S["ld_x2"], 16)
            for b in range(1, NB):
                stats_of(0, b, "ln_mv")
            dve.memset(vz[:, :, :, :], 0.0).then_inc(S["zero_v"], 1)
            for i in range(NB + 5):
                if i + 1 < NB:
                    norm_x(i + 1)
                for k in range(16):
                    if 2 <= i < NB + 2:
                        row_max(i - 2, k)
                    if k == 6 and i >= 5:
                        recip_sums(i - 5)
                    if k == 10 and 4 <= i < 7:
                        quantise_weights(0, w1f, w1q, "w1_done", i - 4)
                    if k == 10 and 7 <= i < 10:
                        quantise_weights(1, w2f, w2q, "w2_done", i - 7)
                    if (i, k) in QUANTISE_X:
                        quantise_x(QUANTISE_X[i, k])
                    if k == 13 and i >= 5:
                        stats_x0(i - 5)
                if 2 <= i < NB + 2:
                    split_maxima(i - 2)
                if i == 2:
                    dve.wait_ge(S["ld_const"], 16 * 7)
                    dve.tensor_copy(ident_b[:, :], ident[:, :]).then_inc(S["ident_ready"], 1)
                    for c in range(4):
                        dve.tensor_copy(causal_b[:, c, :], causal[:, :])
                if i == 3:
                    dve.wait_ge(S["tanh_ready"], 1)
                    dve.wait_ge(S["ld_gate"], 16)
                    dve.tensor_scalar(gate_mask[:, :, :], gate_mask[:, :, :], tg[:, 0:1], None, ALU.mult)\
                        .then_inc(S["gate_ready"], 1)
                    weight_scales()

            def hidden(b):
                dve.wait_ge(S["h_ps"], b + 1)
                if b == 0:
                    dve.wait_ge(S["ld_rest"], 96)
                    dve.wait_ge(S["w1_abs"], 2)
                if b >= 2:
                    dve.wait_ge(S["h_gelu"], b - 1)
                bank = 4 * (b % 2)
                dve.scalar_tensor_tensor(out=hs[:, b % 2, :], in0=PS[:, bank:bank + 2, :].rearrange("p a f -> p (a f)"),
                                         scalar=inv1[:, b:b + 1], in1=b1[:, :], op0=ALU.mult, op1=ALU.add)\
                    .then_inc(S["h_lin"], 1)

            def hidden_scales(b):
                dve.wait_ge(S["h_gelu"], b + 1)
                link(dve.tensor_reduce(amax2[:, b, 0:1], hg[:, b % 2, :], AX.X, ALU.max, apply_absolute_value=True))
                scales(amax2[:, b, :], inv2[:, b:b + 1], 1, b).then_inc(S["h_scales"], 1)

            def ffn_out(b):
                dve.wait_ge(S["y_ps"], b + 1)
                dve.scalar_tensor_tensor(out=y_ffn[:, :], in0=PS[:, 6, 0:F], scalar=inv2[:, b:b + 1],
                                         in1=b2[:, :], op0=ALU.mult, op1=ALU.add).then_inc(S["y_read"], 1)
                dve.wait_ge(S["y_read"], b + 1)
                link(dve.scalar_tensor_tensor(out=xs[:, b, :], in0=y_ffn[:, :], scalar=tg[:, 2:3], in1=xs[:, b, :],
                                              op0=ALU.mult, op1=ALU.add))
                stats_of(2, b, "mv2")

            for i in range(NB + 5):
                if 1 <= i <= NB:
                    hidden(i - 1)
                if i >= 5:
                    ffn_out(i - 5)
                if 2 <= i < NB + 2:
                    hidden_scales(i - 2)

            def norm_1(b):
                dve.wait_ge(S["rstd2"], b + 1)
                if b >= 2:
                    dve.wait_ge(S["c_ps"], b - 1)
                normalise(2, b, xn[:, b % 2, :]).then_inc(S["c_xn"], 1)

            def spread_k(b):
                dve.wait_ge(S["c_evac"], 2 * (b + 1))
                if b == 0:
                    dve.wait_ge(S["t_ps"], NP * NB)
                if b >= 2:
                    dve.wait_ge(S["c_s"], 2 * (b - 1))
                for v in range(KA, NH2):
                    last = dve.tensor_scalar(kz[:, b % 2, :, v, :], kt, head_of[:, v:v + 1], None, ALU.mult)
                last.then_inc(S["c_kz"], 1)

            def less_max(b, hf):
                dve.wait_ge(S["c_s"], 2 * b + hf + 1)
                if b >= 2:
                    dve.wait_ge(S["c_tps"], 2 * (b - 2) + hf + 1)
                s = PS[:, 2 * hf:2 * hf + 2, :].rearrange("p a (h s) -> p (a h) s", h=4)
                link(dve.tensor_reduce(m1[:, b % 2, hf, :], s, AX.X, ALU.max))
                dve.tensor_tensor(dif[:, b % 2, hf * NH2:(hf + 1) * NH2, :], s,
                                  m1[:, b % 2, hf, :].unsqueeze(2).broadcast_to([P, NH2, P]), ALU.subtract)\
                    .then_inc(S["c_dif"], 1)

            def attn1_out(b):
                dve.wait_ge(S["c_ots"], b + 1)
                o = PS[:, 6, :].rearrange("p (h d) -> p h d", h=H1)
                link(dve.reciprocal(rz1[:, :], o[:, :, D1:D1 + 1].rearrange("p h d -> p (h d)")))
                dve.tensor_tensor(attn[:, :].rearrange("p (h d) -> p h d", h=H1), o[:, :, 0:D1],
                                  rz1[:, :].unsqueeze(2).broadcast_to([P, H1, D1]), ALU.mult).then_inc(S["c_oread"], 1)
                dve.wait_ge(S["c_oread"], b + 1)
                link(dve.scalar_tensor_tensor(out=xs[:, b, :], in0=attn[:, :], scalar=tg[:, 1:2], in1=xs[:, b, :],
                                              op0=ALU.mult, op1=ALU.add))
                stats_of(3, b, "mv3")

            def norm_3(b):
                dve.wait_ge(S["rstd3"], b + 1)
                if b >= 2:
                    dve.wait_ge(S["d_ps"], b - 1)
                normalise(3, b, xn3[:, b % 2, :]).then_inc(S["d_xn"], 1)

            norm_1(0)
            for i in range(NB + 5):
                if i + 1 < NB:
                    norm_1(i + 1)
                if 1 <= i <= NB:
                    less_max(i - 1, 0)
                if 3 <= i < NB + 3:
                    attn1_out(i - 3)
                if i < NB:
                    spread_k(i)
                if 1 <= i <= NB:
                    less_max(i - 1, 1)
                if 4 <= i < NB + 4:
                    norm_3(i - 4)

            dve.wait_ge(S["d_router"], 1)
            link(dve.tensor_tensor(logits[:, :, :], PS[:, 7, R0:R0 + NB * NE].rearrange("p (b e) -> p b e", b=NB),
                                   rb[:, :].unsqueeze(1).broadcast_to([P, NB, NE]), ALU.add))
            for b in range(NB):
                last = dve.max(top[:, b, :], logits[:, b, :])
            link(last)
            for b in range(NB):
                last = dve.max_index(topi[:, b, :], top[:, b, :], logits[:, b, :])
            link(last)
            dve.tensor_tensor(p2[:, 0, :], top[:, :, 1], top[:, :, 0], ALU.subtract).then_inc(S["d_chain"], 1)
            link(dve.tensor_copy(topf[:, :, :], topi[:, :, :]))
            io = iota_e[:, :].rearrange("p (b e) -> p b e", b=NB)
            for k in range(2):
                dve.tensor_tensor(oh[:, k, :, :], io, topf[:, :, k:k + 1].broadcast_to([P, NB, NE]), ALU.is_equal)
            dve.wait_ge(S["d_e"], 1)
            link(dve.tensor_scalar(p2[:, 2, :], p2[:, 1, :], 1.0, None, ALU.add))
            link(dve.reciprocal(p2[:, 2, :], p2[:, 2, :]))
            link(dve.tensor_tensor(p2[:, 3, :], p2[:, 1, :], p2[:, 2, :], ALU.mult))
            for k in range(2):
                link(dve.tensor_tensor(oh[:, k, :, :], oh[:, k, :, :],
                                       p2[:, 2 + k, :].unsqueeze(2).broadcast_to([P, NB, NE]), ALU.mult))
            dve.tensor_tensor(gates[:, :, :], oh[:, 0, :, :], oh[:, 1, :, :], ALU.add).then_inc(S["d_gates"], 1)
            dve.wait_ge(S["d_gates"], 1)
            dve.wait_ge(S["ld_eb"], 16)

            def expert_bias(n):
                dve.wait_ge(S["e_ps"], n + 1)
                if n >= 2:
                    dve.wait_ge(S["e_gelu"], n - 1)
                c = n % 4
                dve.tensor_tensor(hb[:, n % 2, :], PS[:, n % 4, :], eb[:, 512 * c:512 * (c + 1)], ALU.add)\
                    .then_inc(S["e_lin"], 1)

            def gate_experts(n):
                dve.wait_ge(S["e_gelu"], n + 1)
                b, c = n // 4, n % 4
                for e in range(2):
                    g = gates[:, b, 2 * c + e:2 * c + e + 1]
                    h = he[:, n % 2, e * F:(e + 1) * F]
                    if c == 0 and e == 0:
                        if b >= 2:
                            dve.wait_ge(S["e_tps"], b - 1)
                        dve.tensor_scalar(acc[:, b % 2, :], h, g, None, ALU.mult).then_inc(S["e_acc"], 1)
                    else:
                        dve.wait_ge(S["e_acc"], 2 * n + e)
                        dve.scalar_tensor_tensor(out=acc[:, b % 2, :], in0=h, scalar=g, in1=acc[:, b % 2, :],
                                                 op0=ALU.mult, op1=ALU.add).then_inc(S["e_acc"], 1)

            def result(b):
                dve.wait_ge(S["e_yps"], b + 1)
                if b >= 2:
                    dve.wait_ge(S["e_out"], 16 * (b - 1))
                link(dve.tensor_tensor(yo[:, b % 2, :], PS[:, 5, 0:F], ob[:, :], ALU.add))
                dve.scalar_tensor_tensor(out=yo[:, b % 2, :], in0=yo[:, b % 2, :], scalar=tg[:, 3:4], in1=xs[:, b, :],
                                         op0=ALU.mult, op1=ALU.add).then_inc(S["e_y"], 1)

            for n in range(4 * NB + 5):
                if n < 4 * NB:
                    expert_bias(n)
                if 1 <= n <= 4 * NB:
                    gate_experts(n - 1)
                if n >= 8 and n % 4 == 0:
                    result((n - 8) // 4)

        @block.tensor
        def _(pe):
            pe.wait_ge(S["ld_qk"], 64)
            pe.wait_ge(S["ld_ctx"], 16)

            def project_qk(b):
                pe.wait_ge(S["xn_ready"], b + 1)
                if b == 1:
                    pe.wait_ge(S["ld_ctx2"], 16)
                if b:
                    pe.wait_ge(S["nat_ready"], 2 * b)
                if b >= 4:
                    pe.wait_ge(S["m_rows"], b - 3)
                pe.matmul(PS[:, 7, 0:F], wq[:, :], xn[:, b % 2, :], start=True, stop=True)
                pe.matmul(PS[:, 7, F:2 * F], wk[:, :], cs[:, b, :], start=True, stop=True).then_inc(S["qk_ps"], 1)

            def project_v(b):
                pe.wait_ge(S["nat_ready"], 2 * min(b + 4, NB))
                if b == 0:
                    pe.wait_ge(S["ld_v"], 32)
                if b:
                    pe.wait_ge(S["m_rows"], b)
                for st in range(2):
                    mm = pe.matmul(PS[:, 7, st * P:(st + 1) * P], cs[:, b, st * P:(st + 1) * P], wv[:, :],
                                   start=True, stop=True)
                mm.then_inc(S["v_ps"], 1)

            def scores_for_max(b, k):
                n = 16 * b + k
                if k == 0:
                    pe.wait_ge(S["stacked"], 48 * (b + 1))
                    if b < NSTACK:
                        pe.wait_ge(S["zero_lower"], b + 1)
                        pe.wait_ge(S["zero_upper"], b + 1)
                if n >= 2:
                    pe.wait_ge(S["s_max"], n - 1)
                pr, tt = k // 2, k % 2
                z = b % NSTACK
                pe.matmul(PS[:, k % 2, :], qst[:, z, pr, tt * P:(tt + 1) * P],
                          kst[:, z, pr, :, :].rearrange("p e s -> p (e s)"), start=True, stop=True)\
                    .then_inc(S["s_ps"], 1)

            def turn_maxima(b):
                pe.wait_ge(S["m_parts"], 2 * (b + 1))
                pe.wait_ge(S["v_evac"], b + 1)
                if b == 0:
                    pe.wait_ge(S["ident_ready"], 1)
                for tt in range(2):
                    mm = pe.transpose(PS[0:2 * H0, 7, tt * 64:(tt + 1) * 64].bitcast(bf16),
                                      mparts[:, tt, :, :, :].rearrange("p a e k -> p (a e k)"), ident_b[:, :])
                mm.then_inc(S["m_ps"], 1)

            def scores_less_max(b, u):
                n = NP * b + u
                if u == 0:
                    pe.wait_ge(S["m_stacked"], 32 * (b + 1))
                if n >= 2:
                    pe.wait_ge(S["prob_ready"], n - 1)
                z, pr = b % NSTACK, pair(u)
                for st in range(2):
                    for e in range(2):
                        mm = pe.matmul(PS[:, 2 + 2 * (u % 2) + st, e * F:(e + 1) * F],
                                       kst[:, z, pr, e, st * P:(st + 1) * P], qst[:, z, pr, :], start=True, stop=True)
                mm.then_inc(S["t_ps"], 1)

            def weigh_values(b, g):
                r, st = g // 2, g % 2
                pe.wait_ge(S["prob_ready"], NP * b + 2 * r + 2)
                if g == 0:
                    pe.wait_ge(S["vz_ready"], 2 * (b + 1))
                    if b == 0:
                        pe.wait_ge(S["wscale_done"], 1)
                    if b:
                        pe.wait_ge(S["o_read"], b)
                for what in range(2):
                    for j in range(4):
                        w = vz[:, b % 2, st, :] if what == 0 else oz[:, :]
                        c0 = r * P + 32 * j
                        p = prob[:, (2 * r + j // 2) % 4, st * 2 * F + (j % 2) * F:st * 2 * F + (j % 2 + 1) * F]
                        mm = pe.matmul(PS[32 * j:32 * j + 32, 6, what * F:(what + 1) * F], w[:, c0:c0 + 32], p,
                                       start=(g == 0 and what == 0), stop=(g == 7), skip_group_check=True)
                mm.then_inc(S["o_ps"], 1)

            def turn_x(b):
                pe.wait_ge(S["a_round"], b + 1)
                if b == 0:
                    pe.wait_ge(S["m_rows"], NB)
                if b:
                    pe.wait_ge(S["a_bf"], b)
                for c in range(FC):
                    mm = pe.transpose(PS[:, 7, c * P:(c + 1) * P], xr[:, b % 2, c * P:(c + 1) * P], ident[:, :])
                mm.then_inc(S["a_ps"], 1)

            for i in range(NB + 5):
                for u in range(NP):
                    if u == 0 and i < NB:
                        project_qk(i)
                    if 4 <= i < NB + 4:
                        scores_less_max(i - 4, u)
                    if 2 <= i < NB + 2:
                        scores_for_max(i - 2, 2 * u)
                    if u >= 2 and 4 <= i < NB + 4:
                        weigh_values(i - 4, u - 2)
                    if u < 2 and i >= 5:
                        weigh_values(i - 5, u + 6)
                    if 2 <= i < NB + 2:
                        scores_for_max(i - 2, 2 * u + 1)
                    if u == v_place(i) and 3 <= i < NB + 3:
                        project_v(i - 3)
                    if u == maxima_place(i) and 3 <= i < NB + 3:
                        turn_maxima(i - 3)
                    if (i, u) in TURN_X:
                        turn_x(TURN_X[i, u])
                if i == 3:
                    pe.wait_ge(S["w1_abs"], 2)
                    pe.matmul(PS[:, 6, 0:2], ones[:, :], wsum[:, :], start=True, stop=True).then_inc(S["wsum_ps"], 1)

            def up(b):
                pe.wait_ge(S["a_bf"], b + 1)
                if b == 0:
                    pe.wait_ge(S["w1_done"], 3)
                    pe.wait_ge(S["s_max"], 16 * NB)
                if b == 1:
                    pe.wait_ge(S["prob_ready"], NP * NB)
                if b >= 2:
                    pe.wait_ge(S["h_lin"], b - 1)
                for hh in range(2):
                    for c in range(FC):
                        mm = pe.matmul(PS[:, 4 * (b % 2) + hh, :], xq[:, b, c, :], w1q[:, c, hh * 512:(hh + 1) * 512],
                                       start=(c == 0), stop=(c == FC - 1))
                mm.then_inc(S["h_ps"], 1)

            def turn_h(b):
                pe.wait_ge(S["h_round"], b + 1)
                if b == 0:
                    pe.wait_ge(S["prob_ready"], NP * NB)
                if b:
                    pe.wait_ge(S["h_bf"], b)
                for c in range(HC):
                    mm = pe.transpose(PS[:, 2 + c // 4, (c % 4) * P:(c % 4 + 1) * P], hr[:, b % 2, c * P:(c + 1) * P],
                                      ident[:, :])
                mm.then_inc(S["h_rps"], 1)

            def down(b):
                pe.wait_ge(S["h_bf"], b + 1)
                if b == 0:
                    pe.wait_ge(S["w2_done"], 3)
                    pe.wait_ge(S["o_read"], NB)
                if b:
                    pe.wait_ge(S["y_read"], b)
                for c in range(HC):
                    mm = pe.matmul(PS[:, 6, 0:F], hq[:, b % 2, c, :], w2q[:, c, :], start=(c == 0), stop=(c == HC - 1))
                mm.then_inc(S["y_ps"], 1)

            for i in range(NB + 4):
                if i < NB:
                    up(i)
                if 3 <= i < NB + 3:
                    turn_h(i - 3)
                if i >= 4:
                    down(i - 4)

            def turn_1(b):
                pe.wait_ge(S["c_xn"], b + 1)
                if b == 0:
                    pe.wait_ge(S["a_bf"], NB)
                if b:
                    pe.wait_ge(S["c_evac"], 2 * b)
                if b > 5:
                    pe.wait_ge(S["d_xt"], b - 5)
                for c in range(FC):
                    pe.transpose(PS[:, 7, c * P:(c + 1) * P], xn[:, b % 2, c * P:(c + 1) * P], ident[:, :])
                for c in range(FC):
                    mm = pe.transpose(PS[:, 7, F + c * P:F + (c + 1) * P], cs[:, b, c * P:(c + 1) * P], ident[:, :])
                mm.then_inc(S["c_ps"], 1)

            def scores_1(b, hf):
                pe.wait_ge(S["c_kz"], b + 1)
                pe.wait_ge(S["c_kza"], b + 1)
                if b == 0:
                    pe.wait_ge(S["h_lin"], NB)
                    pe.wait_ge(S["h_bf"], NB)
                if b:
                    pe.wait_ge(S["c_dif"], 2 * (b - 1) + hf + 1)
                for q in range(2):
                    pe.matmul(PS[:, 2 * hf + q, :], ident_b[:, :], causal_b[:, :, :].rearrange("p a s -> p (a s)"),
                              start=True, stop=False)
                    mm = pe.matmul(PS[:, 2 * hf + q, :], qt[:, b % 2, hf, :],
                                   kz[:, b % 2, hf, 4 * q:4 * q + 4, :].rearrange("p v s -> p (v s)"),
                                   start=False, stop=True)
                mm.then_inc(S["c_s"], 1)

            def turn_p(b, hf):
                n = 2 * b + hf
                pe.wait_ge(S["c_exp"], n + 1)
                if n == 0:
                    pe.wait_ge(S["h_lin"], NB)
                if n:
                    pe.wait_ge(S["c_pt"], n)
                for h in range(NH2):
                    mm = pe.transpose(PS[:, 4 + h // 4, (h % 4) * P:(h % 4 + 1) * P], dif[:, b % 2, hf * NH2 + h, :],
                                      ident[:, :])
                mm.then_inc(S["c_tps"], 1)

            def weigh_1(b):
                pe.wait_ge(S["c_pt"], 2 * (b + 1))
                pe.wait_ge(S["c_vaug"], b + 1)
                if b == 0:
                    pe.wait_ge(S["y_read"], NB)
                if b:
                    pe.wait_ge(S["c_oread"], b)
                for g in range(4):
                    for j in range(4):
                        h = 4 * g + j
                        mm = pe.matmul(PS[VC * j:VC * (j + 1), 6, g * P:(g + 1) * P], vaug[:, b % 2, h, :],
                                       pt[:, h // NH2, h % NH2, :], start=True, stop=True, skip_group_check=True)
                mm.then_inc(S["c_ops"], 1)

            def turn_o(b):
                pe.wait_ge(S["c_ot"], b + 1)
                for g in range(4):
                    mm = pe.transpose(PS[:, 6, g * P:(g + 1) * P], ot[:, g * P:(g + 1) * P], ident[:, :])
                mm.then_inc(S["c_ots"], 1)

            def turn_3(b):
                pe.wait_ge(S["d_xn"], b + 1)
                pe.wait_ge(S["c_evac"], 2 * min(b + 6, NB))
                if b:
                    pe.wait_ge(S["d_xt"], b)
                for c in range(FC):
                    mm = pe.transpose(PS[:, 7, c * P:(c + 1) * P], xn3[:, b % 2, c * P:(c + 1) * P], ident[:, :])
                mm.then_inc(S["d_ps"], 1)

            def route(b):
                pe.wait_ge(S["d_xt"], max(4, min(b + 2, NB)))
                pe.wait_ge(S["c_evac"], 2 * NB)
                for c in range(FC):
                    mm = pe.matmul(PS[:, 7, R0 + b * NE:R0 + (b + 1) * NE], xt[:, b, c, :], rw[:, c, :],
                                   start=(c == 0), stop=(c == FC - 1))
                if b == NB - 1:
                    mm.then_inc(S["d_router"], 1)

            def experts(n):
                b, q = n // 4, n % 4
                if n == 0:
                    pe.wait_ge(S["ld_ew"], 32)
                    pe.wait_ge(S["c_dif"], 2 * NB)
                if n >= 4:
                    pe.wait_ge(S["e_lin"], n - 3)
                for c in range(FC):
                    mm = pe.matmul(PS[:, q, :], xt[:, b, c, :], ew[c][:, 2 * q:2 * q + 2, :].rearrange("p e d -> p (e d)"),
                                   start=(c == 0), stop=(c == FC - 1))
                mm.then_inc(S["e_ps"], 1)

            for i in range(NB + 6):
                if i < NB:
                    turn_1(i)
                if 2 <= i < NB + 2:
                    turn_p(i - 2, 0)
                if 1 <= i <= NB:
                    scores_1(i - 1, 0)
                if 3 <= i < NB + 3:
                    turn_o(i - 3)
                if 5 <= i < NB + 5:
                    turn_3(i - 5)
                if 2 <= i < NB + 2:
                    turn_p(i - 2, 1)
                if 1 <= i <= NB:
                    scores_1(i - 1, 1)
                if i == NB:
                    for b in range(3):
                        route(b)
                if NB < i:
                    route(i - 6)
                if 2 <= i < NB + 2:
                    weigh_1(i - 2)
                if NB + 2 <= i:
                    experts(i - NB - 2)

            def turn_acc(b):
                pe.wait_ge(S["e_acc"], 8 * (b + 1))
                if b:
                    pe.wait_ge(S["e_acct"], b)
                for c in range(FC):
                    mm = pe.transpose(PS[:, 4, c * P:(c + 1) * P], acc[:, b % 2, c * P:(c + 1) * P], ident[:, :])
                mm.then_inc(S["e_tps"], 1)

            def project_out(b):
                pe.wait_ge(S["e_acct"], b + 1)
                if b:
                    pe.wait_ge(S["e_y"], b)
                for c in range(FC):
                    mm = pe.matmul(PS[:, 5, 0:F], acct[:, b % 2, c, :], ow[:, c, :], start=(c == 0), stop=(c == FC - 1))
                mm.then_inc(S["e_yps"], 1)

            for n in range(4 * NB + 4):
                if 4 <= n < 4 * NB:
                    experts(n)
                if n >= 5 and n % 4 == 1:
                    turn_acc((n - 5) // 4)
                if n >= 7 and n % 4 == 3:
                    project_out((n - 7) // 4)


def _heads_in_stack_order(n_tokens, heads):
    d = n_tokens // heads
    return [64 * jj + 32 * e + 8 * r + c for jj in range(2) for r in range(4) for e in range(2) for c in range(d)]


def kernel(**inputs):
    import concourse.bacc as _bacc
    from concourse import mybir as _mybir
    from concourse.bass_utils import run_bass_kernel_spmd as _run

    a = {k: np.asarray(v) for k, v in inputs.items()}
    NB, T, F = a["x"].shape
    order = _heads_in_stack_order(T, 16)
    mask = a["mask_Bx1x2048_fk1"].reshape(NB, F)
    laid = {
        "x": a["x"], "ctx": a["ctx_2048"],
        "mask_rows": mask, "mask_cols": mask.reshape(NB, 2, 128).transpose(2, 0, 1),
        "g_xattn": a["g_xattn"], "g_ffn": a["g_ffn"],
        "wq_t": a["L0_xattn_Wq"][order].T, "bq": a["L0_xattn_bq"][order],
        "wk_t": a["L0_xattn_Wk"][order].T, "bk": a["L0_xattn_bk"][order],
        "wv_t": a["L0_xattn_Wv"].T, "bv": a["L0_xattn_bv"],
        "w1_t": a["L0_ffn_w1"].T, "b1": a["L0_ffn_b1"], "w2_t": a["L0_ffn_w2"].T, "b2": a["L0_ffn_b2"],
        "router_w": a["L1_ffn_router_w"], "router_b": a["L1_ffn_router_b"],
        "expert_w": a["L1_ffn_expert_w"], "expert_b": a["L1_ffn_expert_b"],
        "out_w": a["L1_ffn_out_w"], "out_b": a["L1_ffn_out_b"],
    }
    nc = _bacc.Bacc("TRN2", target_bir_lowering=False, num_devices=1)
    arrays, args = {}, []
    for name, v in laid.items():
        v = np.ascontiguousarray(v)
        arrays[f"in_{name}"] = v
        args.append(nc.dram_tensor(f"in_{name}", v.shape, _mybir.dt.from_np(v.dtype), kind="ExternalInput").ap())
    args.append(nc.dram_tensor("out_0", a["x"].shape, _mybir.dt.from_np(a["x"].dtype), kind="ExternalOutput").ap())
    gated_cross_attention_blocks(nc, *args)
    r = _run(nc, [arrays], core_ids=[0])
    return r.results[0]["out_0"]
```

```python
import concourse.bass as bass
import numpy as np
from concourse import mybir
from contextlib import ExitStack


def gated_cross_attention_blocks(nc, x_in, ctx_in, mask_rows, mask_cols, g_xattn, g_ffn,
                                 wq_t, bq_in, wk_t, bk_in, wv_t, bv_in,
                                 w1_t, b1_in, w2_t, b2_in,
                                 router_w, router_b, expert_w, expert_b, out_w, out_b, out):
    f32, bf16, u16, u32 = mybir.dt.float32, mybir.dt.bfloat16, mybir.dt.uint16, mybir.dt.uint32
    ALU, ACT, AX = mybir.AluOpType, mybir.ActivationFunctionType, mybir.AxisListType

    NB, T, F = x_in.shape
    P = 128
    H0, D0 = 16, T // 16
    H1, D1 = 16, F // 16
    NP = H0 // 2
    HID = w1_t.shape[1]
    HC = HID // P
    FC = F // P
    NE = router_w.shape[1]
    EPS_LN, EPS_Q = 1e-5, 1e-5
    SCALE0, SCALE1 = float(D0) ** -0.5, float(D1) ** -0.5
    ROUND = 12582912.0
    MASKED = -1e30

    NT, SLOTS = 6, 8
    NSTACK = 5

    def bf16_bits(v):
        u = int(np.float32(v).view(np.uint32))
        return (u + 0x7FFF + ((u >> 16) & 1)) >> 16

    def bf16_value(bits):
        return float(np.uint32(bits << 16).view(np.float32))

    neg = float(np.float32(1e6 / SCALE0))
    neg_bits = []
    for _ in range(3):
        neg_bits.append(bf16_bits(neg))
        neg -= bf16_value(neg_bits[-1])
    free_rows = np.zeros((2, D0, SLOTS - NT, F), np.uint16)
    free_rows[0, 1:4, 0] = np.array(neg_bits, np.uint16)[:, None]
    free_rows[1, 0] = bf16_bits(1.0)

    c_ident = nc.inline_tensor(np.eye(P, dtype=np.float32), "c_ident").ap()
    c_causal = nc.inline_tensor(np.triu(np.full((P, P), MASKED, np.float32), 1), "c_causal").ap()
    c_free = nc.inline_tensor(free_rows, "c_free").ap()
    c_head = nc.inline_tensor((np.arange(P)[:, None] // D1 == np.arange(P // D1)[None]).astype(np.float32),
                              "c_head").ap()
    c_iota = nc.inline_tensor(np.tile(np.arange(NE, dtype=np.float32), (P, NB)), "c_iota").ap()

    qk_rows = nc.dram_tensor("qk_rows", (2, 2, P, SLOTS, F), bf16, kind="Internal").ap()
    maxima = nc.dram_tensor("maxima", (2, 2, NP * F), bf16, kind="Internal").ap()
    mask_less_one = nc.dram_tensor("mask_less_one", (NB, F), bf16, kind="Internal").ap()

    stack = ExitStack()
    with stack:
        def sb(name, shape, dt=f32):
            return stack.enter_context(nc.sbuf_tensor(name, shape, dt))

        def sem(name):
            return stack.enter_context(nc.semaphore(name))

        PS = stack.enter_context(nc.psum_tensor("PS", [P, 8, 512], f32))

        ident = sb("ident", [P, P])
        ident_b = sb("ident_b", [P, P], bf16)
        causal = sb("causal", [P, P])
        causal_b = sb("causal_b", [P, 4, P], bf16)
        head_of = sb("head_of", [P, P // D1])
        iota_e = sb("iota_e", [P, NB * NE])
        ones = sb("ones", [P, P])
        wq = sb("wq", [P, P])
        wk = sb("wk", [P, P])
        wv = sb("wv", [P, P])
        bq = sb("bq", [P, 1])
        bk = sb("bk", [P, 1])
        bv = sb("bv", [P, P])
        w1f = sb("w1f", [P, FC, HID])
        w2f = sb("w2f", [P, HC, F])
        w1q = sb("w1q", [P, FC, HID], bf16)
        w2q = sb("w2q", [P, HC, F], bf16)
        b1 = sb("b1", [P, HID])
        b2 = sb("b2", [P, F])
        rw = sb("rw", [P, FC, NE])
        rb = sb("rb", [P, NE])
        ew = [w[:, :, :].rearrange("p a b -> p (a b)").rearrange("p (e d) -> p e d", e=NE) for w in (w1f, w2f)]
        ow = sb("ow", [P, FC, F])
        ob = sb("ob", [P, F])
        g_raw = sb("g_raw", [P, 4])
        tg = sb("tg", [P, 4])
        wsum = sb("wsum", [P, 2])
        wtotal = sb("wtotal", [P, 2])
        wmean = sb("wmean", [P, 2])
        wscale = sb("wscale", [P, 2])
        mean127 = sb("mean127", [P, 2])

        xs = sb("xs", [P, NB, F])
        cs = sb("cs", [P, NB, F])
        stats = sb("stats", [P, 2, 6])
        mv = [sb(f"mv{n}", [P, NB, 2]) for n in range(4)]
        var_eps = sb("var_eps", [P, 4, NB])
        rstd = sb("rstd", [P, 4, NB])
        power = sb("power", [P, NB])
        xn = sb("xn", [P, 2, F])

        gate_mask = sb("gate_mask", [P, NB, F])
        src_mask = sb("src_mask", [P, NB, 2])
        mask_f = sb("mask_f", [NB, F])
        mask_b = sb("mask_b", [NB, F], bf16)
        nat = sb("nat", [P, 2 * F])
        rest = sb("rest", [P, 2 * F])
        parts = sb("parts", [P, 6, F], bf16)
        hi_parts, mid_parts, lo_parts = [parts[:, n:n + 1 + 5 - 2 * n:5 - 2 * n, :] for n in range(3)]
        qst = sb("qst", [P, NSTACK, NP, F], bf16)
        kst = sb("kst", [P, NSTACK, NP, 2, F], bf16)
        vsb = sb("vsb", [P, 2, P])
        VW = 4 * (P + D0)
        vz = sb("vz", [P, 2, 2, VW])
        oz = sb("oz", [P, VW])
        m32 = sb("m32", [P, 2, 2, NP])
        mparts = sb("mparts", [P, 2, 2, 2, NP], bf16)
        mrows = sb("mrows", [2 * H0, 2, P], bf16)
        wide = sb("wide", [P, 4 * 4 * F])
        prob = wide[:, :].rearrange("p (a f) -> p a f", a=4)
        recip_z = sb("recip_z", [P, F])
        attn = sb("attn", [P, F])
        zero = sb("zero", [P, 1])

        amax = sb("amax", [P, NB, 4])
        amax2 = sb("amax2", [P, NB, 4])
        inv1 = sb("inv1", [P, NB])
        inv2 = sb("inv2", [P, NB])
        xr = rest[:, :].rearrange("p (a f) -> p a f", a=2)
        ozs = sb("ozs", [P, 2 * F])
        xq = sb("xq", [P, NB, FC, P], bf16)
        hs = wide[:, 0:2 * HID].rearrange("p (a h) -> p a h", a=2)
        hg = wide[:, 2 * HID:4 * HID].rearrange("p (a h) -> p a h", a=2)
        hr = sb("hr", [P, 2, HID])
        hq = sb("hq", [P, 2, HC, P], bf16)
        y_ffn = sb("y_ffn", [P, 2, F])

        flat_k = kst[:, :, :, :, :].rearrange("p a b c d -> p (a b c d)").bitcast(f32)
        flat_q = qst[:, :, :, :].rearrange("p a b c -> p (a b c)").bitcast(f32)
        NH2 = P // D1
        KA, KG = 3, 2
        kz = flat_k[:, 0:2 * FC * NH2 * P].rearrange("p (a c v s) -> p a c v s", a=2, c=FC, v=NH2)
        qt = nat[:, :].rearrange("p (a c t) -> p a c t", a=2, c=FC)
        kt = rest[:, 0:F].rearrange("p (c s) -> p c s", c=FC)
        dif = flat_q[:, 0:2 * H1 * P].rearrange("p (a h s) -> p a h s", a=2, h=H1)
        pt = hs[:, :, :].rearrange("p a (h t) -> p a h t", h=NH2)
        VC = 32
        vaug = sb("vaug", [P, 2, H1, VC])
        ot = hr[:, 0, 0:4 * P]
        m1 = sb("m1", [P, 2, 2, NH2])
        rz1 = sb("rz1", [P, H1])
        xn3 = ozs[:, :].rearrange("p (a f) -> p a f", a=2)
        R0 = F

        xt = sb("xt", [P, NB, FC, P])
        eb = hg[:, :, :].rearrange("p a b -> p (a b)")
        logits = sb("logits", [P, NB, NE])
        top = sb("top", [P, NB, 8])
        topi = sb("topi", [P, NB, 8], u32)
        topf = sb("topf", [P, NB, 8])
        p2 = sb("p2", [P, 4, NB])
        oh = sb("oh", [P, 2, NB, NE])
        gates = sb("gates", [P, NB, NE])
        hb = hr[:, 0, :].rearrange("p (a f) -> p a f", a=2)
        he = hr[:, 1, :].rearrange("p (a f) -> p a f", a=2)
        acc = sb("acc", [P, 2, F])
        acct = sb("acct", [P, 2, FC, P])
        yo = sb("yo", [P, 2, F])

        names = """ld_x ld_x2 ld_ctx ld_ctx2 ld_qk ld_v ld_mask ld_const ld_gate ld_w ld_rest
            free_stored st_mask masks_stored setup_zero mask_ready ident_ready gate_ready tanh_ready
            zero_lower zero_upper zero_v
            wsum_ps wtotal_ready wscale_done w1_done w2_done w1_abs ln_mv ln_rstd
            xn_ready qk_ps v_ps nat_ready hi_ready rest_ready mid_ready v_ready split_ready stored stacked_even stacked_odd vz_ready
            s_ps s_max m_parts m_ps m_rows m_stored m_stacked t_ps prob_ready o_ps o_read z_recip o_scaled v_evac x0_ready mv1_ready rstd1
            dve_chain
            a_round a_ps a_bf h_ps h_lin h_gelu h_scales h_round h_rps h_bf y_ps y_read x1_ready mv2 rstd2 pool_chain
            c_xn c_ps c_evac c_kz c_kza c_kzg c_vaug c_s c_dif c_exp c_tps c_pt c_ops c_ot c_ots c_oread mv3 rstd3
            d_xn d_ps d_xt d_router d_chain d_e d_gates
            e_ps e_lin e_gelu e_acc e_tps e_acct e_yps e_y e_out ld_ew ld_eb""".split()
        S = {n: sem(n) for n in names}

        block = stack.enter_context(nc.Block())

        def pair(u):
            return (u % 2) * 4 + u // 2

        def both(tile):
            return tile[:, :].rearrange("p (w t) -> p w t", w=2)

        def stacked(b):
            return S["stacked_odd" if b % 2 else "stacked_even"]

        def stacked_count(b):
            return 48 * (b // 2 + 1)

        FIRST = 3 * NP + 6
        LAST = NB + 3
        V_PLACE, MAXIMA_PLACE = 4, 1

        def pair_at(i, u, behind):
            n = NP * i + u - behind
            return (n // NP, n % NP) if 0 <= n < NP * NB else None

        QUANTISE_X = {(LAST - 1, 11): 0, (LAST - 1, 12): 1, (LAST, 3): 2, (LAST, 4): 3, (LAST, 5): 4,
                      (LAST, 10): 5, (LAST, 14): 6}
        TURN_X = {(LAST, 2): 0, (LAST, 3): 1, (LAST, 5): 2, (LAST, 6): 3, (LAST, 7): 4}

        ADDED_BY_POOL = NB - 3

        def bcast(ap1d, n):
            return ap1d.partition_broadcast(n)

        @block.sync
        def _(sp):
            def load(name, *pairs):
                for dst, src in pairs:
                    sp.dma_start(dst, src).then_inc(S[name], 16)

            load("ld_x", (xs[:, 0, :], x_in[0]))
            load("ld_qk", (wq[:, :], wq_t), (wk[:, :], wk_t),
                 (bq[:, :], bq_in.rearrange("(p a) -> p a", a=1)), (bk[:, :], bk_in.rearrange("(p a) -> p a", a=1)))
            load("ld_ctx", (cs[:, 0, :], ctx_in[0]))
            load("ld_mask", (mask_f[:, :], mask_rows))
            load("ld_x2", (xs[:, 1:NB, :], x_in[1:NB].rearrange("b p f -> p b f")))
            def store_free_rows(z):
                for w in range(2):
                    sp.dma_start(qk_rows[z, w, :, NT:SLOTS, :].rearrange("(h d) k t -> h d (k t)", d=D0).bitcast(u16),
                                 c_free[w].rearrange("d k t -> d (k t)").unsqueeze(0)
                                 .broadcast_to([H0, D0, (SLOTS - NT) * F])).then_inc(S["free_stored"], 16)

            store_free_rows(0)
            load("ld_ctx2", (cs[:, 1:NB, :], ctx_in[1:NB].rearrange("b p f -> p b f")))
            sp.wait_ge(S["mask_ready"], 1)
            sp.dma_start(mask_less_one, mask_b[:, :]).then_inc(S["st_mask"], 16)
            sp.wait_ge(S["st_mask"], 16)
            sp.wait_ge(S["free_stored"], 32)

            def store_masks(b):
                if b == 1:
                    sp.wait_ge(S["free_stored"], 64)
                if b >= 2:
                    sp.wait_ge(stacked(b - 2), stacked_count(b - 2))
                sp.dma_start(qk_rows[b % 2, 1, :, NT, :].rearrange("(h d) t -> d h t", d=D0)[1:4],
                             mask_less_one[b:b + 1, :].unsqueeze(1).broadcast_to([3, H0, F])).then_inc(S["masks_stored"], 16)

            def store_parts(b):
                sp.wait_ge(S["split_ready"], b + 1)
                both = parts[:, :, :].rearrange("p n t -> p (n t)")
                dst = qk_rows[b % 2].rearrange("w p k t -> p w (k t)")
                for n0, first, far in ((0, 3, 3), (3, 2, 4), (5, 1, 5)):
                    src = bass.AP(both.tensor, both.offset, [list(both.ap[0]), [far * F, 2], [1, first * F]])
                    sp.dma_start(dst[:, :, n0 * F:(n0 + first) * F], src).then_inc(S["stored"], 16)

            def load_stacks(b):
                sp.wait_ge(S["stored"], 48 * (b + 1))
                sp.wait_ge(S["masks_stored"], 16 * (b + 1))
                if b >= NSTACK:
                    sp.wait_ge(S["t_ps"], NP * (b - NSTACK + 1))
                z = b % NSTACK
                rows = qk_rows[b % 2].rearrange("w (a e d) k t -> w (e d k) a t", a=NP, e=2)
                sp.dma_start(qst[:, z], rows[0]).then_inc(stacked(b), 16)
                for e in range(2):
                    r = slice(64 * e, 64 * e + 64)
                    sp.dma_start(kst[r, z, :, e, :], rows[1, r]).then_inc(stacked(b), 16)

            def store_maxima(b):
                sp.wait_ge(S["m_rows"], b + 1)
                if b:
                    sp.wait_ge(S["m_stacked"], 32 * b)
                sp.dma_start(maxima.rearrange("l e (a t) -> (l e a) t", a=NP), mrows[:, :, :].rearrange("k a t -> k (a t)"))\
                    .then_inc(S["m_stored"], 16)

            def load_maxima(b):
                sp.wait_ge(S["m_stored"], 16 * (b + 1))
                sp.wait_ge(S["s_ps"], 16 * (b + 1))
                for e in range(2):
                    sp.dma_start(qst[64 * e + NT:64 * e + SLOTS, b % NSTACK].rearrange("p a f -> p (a f)"), maxima[:, e, :])\
                        .then_inc(S["m_stacked"], 16)

            for i in range(NB + 3):
                if i >= 3:
                    store_maxima(i - 3)
                    load_maxima(i - 3)
                if i < NB:
                    store_masks(i)
                    store_parts(i)
                if i < NB:
                    load_stacks(i)
                if i == 0:
                    store_free_rows(1)
                    load("ld_const", (ident[:, :], c_ident), (src_mask[:, :, :], mask_cols),
                         (g_raw[:, 0:2], bcast(g_xattn, P)), (g_raw[:, 2:4], bcast(g_ffn, P)),
                         (causal[:, :], c_causal), (head_of[:, :], c_head), (iota_e[:, :], c_iota))
                    load("ld_v", (wv[:, :], wv_t), (bv[:, :], bcast(bv_in, P)))
                if i == 3:
                    load("ld_gate", (gate_mask[:, :, :], bcast(mask_rows, P)))
                if i == 4:
                    load("ld_w", (w1f[:, :, :], w1_t.rearrange("(c p) h -> p c h", p=P)))
                if i == 5:
                    load("ld_w", (w2f[:, :, :], w2_t.rearrange("(c p) f -> p c f", p=P)))
                if i == 6:
                    load("ld_rest", (b1[:, :], bcast(b1_in, P)), (b2[:, :], bcast(b2_in, P)),
                         (rw[:, :, :], router_w.rearrange("(c p) e -> p c e", p=P)), (rb[:, :], bcast(router_b, P)),
                         (ow[:, :, :], out_w.rearrange("(c p) f -> p c f", p=P)), (ob[:, :], bcast(out_b, P)))

            sp.wait_ge(S["w1_done"], 3)
            sp.wait_ge(S["w2_done"], 3)
            for c in range(FC):
                sp.dma_start(ew[c], expert_w[:, c * P:(c + 1) * P, :].rearrange("e p d -> p e d"))\
                    .then_inc(S["ld_ew"], 16)
            sp.wait_ge(S["h_round"], NB)
            sp.dma_start(eb.rearrange("p (e d) -> p e d", e=NE), bcast(expert_b, P)).then_inc(S["ld_eb"], 16)
            for b in range(NB):
                sp.wait_ge(S["e_y"], b + 1)
                sp.dma_start(out[b], yo[:, b % 2, :]).then_inc(S["e_out"], 16)
                sp.wait_ge(S["e_out"], 16 * (b + 1))

        @block.gpsimd
        def _(pool):
            chain = [0]

            def link(ins):
                chain[0] += 1
                ins.then_inc(S["pool_chain"], 1)
                pool.wait_ge(S["pool_chain"], chain[0])

            link(pool.memset(power[:, :], -0.5))
            def rstd_of(n, b, ready, value, done):
                pool.wait_ge(S[ready], value)
                link(pool.tensor_scalar(var_eps[:, n, b:b + 1], mv[n][:, b, 1:2], EPS_LN, None, ALU.add))
                pool.tensor_tensor(rstd[:, n, b:b + 1], var_eps[:, n, b:b + 1], power[:, 0:1], ALU.pow)\
                    .then_inc(S[done], 1)

            def split(b):
                pool.wait_ge(S["hi_ready"], b + 1)
                if b:
                    pool.wait_ge(S["stored"], 48 * b)
                pool.tensor_tensor(both(rest), both(nat), hi_parts, ALU.subtract).then_inc(S["rest_ready"], 1)
                pool.wait_ge(S["mid_ready"], b + 1)
                pool.tensor_tensor(lo_parts, both(rest), mid_parts, ALU.subtract)\
                    .then_inc(S["split_ready"], 1)

            def spread_v(b):
                pool.wait_ge(S["v_evac"], b + 1)
                if b == 0:
                    pool.wait_ge(S["zero_v"], 1)
                    pool.wait_ge(S["ld_v"], 32)
                    pool.wait_ge(S["ld_const"], 16 * 7)
                pool.tensor_tensor(vsb[:, :, :], vsb[:, :, :], bv[:, :].unsqueeze(1).broadcast_to([P, 2, P]), ALU.add)\
                    .then_inc(S["v_ready"], 1)
                pool.wait_ge(S["v_ready"], b + 1)
                if b >= 2:
                    pool.wait_ge(S["o_ps"], 8 * (b - 1))
                for st in range(2):
                    dst = vz[:, b % 2, st, :].rearrange("p (r y) -> p r y", r=4)[:, :, 0:P]\
                        .rearrange("p r (j y) -> p r j y", j=4)[:, :, :, 0:D0]
                    src = vsb[:, st, :].rearrange("p (j r d) -> p r j d", j=4, r=4)
                    pool.tensor_scalar(dst, src, src_mask[:, b, st:st + 1], None, ALU.mult)\
                        .then_inc(S["vz_ready"], 1)

            def attn_out(b):
                pool.wait_ge(S["z_recip"], b + 1)
                pool.tensor_tensor(attn[:, :], ozs[:, 0:F], recip_z[:, :], ALU.mult).then_inc(S["o_scaled"], 1)
                pool.wait_ge(S["o_scaled"], b + 1)
                if b == 0:
                    pool.wait_ge(S["gate_ready"], 1)
                link(pool.tensor_tensor(attn[:, :], attn[:, :], gate_mask[:, b, :], ALU.mult))
                pool.tensor_tensor(xs[:, b, :], xs[:, b, :], attn[:, :], ALU.add).then_inc(S["x0_ready"], 1)

            for b in range(NB):
                rstd_of(0, b, "ln_mv", b + 1, "ln_rstd")
                if b < NSTACK:
                    pool.memset(kst[0:64, b, :, 1, :].bitcast(f32), 0.0).then_inc(S["zero_lower"], 1)
                if b == 0:
                    split(0)
            link(pool.memset(vaug[:, :, :, :], 0.0))
            link(pool.memset(vaug[:, :, :, D1:D1 + 1], 1.0))

            for i in range(NB + 6):
                if 1 <= i < NB:
                    split(i)
                if i >= 6:
                    rstd_of(1, i - 6, "mv1_ready", i - 5, "rstd1")
                if 5 <= i < NB + 5:
                    attn_out(i - 5)
                if 3 <= i < NB + 3:
                    spread_v(i - 3)

            def round_hidden(b):
                pool.wait_ge(S["h_scales"], b + 1)
                if b >= 2:
                    pool.wait_ge(S["h_rps"], b - 1)
                pool.tensor_scalar(hr[:, b % 2, :], hg[:, b % 2, :], amax2[:, b, 3:4], ROUND, ALU.mult, ALU.add)\
                    .then_inc(S["h_round"], 1)

            def augment_v(b):
                if b >= 2:
                    pool.wait_ge(S["c_ops"], b - 1)
                pool.tensor_copy(vaug[:, b % 2, :, 0:D1], cs[:, b, :].rearrange("p (h d) -> p h d", h=H1))\
                    .then_inc(S["c_vaug"], 1)

            def spread_k_g(b):
                pool.wait_ge(S["c_evac"], 2 * (b + 1))
                if b == 1:
                    pool.wait_ge(S["t_ps"], NP * NB)
                if b >= 2:
                    pool.wait_ge(S["c_s"], 2 * (b - 1))
                for v in range(KA, KA + KG):
                    last = pool.tensor_scalar(kz[:, b % 2, :, v, :], kt, head_of[:, v:v + 1], None, ALU.mult)
                last.then_inc(S["c_kzg"], 1)

            def add_ffn(b):
                pool.wait_ge(S["y_read"], b + 1)
                link(pool.tensor_scalar(y_ffn[:, b % 2, :], y_ffn[:, b % 2, :], tg[:, 2:3], None, ALU.mult))
                pool.tensor_tensor(xs[:, b, :], xs[:, b, :], y_ffn[:, b % 2, :], ALU.add).then_inc(S["x1_ready"], 1)

            for i in range(NB + 7):
                if 5 <= i < ADDED_BY_POOL + 5:
                    add_ffn(i - 5)
                if 2 <= i < NB + 2:
                    round_hidden(i - 2)
                if 6 <= i < NB + 6:
                    rstd_of(2, i - 6, "mv2", i - 5, "rstd2")
                if i == NB + 1:
                    augment_v(0)

            for i in range(1, NB + 3):
                if i < NB:
                    spread_k_g(i)
                    augment_v(i)
                if i >= 3:
                    rstd_of(3, i - 3, "mv3", i - 2, "rstd3")

        @block.scalar
        def _(act):
            act.wait_ge(S["setup_zero"], 1)
            for z in range(NSTACK):
                act.activation(kst[64:P, z, :, 0, :].bitcast(f32),
                               zero[64:P, 0:1].unsqueeze(2).broadcast_to([64, NP, F // 2]), ACT.Copy)\
                    .then_inc(S["zero_upper"], 1)

            def sum_magnitudes(w, src):
                act.wait_ge(S["ld_w"], 32)
                if w:
                    act.wait_ge(S["w1_abs"], w)
                act.activation(hr[:, :, :].rearrange("p a b -> p (a b)"), src[:, :, :].rearrange("p a b -> p (a b)"),
                               ACT.Abs, accum_out=wsum[:, w:w + 1]).then_inc(S["w1_abs"], 1)

            def evac_qk(b):
                act.wait_ge(S["qk_ps"], b + 1)
                if b:
                    act.wait_ge(S["split_ready"], b)
                act.activation(nat[:, 0:F], PS[:, 7, 0:F], ACT.Identity, bias=bq[:, 0:1]).then_inc(S["nat_ready"], 1)
                act.activation(nat[:, F:2 * F], PS[:, 7, F:2 * F], ACT.Identity, bias=bk[:, 0:1])\
                    .then_inc(S["nat_ready"], 1)
                act.wait_ge(S["nat_ready"], 2 * (b + 1))
                if b:
                    act.wait_ge(S["stored"], 48 * b)
                act.activation(hi_parts, both(nat), ACT.Copy).then_inc(S["hi_ready"], 1)

            def middle_parts(b):
                act.wait_ge(S["rest_ready"], b + 1)
                act.activation(mid_parts, both(rest), ACT.Copy).then_inc(S["mid_ready"], 1)

            def exps(b, u):
                n = NP * b + u
                act.wait_ge(S["t_ps"], n + 1)
                if n >= 4:
                    act.wait_ge(S["o_ps"], n // 2 * 2 - 2)
                bank = 2 + 2 * (u % 2)
                act.activation(prob[:, u % 4, :], PS[:, bank:bank + 2, :].rearrange("p a f -> p (a f)"),
                               ACT.Exp, scale=SCALE0).then_inc(S["prob_ready"], 1)

            def evac_maxima(b):
                act.wait_ge(S["m_ps"], b + 1)
                if b:
                    act.wait_ge(S["m_stored"], 16 * b)
                act.activation(mrows[:, :, :].rearrange("p a t -> p (a t)"),
                               PS[0:2 * H0, 7, 0:P].bitcast(bf16), ACT.Copy).then_inc(S["m_rows"], 1)

            def evac_v(b):
                act.wait_ge(S["v_ps"], b + 1)
                if b:
                    act.wait_ge(S["vz_ready"], 2 * b)
                act.activation(vsb[:, :, :].rearrange("p a o -> p (a o)"), PS[:, 7, 0:2 * P], ACT.Copy)\
                    .then_inc(S["v_evac"], 1)

            def evac_oz(b):
                act.wait_ge(S["o_ps"], 8 * (b + 1))
                if b:
                    act.wait_ge(S["o_scaled"], b)
                act.activation(ozs[:, :], PS[:, 6, :], ACT.Copy).then_inc(S["o_read"], 1)

            def evac_weight_sums():
                act.wait_ge(S["wsum_ps"], 1)
                act.activation(wtotal[:, :], PS[:, 7, F:F + 2], ACT.Copy).then_inc(S["wtotal_ready"], 1)

            def evac_x(b):
                act.wait_ge(S["a_ps"], b + 1)
                act.activation(xq[:, b, :, :].rearrange("p c t -> p (c t)"), PS[:, 7, 0:F], ACT.Copy, bias=-ROUND)\
                    .then_inc(S["a_bf"], 1)

            for i in range(LAST + 1):
                for u in range(NP):
                    at = pair_at(i, u, FIRST)
                    if at:
                        exps(*at)
                    if (i, u) in TURN_X:
                        evac_x(TURN_X[i, u])
                    if i < NB and u == 0:
                        evac_qk(i)
                    at = pair_at(i, u, FIRST + 2)
                    if at and at[1] == NP - 1:
                        evac_oz(at[0])
                    if i < NB and u == 2:
                        middle_parts(i)
                    if i == NB and u == 1:
                        evac_weight_sums()
                    if 3 <= i < NB + 3 and u == MAXIMA_PLACE:
                        evac_maxima(i - 3)
                    if 3 <= i < NB + 3 and u == V_PLACE:
                        evac_v(i - 3)
                if i == 2:
                    act.wait_ge(S["ld_const"], 16 * 7)
                    act.activation(tg[:, :], g_raw[:, :], ACT.Tanh).then_inc(S["tanh_ready"], 1)
                if i == 6:
                    sum_magnitudes(0, w1f)
                if i == 7:
                    sum_magnitudes(1, w2f)

            def gelu(b):
                act.wait_ge(S["h_lin"], b + 1)
                if b >= 2:
                    act.wait_ge(S["h_round"], b - 1)
                act.activation(hg[:, b % 2, :], hs[:, b % 2, :], ACT.Gelu).then_inc(S["h_gelu"], 1)

            def evac_h(b):
                act.wait_ge(S["h_rps"], b + 1)
                if b >= 2:
                    act.wait_ge(S["y_ps"], b - 1)
                act.activation(hq[:, b % 2, :, :].rearrange("p c t -> p (c t)"),
                               PS[:, 2:4, :].rearrange("p a f -> p (a f)"), ACT.Copy, bias=-ROUND)\
                    .then_inc(S["h_bf"], 1)

            def evac_t(b):
                act.wait_ge(S["c_ps"], b + 1)
                if b == 0:
                    act.wait_ge(S["split_ready"], NB)
                if b >= 2:
                    act.wait_ge(S["c_s"], 2 * (b - 1))
                if b >= 1:
                    act.wait_ge(S["c_kz"], b)
                    act.wait_ge(S["c_kza"], b)
                if b >= 2:
                    act.wait_ge(S["c_kzg"], b - 1)
                act.activation(qt[:, b % 2, :, :].rearrange("p c t -> p (c t)"), PS[:, 7, 0:F], ACT.Copy)\
                    .then_inc(S["c_evac"], 1)
                act.activation(kt.rearrange("p c t -> p (c t)"), PS[:, 7, F:2 * F], ACT.Copy)\
                    .then_inc(S["c_evac"], 1)

            def spread_k_a(b):
                act.wait_ge(S["c_evac"], 2 * (b + 1))
                if b == 0:
                    act.wait_ge(S["t_ps"], NP * NB)
                for v in range(KA):
                    mm = act.activation(kz[:, b % 2, :, v, :], kt, ACT.Copy, scale=head_of[:, v:v + 1])
                mm.then_inc(S["c_kza"], 1)

            for i in range(NB + 3):
                if 1 <= i <= NB:
                    gelu(i - 1)
                if i >= 3:
                    evac_h(i - 3)
                if i in (2, 3, 4):
                    evac_x(NB + i - 5)
                if i == NB + 1:
                    evac_t(0)
                    spread_k_a(0)

            def exp1(b, hf):
                act.wait_ge(S["c_dif"], 2 * b + hf + 1)
                d = dif[:, b % 2, hf * NH2:(hf + 1) * NH2, :].rearrange("p h s -> p (h s)")
                act.activation(d, d, ACT.Exp, scale=SCALE1).then_inc(S["c_exp"], 1)

            def evac_p(b, hf):
                n = 2 * b + hf
                act.wait_ge(S["c_tps"], n + 1)
                if n >= 2:
                    act.wait_ge(S["c_ops"], (n - 2) // 2 + 1)
                act.activation(pt[:, hf, :, :].rearrange("p h t -> p (h t)"),
                               PS[:, 4:6, :].rearrange("p a f -> p (a f)"), ACT.Copy).then_inc(S["c_pt"], 1)

            def evac_ot(b):
                act.wait_ge(S["c_ops"], b + 1)
                if b:
                    act.wait_ge(S["c_ots"], b)
                act.activation(ot, PS[:, 6, :], ACT.Copy).then_inc(S["c_ot"], 1)

            def evac_x3(b):
                act.wait_ge(S["d_ps"], b + 1)
                act.activation(xt[:, b, :, :].rearrange("p c t -> p (c t)"), PS[:, 7, 0:F], ACT.Copy)\
                    .then_inc(S["d_xt"], 1)

            for i in range(NB + 5):
                if 3 <= i < NB + 3:
                    evac_ot(i - 3)
                if 1 <= i < NB:
                    evac_t(i)
                if 2 <= i < NB + 2:
                    evac_p(i - 2, 0)
                if i >= 5:
                    evac_x3(i - 5)
                if 1 <= i < NB:
                    spread_k_a(i)
                if 2 <= i < NB + 2:
                    evac_p(i - 2, 1)
                for hf in range(2):
                    if 1 <= i <= NB:
                        exp1(i - 1, hf)

            act.wait_ge(S["d_chain"], 1)
            act.activation(p2[:, 1, :], p2[:, 0, :], ACT.Exp).then_inc(S["d_e"], 1)

            def gelu_experts(n):
                act.wait_ge(S["e_lin"], n + 1)
                if n >= 2:
                    act.wait_ge(S["e_acc"], 2 * (n - 1))
                act.activation(he[:, n % 2, :], hb[:, n % 2, :], ACT.Gelu_apprx_tanh).then_inc(S["e_gelu"], 1)

            def evac_acc(b):
                act.wait_ge(S["e_tps"], b + 1)
                if b >= 2:
                    act.wait_ge(S["e_yps"], b - 1)
                act.activation(acct[:, b % 2, :, :].rearrange("p c t -> p (c t)"), PS[:, 4, 0:F], ACT.Copy)\
                    .then_inc(S["e_acct"], 1)

            for n in range(4 * NB + 3):
                if n < 4 * NB:
                    gelu_experts(n)
                if n % 4 == 2 and n >= 6:
                    evac_acc((n - 6) // 4)

        @block.vector
        def _(dve):
            chain = [0]

            def link(ins):
                chain[0] += 1
                ins.then_inc(S["dve_chain"], 1)
                dve.wait_ge(S["dve_chain"], chain[0])

            def stats_of(n, b, done):
                link(dve.bn_stats(stats[:, b % 2, :], xs[:, b, :]))
                dve.bn_aggr(mv[n][:, b, :], stats[:, b % 2, :]).then_inc(S[done], 1)

            def normalise(n, b, dst):
                return dve.tensor_scalar(dst, xs[:, b, :], mv[n][:, b, 0:1], rstd[:, n, b:b + 1],
                                         ALU.subtract, ALU.mult)

            dve.memset(zero[:, :], 0.0).then_inc(S["setup_zero"], 1)
            dve.memset(ones[:, :], 1.0)
            link(dve.memset(oz[:, :], 0.0))
            for r in range(4):
                v = oz[:, r * (P + D0):r * (P + D0) + P].rearrange("p (j y) -> p j y", j=4)[:, :, 0:D0]
                dve.memset(v, 1.0)
            def norm_x(b):
                dve.wait_ge(S["ln_rstd"], b + 1)
                if b >= 2:
                    dve.wait_ge(S["qk_ps"], b - 1)
                normalise(0, b, xn[:, b % 2, :]).then_inc(S["xn_ready"], 1)

            def row_max(b, k):
                n = 16 * b + k
                dve.wait_ge(S["s_ps"], n + 1)
                if k == 0 and b:
                    dve.wait_ge(S["m_parts"], 2 * b)
                pr, tt = k // 2, k % 2
                dve.tensor_reduce(m32[:, tt, :, pr], PS[:, k % 2, :].rearrange("p (e s) -> p e s", e=2),
                                  AX.X, ALU.max, negate=True).then_inc(S["s_max"], 1)

            def split_maxima(b):
                dve.wait_ge(S["s_max"], 16 * (b + 1))
                if b:
                    dve.wait_ge(S["m_ps"], b)
                dve.tensor_copy(mparts[:, :, 0, :, :], m32[:, :, :, :]).then_inc(S["m_parts"], 1)
                dve.wait_ge(S["m_parts"], 2 * b + 1)
                dve.tensor_tensor(mparts[:, :, 1, :, :], m32[:, :, :, :], mparts[:, :, 0, :, :], ALU.subtract)\
                    .then_inc(S["m_parts"], 1)

            def recip_sums(b):
                dve.wait_ge(S["o_read"], b + 1)
                if b:
                    dve.wait_ge(S["x0_ready"], b)
                dve.reciprocal(recip_z[:, :], ozs[:, F:2 * F]).then_inc(S["z_recip"], 1)

            def stats_x0(b):
                dve.wait_ge(S["x0_ready"], b + 1)
                stats_of(1, b, "mv1_ready")

            def weight_scales():
                dve.wait_ge(S["wtotal_ready"], 1)
                link(dve.tensor_scalar(wmean[:, :], wtotal[:, :], 1.0 / (HID * F), EPS_Q, ALU.mult, ALU.max))
                dve.tensor_scalar(mean127[:, :], wmean[:, :], 1.0 / 127.0, None, ALU.mult)
                dve.reciprocal(wscale[:, :], wmean[:, :]).then_inc(S["wscale_done"], 1)
                dve.wait_ge(S["wscale_done"], 1)

            def quantise_weights(w, src, dst, done, step):
                src = src[:, :, :].rearrange("p a b -> p (a b)")
                if step:
                    dve.wait_ge(S[done], step)
                if step == 0:
                    dve.tensor_scalar(src, src, wscale[:, w:w + 1], 1.0, ALU.mult, ALU.min).then_inc(S[done], 1)
                elif step == 1:
                    dve.tensor_scalar(src, src, -1.0, ROUND, ALU.max, ALU.add).then_inc(S[done], 1)
                else:
                    dve.tensor_scalar(dst[:, :, :].rearrange("p a b -> p (a b)"), src, ROUND, None, ALU.subtract)\
                        .then_inc(S[done], 1)

            def scales(a, inv, w):
                link(dve.tensor_scalar(a[:, 1:2], a[:, 0:1], EPS_Q, None, ALU.max))
                dve.tensor_scalar(inv, a[:, 1:2], mean127[:, w:w + 1], None, ALU.mult)
                link(dve.reciprocal(a[:, 2:3], a[:, 1:2]))
                return dve.tensor_scalar(a[:, 3:4], a[:, 2:3], 127.0, None, ALU.mult)

            def quantise_x(b):
                dve.wait_ge(S["rstd1"], b + 1)
                if b == 0:
                    dve.wait_ge(S["split_ready"], NB)
                    dve.wait_ge(S["qk_ps"], NB)
                link(normalise(1, b, xn[:, b % 2, :]))
                link(dve.tensor_reduce(amax[:, b, 0:1], xn[:, b % 2, :], AX.X, ALU.max, apply_absolute_value=True))
                link(scales(amax[:, b, :], inv1[:, b:b + 1], 0))
                if b >= 2:
                    dve.wait_ge(S["a_ps"], b - 1)
                dve.tensor_scalar(xr[:, b % 2, :], xn[:, b % 2, :], amax[:, b, 3:4], ROUND, ALU.mult, ALU.add)\
                    .then_inc(S["a_round"], 1)

            dve.wait_ge(S["ld_x"], 16)
            stats_of(0, 0, "ln_mv")
            norm_x(0)
            dve.wait_ge(S["ld_mask"], 16)
            dve.tensor_scalar(mask_b[:, :], mask_f[:, :], -1.0, None, ALU.add).then_inc(S["mask_ready"], 1)
            dve.wait_ge(S["ld_x2"], 16)
            for b in range(1, NB):
                stats_of(0, b, "ln_mv")
            dve.memset(vz[:, :, :, :], 0.0).then_inc(S["zero_v"], 1)
            for i in range(NB + 5):
                if i + 1 < NB:
                    norm_x(i + 1)
                for k in range(16):
                    if 2 <= i < NB + 2:
                        row_max(i - 2, k)
                    if k == 3 and i >= 5:
                        recip_sums(i - 5)
                    if i == NB and k == 8:
                        weight_scales()
                    if i == NB + 1 and k in (4, 8, 12):
                        quantise_weights(0, w1f, w1q, "w1_done", k // 4 - 1)
                    if i == NB + 2 and k in (7, 8, 9):
                        quantise_weights(1, w2f, w2q, "w2_done", k - 7)
                    if (i, k) in QUANTISE_X:
                        quantise_x(QUANTISE_X[i, k])
                    if k == 8 and 5 <= i < NB + 4:
                        stats_x0(i - 5)
                if 2 <= i < NB + 2:
                    split_maxima(i - 2)
                if i == 2:
                    dve.wait_ge(S["ld_const"], 16 * 7)
                    dve.tensor_copy(ident_b[:, :], ident[:, :]).then_inc(S["ident_ready"], 1)
                    for c in range(4):
                        dve.tensor_copy(causal_b[:, c, :], causal[:, :])
                if i == 4:
                    dve.wait_ge(S["tanh_ready"], 1)
                    dve.wait_ge(S["ld_gate"], 16)
                    dve.tensor_scalar(gate_mask[:, :, :], gate_mask[:, :, :], tg[:, 0:1], None, ALU.mult)\
                        .then_inc(S["gate_ready"], 1)

            def hidden(b):
                dve.wait_ge(S["h_ps"], b + 1)
                if b == 0:
                    dve.wait_ge(S["ld_rest"], 96)
                    dve.wait_ge(S["w1_abs"], 2)
                if b >= 2:
                    dve.wait_ge(S["h_gelu"], b - 1)
                bank = 4 * (b % 2)
                dve.scalar_tensor_tensor(out=hs[:, b % 2, :], in0=PS[:, bank:bank + 2, :].rearrange("p a f -> p (a f)"),
                                         scalar=inv1[:, b:b + 1], in1=b1[:, :], op0=ALU.mult, op1=ALU.add)\
                    .then_inc(S["h_lin"], 1)

            def hidden_scales(b):
                dve.wait_ge(S["h_gelu"], b + 1)
                link(dve.tensor_reduce(amax2[:, b, 0:1], hg[:, b % 2, :], AX.X, ALU.max, apply_absolute_value=True))
                scales(amax2[:, b, :], inv2[:, b:b + 1], 1).then_inc(S["h_scales"], 1)

            def ffn_out(b):
                dve.wait_ge(S["y_ps"], b + 1)
                if b >= 2:
                    dve.wait_ge(S["x1_ready"], min(b - 1, ADDED_BY_POOL))
                dve.scalar_tensor_tensor(out=y_ffn[:, b % 2, :], in0=PS[:, 6, 0:F], scalar=inv2[:, b:b + 1],
                                         in1=b2[:, :], op0=ALU.mult, op1=ALU.add).then_inc(S["y_read"], 1)

            def stats_x1(b):
                if b < ADDED_BY_POOL:
                    dve.wait_ge(S["x1_ready"], b + 1)
                else:
                    dve.wait_ge(S["y_read"], b + 1)
                    link(dve.scalar_tensor_tensor(out=xs[:, b, :], in0=y_ffn[:, b % 2, :], scalar=tg[:, 2:3],
                                                  in1=xs[:, b, :], op0=ALU.mult, op1=ALU.add))
                stats_of(2, b, "mv2")

            def norm_1(b):
                dve.wait_ge(S["rstd2"], b + 1)
                if b >= 2:
                    dve.wait_ge(S["c_ps"], b - 1)
                normalise(2, b, xn[:, b % 2, :]).then_inc(S["c_xn"], 1)

            def spread_k(b):
                dve.wait_ge(S["c_evac"], 2 * (b + 1))
                if b == 0:
                    dve.wait_ge(S["t_ps"], NP * NB)
                if b >= 2:
                    dve.wait_ge(S["c_s"], 2 * (b - 1))
                for v in range(KA + KG if b else KA, NH2):
                    last = dve.tensor_scalar(kz[:, b % 2, :, v, :], kt, head_of[:, v:v + 1], None, ALU.mult)
                last.then_inc(S["c_kz"], 1)

            def less_max(b, hf):
                dve.wait_ge(S["c_s"], 2 * b + hf + 1)
                if b >= 2:
                    dve.wait_ge(S["c_tps"], 2 * (b - 2) + hf + 1)
                s = PS[:, 2 * hf:2 * hf + 2, :].rearrange("p a (h s) -> p (a h) s", h=4)
                link(dve.tensor_reduce(m1[:, b % 2, hf, :], s, AX.X, ALU.max))
                dve.tensor_tensor(dif[:, b % 2, hf * NH2:(hf + 1) * NH2, :], s,
                                  m1[:, b % 2, hf, :].unsqueeze(2).broadcast_to([P, NH2, P]), ALU.subtract)\
                    .then_inc(S["c_dif"], 1)

            for i in range(NB + 6):
                if 1 <= i <= NB:
                    hidden(i - 1)
                if i == 2:
                    stats_x0(NB - 1)
                if i == 3:
                    quantise_x(NB - 1)
                if 5 <= i < NB + 5:
                    ffn_out(i - 5)
                if 6 <= i < ADDED_BY_POOL + 6:
                    stats_x1(i - 6)
                if ADDED_BY_POOL + 5 <= i < NB + 5:
                    stats_x1(i - 5)
                if 2 <= i < NB + 2:
                    hidden_scales(i - 2)
                if i == NB:
                    norm_1(0)
                if i == NB + 1:
                    norm_1(1)
                    spread_k(0)
                if i == NB + 3:
                    less_max(0, 0)

            def attn1_out(b):
                dve.wait_ge(S["c_ots"], b + 1)
                o = PS[:, 6, :].rearrange("p (h d) -> p h d", h=H1)
                link(dve.reciprocal(rz1[:, :], o[:, :, D1:D1 + 1].rearrange("p h d -> p (h d)")))
                dve.tensor_tensor(attn[:, :].rearrange("p (h d) -> p h d", h=H1), o[:, :, 0:D1],
                                  rz1[:, :].unsqueeze(2).broadcast_to([P, H1, D1]), ALU.mult).then_inc(S["c_oread"], 1)
                dve.wait_ge(S["c_oread"], b + 1)
                link(dve.scalar_tensor_tensor(out=xs[:, b, :], in0=attn[:, :], scalar=tg[:, 1:2], in1=xs[:, b, :],
                                              op0=ALU.mult, op1=ALU.add))
                stats_of(3, b, "mv3")

            def norm_3(b):
                dve.wait_ge(S["rstd3"], b + 1)
                if b >= 2:
                    dve.wait_ge(S["d_ps"], b - 1)
                normalise(3, b, xn3[:, b % 2, :]).then_inc(S["d_xn"], 1)

            for i in range(1, NB + 5):
                if i + 1 < NB:
                    norm_1(i + 1)
                if 2 <= i <= NB:
                    less_max(i - 1, 0)
                if 3 <= i < NB + 3:
                    attn1_out(i - 3)
                if i < NB:
                    spread_k(i)
                if 1 <= i <= NB:
                    less_max(i - 1, 1)
                if 4 <= i < NB + 4:
                    norm_3(i - 4)

            def expert_bias(n):
                dve.wait_ge(S["e_ps"], n + 1)
                if n >= 2:
                    dve.wait_ge(S["e_gelu"], n - 1)
                c = n % 4
                dve.tensor_tensor(hb[:, n % 2, :], PS[:, n % 4, :], eb[:, 512 * c:512 * (c + 1)], ALU.add)\
                    .then_inc(S["e_lin"], 1)

            dve.wait_ge(S["ld_eb"], 16)
            expert_bias(0)

            dve.wait_ge(S["d_router"], 1)
            link(dve.tensor_tensor(logits[:, :, :], PS[:, 7, R0:R0 + NB * NE].rearrange("p (b e) -> p b e", b=NB),
                                   rb[:, :].unsqueeze(1).broadcast_to([P, NB, NE]), ALU.add))
            for b in range(NB):
                last = dve.max(top[:, b, :], logits[:, b, :])
            link(last)
            for b in range(NB):
                last = dve.max_index(topi[:, b, :], top[:, b, :], logits[:, b, :])
            link(last)
            dve.tensor_tensor(p2[:, 0, :], top[:, :, 1], top[:, :, 0], ALU.subtract).then_inc(S["d_chain"], 1)
            link(dve.tensor_copy(topf[:, :, :], topi[:, :, :]))
            io = iota_e[:, :].rearrange("p (b e) -> p b e", b=NB)
            for k in range(2):
                dve.tensor_tensor(oh[:, k, :, :], io, topf[:, :, k:k + 1].broadcast_to([P, NB, NE]), ALU.is_equal)
            dve.wait_ge(S["d_e"], 1)
            link(dve.tensor_scalar(p2[:, 2, :], p2[:, 1, :], 1.0, None, ALU.add))
            link(dve.reciprocal(p2[:, 2, :], p2[:, 2, :]))
            link(dve.tensor_tensor(p2[:, 3, :], p2[:, 1, :], p2[:, 2, :], ALU.mult))
            for k in range(2):
                link(dve.tensor_tensor(oh[:, k, :, :], oh[:, k, :, :],
                                       p2[:, 2 + k, :].unsqueeze(2).broadcast_to([P, NB, NE]), ALU.mult))
            dve.tensor_tensor(gates[:, :, :], oh[:, 0, :, :], oh[:, 1, :, :], ALU.add).then_inc(S["d_gates"], 1)
            dve.wait_ge(S["d_gates"], 1)

            def gate_experts(n):
                dve.wait_ge(S["e_gelu"], n + 1)
                b, c = n // 4, n % 4
                for e in range(2):
                    g = gates[:, b, 2 * c + e:2 * c + e + 1]
                    h = he[:, n % 2, e * F:(e + 1) * F]
                    if c == 0 and e == 0:
                        if b >= 2:
                            dve.wait_ge(S["e_tps"], b - 1)
                        dve.tensor_scalar(acc[:, b % 2, :], h, g, None, ALU.mult).then_inc(S["e_acc"], 1)
                    else:
                        dve.wait_ge(S["e_acc"], 2 * n + e)
                        dve.scalar_tensor_tensor(out=acc[:, b % 2, :], in0=h, scalar=g, in1=acc[:, b % 2, :],
                                                 op0=ALU.mult, op1=ALU.add).then_inc(S["e_acc"], 1)

            def result(b):
                dve.wait_ge(S["e_yps"], b + 1)
                if b >= 2:
                    dve.wait_ge(S["e_out"], 16 * (b - 1))
                link(dve.tensor_tensor(yo[:, b % 2, :], PS[:, 5, 0:F], ob[:, :], ALU.add))
                dve.scalar_tensor_tensor(out=yo[:, b % 2, :], in0=yo[:, b % 2, :], scalar=tg[:, 3:4], in1=xs[:, b, :],
                                         op0=ALU.mult, op1=ALU.add).then_inc(S["e_y"], 1)

            for n in range(4 * NB + 5):
                if 1 <= n < 4 * NB:
                    expert_bias(n)
                if 1 <= n <= 4 * NB:
                    gate_experts(n - 1)
                if n >= 8 and n % 4 == 0:
                    result((n - 8) // 4)

        @block.tensor
        def _(pe):
            pe.wait_ge(S["ld_qk"], 64)
            pe.wait_ge(S["ld_ctx"], 16)

            def project_qk(b):
                pe.wait_ge(S["xn_ready"], b + 1)
                if b == 1:
                    pe.wait_ge(S["ld_ctx2"], 16)
                if b:
                    pe.wait_ge(S["nat_ready"], 2 * b)
                if b >= 4:
                    pe.wait_ge(S["v_evac"], b - 3)
                pe.matmul(PS[:, 7, 0:F], wq[:, :], xn[:, b % 2, :], start=True, stop=True)
                pe.matmul(PS[:, 7, F:2 * F], wk[:, :], cs[:, b, :], start=True, stop=True).then_inc(S["qk_ps"], 1)

            def sum_over_partitions():
                pe.wait_ge(S["w1_abs"], 2)
                pe.wait_ge(S["nat_ready"], 2 * NB)
                pe.wait_ge(S["v_evac"], NB - 3)
                pe.matmul(PS[:, 7, F:F + 2], ones[:, :], wsum[:, :], start=True, stop=True).then_inc(S["wsum_ps"], 1)

            def project_v(b):
                pe.wait_ge(S["m_rows"], b + 1)
                if b == 0:
                    pe.wait_ge(S["ld_v"], 32)
                for st in range(2):
                    mm = pe.matmul(PS[:, 7, st * P:(st + 1) * P], cs[:, b, st * P:(st + 1) * P], wv[:, :],
                                   start=True, stop=True)
                mm.then_inc(S["v_ps"], 1)

            def scores_for_max(b, k):
                n = 16 * b + k
                if k == 0:
                    pe.wait_ge(stacked(b), stacked_count(b))
                    if b < NSTACK:
                        pe.wait_ge(S["zero_lower"], b + 1)
                        pe.wait_ge(S["zero_upper"], b + 1)
                if n >= 2:
                    pe.wait_ge(S["s_max"], n - 1)
                pr, tt = k // 2, k % 2
                z = b % NSTACK
                pe.matmul(PS[:, k % 2, :], qst[:, z, pr, tt * P:(tt + 1) * P],
                          kst[:, z, pr, :, :].rearrange("p e s -> p (e s)"), start=True, stop=True)\
                    .then_inc(S["s_ps"], 1)

            def turn_maxima(b):
                pe.wait_ge(S["m_parts"], 2 * (b + 1))
                pe.wait_ge(S["nat_ready"], 2 * min(b + 4, NB))
                if b:
                    pe.wait_ge(S["v_evac"], b)
                if b == NB - 3:
                    pe.wait_ge(S["wtotal_ready"], 1)
                if b == 0:
                    pe.wait_ge(S["ident_ready"], 1)
                for tt in range(2):
                    mm = pe.transpose(PS[0:2 * H0, 7, tt * 64:(tt + 1) * 64].bitcast(bf16),
                                      mparts[:, tt, :, :, :].rearrange("p a e k -> p (a e k)"), ident_b[:, :])
                mm.then_inc(S["m_ps"], 1)

            def scores_less_max(b, u):
                n = NP * b + u
                if u == 0:
                    pe.wait_ge(S["m_stacked"], 32 * (b + 1))
                if n >= 2:
                    pe.wait_ge(S["prob_ready"], n - 1)
                z, pr = b % NSTACK, pair(u)
                for st in range(2):
                    for e in range(2):
                        mm = pe.matmul(PS[:, 2 + 2 * (u % 2) + st, e * F:(e + 1) * F],
                                       kst[:, z, pr, e, st * P:(st + 1) * P], qst[:, z, pr, :], start=True, stop=True)
                mm.then_inc(S["t_ps"], 1)

            def weigh_values(b, g):
                r, st = g // 2, g % 2
                pe.wait_ge(S["prob_ready"], NP * b + 2 * r + 2)
                if g == 0:
                    pe.wait_ge(S["vz_ready"], 2 * (b + 1))
                    if b:
                        pe.wait_ge(S["o_read"], b)
                for what in range(2):
                    for j in range(4):
                        w = vz[:, b % 2, st, :] if what == 0 else oz[:, :]
                        c0 = r * P + 32 * j
                        p = prob[:, (2 * r + j // 2) % 4, st * 2 * F + (j % 2) * F:st * 2 * F + (j % 2 + 1) * F]
                        mm = pe.matmul(PS[32 * j:32 * j + 32, 6, what * F:(what + 1) * F], w[:, c0:c0 + 32], p,
                                       start=(g == 0 and what == 0), stop=(g == 7), skip_group_check=True)
                mm.then_inc(S["o_ps"], 1)

            def turn_x(b):
                pe.wait_ge(S["a_round"], b + 1)
                if b == 0:
                    pe.wait_ge(S["v_evac"], NB)
                if b:
                    pe.wait_ge(S["a_bf"], b)
                for c in range(FC):
                    mm = pe.transpose(PS[:, 7, c * P:(c + 1) * P], xr[:, b % 2, c * P:(c + 1) * P], ident[:, :])
                mm.then_inc(S["a_ps"], 1)

            for i in range(LAST + 1):
                for u in range(NP):
                    if u == 0 and i < NB:
                        project_qk(i)
                    at = pair_at(i, u, FIRST)
                    if at:
                        scores_less_max(*at)
                    if 2 <= i < NB + 2:
                        scores_for_max(i - 2, 2 * u)
                    at = pair_at(i, u, FIRST + 2)
                    if at:
                        weigh_values(*at)
                    if 2 <= i < NB + 2:
                        scores_for_max(i - 2, 2 * u + 1)
                    if i == NB and u == 1:
                        sum_over_partitions()
                    if 3 <= i < NB + 3 and u == MAXIMA_PLACE:
                        turn_maxima(i - 3)
                    if 3 <= i < NB + 3 and u == V_PLACE:
                        project_v(i - 3)
                    if (i, u) in TURN_X:
                        turn_x(TURN_X[i, u])

            def up(b):
                pe.wait_ge(S["a_bf"], b + 1)
                if b == 0:
                    pe.wait_ge(S["w1_done"], 3)
                    pe.wait_ge(S["s_max"], 16 * NB)
                if b == 1:
                    pe.wait_ge(S["prob_ready"], NP * NB)
                if b >= 2:
                    pe.wait_ge(S["h_lin"], b - 1)
                for hh in range(2):
                    for c in range(FC):
                        mm = pe.matmul(PS[:, 4 * (b % 2) + hh, :], xq[:, b, c, :], w1q[:, c, hh * 512:(hh + 1) * 512],
                                       start=(c == 0), stop=(c == FC - 1))
                mm.then_inc(S["h_ps"], 1)

            def turn_h(b):
                pe.wait_ge(S["h_round"], b + 1)
                if b == 0:
                    pe.wait_ge(S["prob_ready"], NP * NB)
                if b:
                    pe.wait_ge(S["h_bf"], b)
                for c in range(HC):
                    mm = pe.transpose(PS[:, 2 + c // 4, (c % 4) * P:(c % 4 + 1) * P], hr[:, b % 2, c * P:(c + 1) * P],
                                      ident[:, :])
                mm.then_inc(S["h_rps"], 1)

            def down(b):
                pe.wait_ge(S["h_bf"], b + 1)
                if b == 0:
                    pe.wait_ge(S["w2_done"], 3)
                    pe.wait_ge(S["o_read"], NB)
                if b:
                    pe.wait_ge(S["y_read"], b)
                for c in range(HC):
                    mm = pe.matmul(PS[:, 6, 0:F], hq[:, b % 2, c, :], w2q[:, c, :], start=(c == 0), stop=(c == HC - 1))
                mm.then_inc(S["y_ps"], 1)

            def turn_1(b):
                pe.wait_ge(S["c_xn"], b + 1)
                if b == 0:
                    pe.wait_ge(S["a_bf"], NB)
                if b:
                    pe.wait_ge(S["c_evac"], 2 * b)
                if b > 5:
                    pe.wait_ge(S["d_xt"], b - 5)
                for c in range(FC):
                    pe.transpose(PS[:, 7, c * P:(c + 1) * P], xn[:, b % 2, c * P:(c + 1) * P], ident[:, :])
                for c in range(FC):
                    mm = pe.transpose(PS[:, 7, F + c * P:F + (c + 1) * P], cs[:, b, c * P:(c + 1) * P], ident[:, :])
                mm.then_inc(S["c_ps"], 1)

            def scores_1(b, hf):
                pe.wait_ge(S["c_kz"], b + 1)
                pe.wait_ge(S["c_kza"], b + 1)
                if b:
                    pe.wait_ge(S["c_kzg"], b)
                if b == 0:
                    pe.wait_ge(S["h_bf"] if hf else S["h_lin"], NB)
                if b:
                    pe.wait_ge(S["c_dif"], 2 * (b - 1) + hf + 1)
                for q in range(2):
                    pe.matmul(PS[:, 2 * hf + q, :], ident_b[:, :], causal_b[:, :, :].rearrange("p a s -> p (a s)"),
                              start=True, stop=False)
                    mm = pe.matmul(PS[:, 2 * hf + q, :], qt[:, b % 2, hf, :],
                                   kz[:, b % 2, hf, 4 * q:4 * q + 4, :].rearrange("p v s -> p (v s)"),
                                   start=False, stop=True)
                mm.then_inc(S["c_s"], 1)

            for i in range(NB + 4):
                if i < NB:
                    up(i)
                if i in (2, 3, 4):
                    turn_x(NB + i - 5)
                if 3 <= i < NB + 3:
                    turn_h(i - 3)
                if i == NB + 2:
                    scores_1(0, 0)
                if i >= 4:
                    down(i - 4)
                if i == NB:
                    turn_1(0)

            def turn_p(b, hf):
                n = 2 * b + hf
                pe.wait_ge(S["c_exp"], n + 1)
                if n == 0:
                    pe.wait_ge(S["h_lin"], NB)
                if n:
                    pe.wait_ge(S["c_pt"], n)
                for h in range(NH2):
                    mm = pe.transpose(PS[:, 4 + h // 4, (h % 4) * P:(h % 4 + 1) * P], dif[:, b % 2, hf * NH2 + h, :],
                                      ident[:, :])
                mm.then_inc(S["c_tps"], 1)

            def weigh_1(b):
                pe.wait_ge(S["c_pt"], 2 * (b + 1))
                pe.wait_ge(S["c_vaug"], b + 1)
                if b == 0:
                    pe.wait_ge(S["y_read"], NB)
                if b:
                    pe.wait_ge(S["c_oread"], b)
                for g in range(4):
                    for j in range(4):
                        h = 4 * g + j
                        mm = pe.matmul(PS[VC * j:VC * (j + 1), 6, g * P:(g + 1) * P], vaug[:, b % 2, h, :],
                                       pt[:, h // NH2, h % NH2, :], start=True, stop=True, skip_group_check=True)
                mm.then_inc(S["c_ops"], 1)

            def turn_o(b):
                pe.wait_ge(S["c_ot"], b + 1)
                for g in range(4):
                    mm = pe.transpose(PS[:, 6, g * P:(g + 1) * P], ot[:, g * P:(g + 1) * P], ident[:, :])
                mm.then_inc(S["c_ots"], 1)

            def turn_3(b):
                pe.wait_ge(S["d_xn"], b + 1)
                pe.wait_ge(S["c_evac"], 2 * min(b + 6, NB))
                if b:
                    pe.wait_ge(S["d_xt"], b)
                for c in range(FC):
                    mm = pe.transpose(PS[:, 7, c * P:(c + 1) * P], xn3[:, b % 2, c * P:(c + 1) * P], ident[:, :])
                mm.then_inc(S["d_ps"], 1)

            def route(b):
                pe.wait_ge(S["d_xt"], max(4, min(b + 2, NB)))
                pe.wait_ge(S["c_evac"], 2 * NB)
                for c in range(FC):
                    mm = pe.matmul(PS[:, 7, R0 + b * NE:R0 + (b + 1) * NE], xt[:, b, c, :], rw[:, c, :],
                                   start=(c == 0), stop=(c == FC - 1))
                if b == NB - 1:
                    mm.then_inc(S["d_router"], 1)

            def experts(n):
                b, q = n // 4, n % 4
                if n == 0:
                    pe.wait_ge(S["ld_ew"], 32)
                    pe.wait_ge(S["c_dif"], 2 * NB)
                if n >= 4:
                    pe.wait_ge(S["e_lin"], n - 3)
                for c in range(FC):
                    mm = pe.matmul(PS[:, q, :], xt[:, b, c, :], ew[c][:, 2 * q:2 * q + 2, :].rearrange("p e d -> p (e d)"),
                                   start=(c == 0), stop=(c == FC - 1))
                mm.then_inc(S["e_ps"], 1)

            for i in range(1, NB + 6):
                if i < NB:
                    turn_1(i)
                if 2 <= i < NB + 2:
                    turn_p(i - 2, 0)
                if 2 <= i <= NB:
                    scores_1(i - 1, 0)
                if 3 <= i < NB + 3:
                    turn_o(i - 3)
                if 5 <= i < NB + 5:
                    turn_3(i - 5)
                if 2 <= i < NB + 2:
                    turn_p(i - 2, 1)
                if 1 <= i <= NB:
                    scores_1(i - 1, 1)
                if i == NB + 2:
                    experts(0)
                if i == NB:
                    for b in range(3):
                        route(b)
                if NB < i:
                    route(i - 6)
                if 2 <= i < NB + 2:
                    weigh_1(i - 2)

            def turn_acc(b):
                pe.wait_ge(S["e_acc"], 8 * (b + 1))
                if b:
                    pe.wait_ge(S["e_acct"], b)
                for c in range(FC):
                    mm = pe.transpose(PS[:, 4, c * P:(c + 1) * P], acc[:, b % 2, c * P:(c + 1) * P], ident[:, :])
                mm.then_inc(S["e_tps"], 1)

            def project_out(b):
                pe.wait_ge(S["e_acct"], b + 1)
                if b:
                    pe.wait_ge(S["e_y"], b)
                for c in range(FC):
                    mm = pe.matmul(PS[:, 5, 0:F], acct[:, b % 2, c, :], ow[:, c, :], start=(c == 0), stop=(c == FC - 1))
                mm.then_inc(S["e_yps"], 1)

            for n in range(4 * NB + 4):
                if 1 <= n < 4 * NB:
                    experts(n)
                if n >= 5 and n % 4 == 1:
                    turn_acc((n - 5) // 4)
                if n >= 7 and n % 4 == 3:
                    project_out((n - 7) // 4)


def _heads_in_stack_order(n_tokens, heads):
    d = n_tokens // heads
    return [64 * jj + 32 * e + 8 * r + c for jj in range(2) for r in range(4) for e in range(2) for c in range(d)]


def kernel(**inputs):
    import concourse.bacc as _bacc
    from concourse import mybir as _mybir
    from concourse.bass_utils import run_bass_kernel_spmd as _run

    a = {k: np.asarray(v) for k, v in inputs.items()}
    NB, T, F = a["x"].shape
    order = _heads_in_stack_order(T, 16)
    mask = a["mask_Bx1x2048_fk1"].reshape(NB, F)
    laid = {
        "x": a["x"], "ctx": a["ctx_2048"],
        "mask_rows": mask, "mask_cols": mask.reshape(NB, 2, 128).transpose(2, 0, 1),
        "g_xattn": a["g_xattn"], "g_ffn": a["g_ffn"],
        "wq_t": a["L0_xattn_Wq"][order].T, "bq": a["L0_xattn_bq"][order],
        "wk_t": a["L0_xattn_Wk"][order].T, "bk": a["L0_xattn_bk"][order],
        "wv_t": a["L0_xattn_Wv"].T, "bv": a["L0_xattn_bv"],
        "w1_t": a["L0_ffn_w1"].T, "b1": a["L0_ffn_b1"], "w2_t": a["L0_ffn_w2"].T, "b2": a["L0_ffn_b2"],
        "router_w": a["L1_ffn_router_w"], "router_b": a["L1_ffn_router_b"],
        "expert_w": a["L1_ffn_expert_w"], "expert_b": a["L1_ffn_expert_b"],
        "out_w": a["L1_ffn_out_w"], "out_b": a["L1_ffn_out_b"],
    }
    nc = _bacc.Bacc("TRN2", target_bir_lowering=False, num_devices=1)
    arrays, args = {}, []
    for name, v in laid.items():
        v = np.ascontiguousarray(v)
        arrays[f"in_{name}"] = v
        args.append(nc.dram_tensor(f"in_{name}", v.shape, _mybir.dt.from_np(v.dtype), kind="ExternalInput").ap())
    args.append(nc.dram_tensor("out_0", a["x"].shape, _mybir.dt.from_np(a["x"].dtype), kind="ExternalOutput").ap())
    gated_cross_attention_blocks(nc, *args)
    r = _run(nc, [arrays], core_ids=[0])
    return r.results[0]["out_0"]
```
